# Optimizing a Trainium2 kernel written in Bass

```python
import numpy as np
import jax
import jax.numpy as jnp

def _softmax(x, axis=-1):
    return jax.nn.softmax(x, axis=axis)

def _gelu(x):
    return jax.nn.gelu(x, approximate=True)

def _silu(x):
    return jax.nn.silu(x)

def _sigmoid(x):
    return jax.nn.sigmoid(x)

def _layernorm(x, axis=-1, eps=1e-05):
    m = jnp.mean(x, axis=axis, keepdims=True)
    v = jnp.var(x, axis=axis, keepdims=True)
    return (x - m) / jnp.sqrt(v + eps)

def _scatter_add(tgt, idx, src, axis=0):
    return tgt.at[idx].add(src)

def _segment_sum(src, seg, n):
    return jax.ops.segment_sum(src, seg, n)
kernel_name = 'mk_early_fusion_embed_d4_tok_img1024_r4_ca3ba5'

def setup_inputs(seed: int=0):
    np.random.seed(seed)
    _w = jnp.asarray

    def _rec_inputs():
        import jax
        import jax.numpy as jnp
        _rk = jax.random.key(seed)
        x = -0.00016672 + 0.999947 * jax.random.normal(jax.random.fold_in(_rk, 1), (16, 3, 96, 96), jnp.float32)
        x_txt = jax.random.randint(jax.random.fold_in(_rk, 51), (16, 32), 0, 31993, jnp.int32)
        return (x, x_txt)
    x, x_txt = _rec_inputs()

    def _L0_tok_setup():
        import jax, jax.numpy as jnp
        import numpy as np
        B, C, H, Wd = (64, 3, 96, 96)
        PH, PW, D = (16, 16, 256)
        PATCH_DIM = C * PH * PW
        N_TOK = H // PH * (Wd // PW)
        key = jax.random.key(seed)
        k1, k2, k3, k4, k5 = jax.random.split(key, 5)
        x = jax.random.normal(k1, (B, C, H, Wd), dtype=jnp.float32)
        W = jax.random.normal(k2, (D, PATCH_DIM), dtype=jnp.float32) * PATCH_DIM ** (-0.5)
        b = jax.random.normal(k3, (D,), dtype=jnp.float32) * 0.02
        cls_token = jax.random.normal(k4, (1, 1, D), dtype=jnp.float32)
        pos_embedding = jax.random.normal(k5, (1, N_TOK + 1, D), dtype=jnp.float32) * 0.02
        return {'x': x, 'W': W, 'b': b, 'cls_token': cls_token, 'pos_embedding': pos_embedding}
    _L0_tok_all = _L0_tok_setup()
    _L0_tok_in = {k: v for k, v in _L0_tok_all.items() if k in ('W', 'b', 'cls_token', 'pos_embedding')}
    del _L0_tok_all

    def _L0_txt_setup():
        import jax, jax.numpy as jnp
        import numpy as np
        EPS = 1e-05

        def layernorm(x, s, b):
            m = jnp.mean(x, axis=-1, keepdims=True)
            v = jnp.mean(jnp.square(x - m), axis=-1, keepdims=True)
            return (x - m) * jax.lax.rsqrt(v + EPS) * s + b

        def ssm(x, a_diag, Bm, Cm, Dm):
            a = jax.nn.sigmoid(a_diag)
            u = jnp.einsum('btd,ds->bts', x, Bm)

            def step(h, u_t):
                h = a * h + u_t
                return (h, h)
            h0 = jnp.zeros((x.shape[0], a.shape[0]), x.dtype)
            _, H = jax.lax.scan(step, h0, jnp.swapaxes(u, 0, 1))
            H = jnp.swapaxes(H, 0, 1)
            return jnp.einsum('bts,sd->btd', H, Cm) + jnp.einsum('btd,de->bte', x, Dm)
        key = jax.random.key(seed)
        ks = jax.random.split(key, 12)
        Bn, T = (4, 512)
        V, Dm, S, L, F = (8000, 256, 64, 4, 1024)

        def xavier(k, shape):
            fan_in, fan_out = (shape[-2], shape[-1])
            lim = float(np.sqrt(6.0 / (fan_in + fan_out)))
            return jax.random.uniform(k, shape, jnp.float32, -lim, lim)
        return {'tokens': jax.random.randint(ks[0], (Bn, T), 0, V), 'emb': jax.random.normal(ks[1], (V, Dm), jnp.float32), 'pos_emb': jax.random.normal(ks[2], (1024, Dm), jnp.float32), 'A_diag': jax.random.uniform(ks[3], (L, S), jnp.float32, -0.5, 0.5), 'B': xavier(ks[4], (L, Dm, S)), 'C': xavier(ks[5], (L, S, Dm)), 'D': xavier(ks[6], (L, Dm, Dm)) * 0.1, 'w1': xavier(ks[7], (L, Dm, F)), 'b1': jnp.zeros((L, F), jnp.float32), 'w2': xavier(ks[8], (L, F, Dm)), 'b2': jnp.zeros((L, Dm), jnp.float32), 'ln1_s': jnp.ones((L, Dm), jnp.float32), 'ln1_b': jnp.zeros((L, Dm), jnp.float32), 'ln2_s': jnp.ones((L, Dm), jnp.float32), 'ln2_b': jnp.zeros((L, Dm), jnp.float32), 'lnf_s': jnp.ones((Dm,), jnp.float32), 'lnf_b': jnp.zeros((Dm,), jnp.float32)}
    _L0_txt_all = _L0_txt_setup()
    _L0_txt_in = {k: v for k, v in _L0_txt_all.items() if k in ('emb', 'pos_emb', 'A_diag', 'B', 'C', 'D', 'w1', 'b1', 'w2', 'b2', 'ln1_s', 'ln1_b', 'ln2_s', 'ln2_b', 'lnf_s', 'lnf_b')}
    del _L0_txt_all

    def _L0_attn_setup():
        import jax, jax.numpy as jnp
        import numpy as np
        from jax import lax
        DIM = 256
        DS = 16
        DC = 4
        EXP = 2
        DI = DIM * EXP
        B, L = (2, 256)

        def _ssm(x, x_proj_w, dt_w, dt_b, A_log, D_skip):
            xp = jnp.einsum('bli,pi->blp', x, x_proj_w)
            delta = jax.nn.softplus(xp[..., :1] * dt_w[:, 0] + dt_b)
            Bp = xp[..., 1:DS + 1]
            Cp = xp[..., DS + 1:]
            A = -jnp.exp(A_log)
            dA = jnp.exp(delta[..., None] * A)
            dB = delta[..., None] * Bp[:, :, None, :] * x[..., None]

            def step(h, inp):
                dA_t, dB_t, C_t = inp
                h = dA_t * h + dB_t
                return (h, jnp.einsum('bdn,bn->bd', h, C_t))
            h0 = jnp.zeros((x.shape[0], DI, DS), x.dtype)
            _, ys = lax.scan(step, h0, (jnp.swapaxes(dA, 0, 1), jnp.swapaxes(dB, 0, 1), jnp.swapaxes(Cp, 0, 1)))
            y = jnp.swapaxes(ys, 0, 1)
            return y + x * D_skip
        key = jax.random.key(seed)
        ks = jax.random.split(key, 10)
        s = lambda k, shape, sc: jax.random.normal(k, shape, jnp.float32) * sc
        return {'x': s(ks[0], (B, L, DIM), 1.0), 'norm_w': jnp.ones((DIM,), jnp.float32), 'norm_b': jnp.zeros((DIM,), jnp.float32), 'in_proj_w': s(ks[1], (2 * DI, DIM), DIM ** (-0.5)), 'conv_w': s(ks[2], (DI, 1, DC), DC ** (-0.5)), 'conv_b': jnp.zeros((DI,), jnp.float32), 'x_proj_w': s(ks[3], (2 * DS + 1, DI), DI ** (-0.5)), 'dt_w': s(ks[4], (DI, 1), 1.0), 'dt_b': jax.random.uniform(ks[5], (DI,), jnp.float32, -0.001, 0.001), 'A_log': s(ks[6], (DI, DS), 1.0), 'D_skip': jnp.ones((DI,), jnp.float32), 'out_proj_w': s(ks[7], (DIM, DI), DI ** (-0.5))}
    _L0_attn_all = _L0_attn_setup()
    _L0_attn_in = {k: v for k, v in _L0_attn_all.items() if k in ('norm_w', 'norm_b', 'in_proj_w', 'conv_w', 'conv_b', 'x_proj_w', 'dt_w', 'dt_b', 'A_log', 'D_skip', 'out_proj_w')}
    del _L0_attn_all

    def _L0_ffn_setup():
        import jax, jax.numpy as jnp
        from jax import lax
        import numpy as np
        D_MODEL = 256
        HIDDEN = 128
        N_EXPERTS = 32
        TOP_K = 2
        B, S = (1, 1024)

        def _moe_group(x2, router_w, wg, wu, wd, top_k):
            T = x2.shape[0]
            n_experts = router_w.shape[1]
            logits = x2 @ router_w
            scores = jax.nn.softmax(logits, axis=-1)
            expert_weights, expert_indices = lax.top_k(scores, top_k)
            flat_e = expert_indices.reshape(-1)
            flat_w = expert_weights.reshape(-1)
            flat_t = jnp.repeat(jnp.arange(T), top_k)
            order = jnp.argsort(flat_e)
            tok = flat_t[order]
            xs = x2[tok]
            group_sizes = jnp.bincount(flat_e, length=n_experts).astype(jnp.int32)
            gate = lax.ragged_dot(xs, wg, group_sizes)
            up = lax.ragged_dot(xs, wu, group_sizes)
            ys = lax.ragged_dot(jax.nn.silu(gate) * up, wd, group_sizes)
            ys = ys * flat_w[order][:, None]
            return jnp.zeros_like(x2).at[tok].add(ys)
        key = jax.random.key(seed)
        ks = jax.random.split(key, 9)
        w = lambda k, shape: jax.random.normal(k, shape, dtype=jnp.float32) * 0.02
        return {'x': jax.random.normal(ks[0], (B, S, D_MODEL), dtype=jnp.float32), 'router_w0': w(ks[1], (D_MODEL, N_EXPERTS)), 'wg0': w(ks[2], (N_EXPERTS, D_MODEL, HIDDEN)), 'wu0': w(ks[3], (N_EXPERTS, D_MODEL, HIDDEN)), 'wd0': w(ks[4], (N_EXPERTS, HIDDEN, D_MODEL)), 'router_w1': w(ks[5], (D_MODEL, N_EXPERTS)), 'wg1': w(ks[6], (N_EXPERTS, D_MODEL, HIDDEN)), 'wu1': w(ks[7], (N_EXPERTS, D_MODEL, HIDDEN)), 'wd1': w(ks[8], (N_EXPERTS, HIDDEN, D_MODEL))}
    _L0_ffn_all = _L0_ffn_setup()
    _L0_ffn_in = {k: v for k, v in _L0_ffn_all.items() if k in ('router_w0', 'wg0', 'wu0', 'wd0', 'router_w1', 'wg1', 'wu1', 'wd1')}
    del _L0_ffn_all

    def _L1_attn_setup():
        import jax, jax.numpy as jnp
        import numpy as np
        BLOCK = 128
        NUM_GLOBAL = 16
        GBL = BLOCK // NUM_GLOBAL
        NEG = -10000.0
        E = 256
        H = 16

        def _sparse_attn(q, k, v, M):
            B, Hn, S, d = q.shape
            nb = S // BLOCK
            rem = S % BLOCK
            Lg = S - S % GBL
            ns = Lg // GBL
            scale = 1.0 / jnp.sqrt(jnp.asarray(d, q.dtype))
            k_str = k[:, :, :Lg].reshape(B, Hn, ns, GBL, d)[:, :, :, -1, :]
            v_str = v[:, :, :Lg].reshape(B, Hn, ns, GBL, d)[:, :, :, -1, :]
            outs = []
            if nb > 0:
                L = nb * BLOCK
                fq = q[:, :, :L].reshape(B, Hn, nb, BLOCK, d)
                fk_loc = k[:, :, :L].reshape(B, Hn, nb, BLOCK, d)
                fv_loc = v[:, :, :L].reshape(B, Hn, nb, BLOCK, d)
                mloc = M[..., :L, :L].reshape(1, 1, nb, BLOCK, nb, BLOCK)
                mloc = jnp.moveaxis(jnp.diagonal(mloc, axis1=2, axis2=4), -1, 2)
                mstr = M[..., :L, :Lg].reshape(1, 1, nb, BLOCK, ns, GBL)[..., -1]
                fmask = jnp.concatenate([mstr, mloc], axis=-1)
                fk = jnp.concatenate([jnp.broadcast_to(k_str[:, :, None], (B, Hn, nb, ns, d)), fk_loc], axis=-2)
                fv = jnp.concatenate([jnp.broadcast_to(v_str[:, :, None], (B, Hn, nb, ns, d)), fv_loc], axis=-2)
                w = jnp.einsum('bhnqd,bhnkd->bhnqk', fq, fk) * scale + fmask
                w = jax.nn.softmax(w, axis=-1)
                o1 = jnp.einsum('bhnqk,bhnkd->bhnqd', w, fv).reshape(B, Hn, L, d)
                outs.append(o1)
            if rem > 0:
                sq = q[:, :, -rem:]
                sk = jnp.concatenate([k_str, k[:, :, -rem:]], axis=2)
                sv = jnp.concatenate([v_str, v[:, :, -rem:]], axis=2)
                mstr2 = M[..., -rem:, :Lg].reshape(1, 1, rem, ns, GBL)[..., -1]
                smask = jnp.concatenate([mstr2, M[..., -rem:, -rem:]], axis=-1)
                w2 = jnp.einsum('bhqd,bhkd->bhqk', sq, sk) * scale + smask
                w2 = jax.nn.softmax(w2, axis=-1)
                o2 = jnp.einsum('bhqk,bhkd->bhqd', w2, sv)
                outs.append(o2)
            return jnp.concatenate(outs, axis=-2) if len(outs) > 1 else outs[0]
        key = jax.random.key(seed)
        ks = jax.random.split(key, 4)
        B, S = (4, 576)
        return {'hidden_states': jax.random.normal(ks[0], (B, S, E), dtype=jnp.float32), 'c_attn_w': jax.random.normal(ks[1], (E, 3 * E), dtype=jnp.float32) * 0.02, 'c_attn_b': jnp.zeros((3 * E,), dtype=jnp.float32), 'c_proj_w': jax.random.normal(ks[2], (E, E), dtype=jnp.float32) * 0.02, 'c_proj_b': jnp.zeros((E,), dtype=jnp.float32)}
    _L1_attn_all = _L1_attn_setup()
    _L1_attn_in = {k: v for k, v in _L1_attn_all.items() if k in ('c_attn_w', 'c_attn_b', 'c_proj_w', 'c_proj_b')}
    del _L1_attn_all

    def _L1_ffn_setup():
        import jax, jax.numpy as jnp
        import numpy as np

        def _bitlinear(x, w_latent):
            scale = jax.lax.stop_gradient(jnp.clip(jnp.mean(jnp.abs(w_latent), axis=1, keepdims=True), 1e-05, None))
            tern = jnp.clip(jnp.round(w_latent / scale), -1.0, 1.0)
            w = w_latent + jax.lax.stop_gradient(tern - w_latent)
            return x @ (w * scale).T
        key = jax.random.key(seed)
        ks = jax.random.split(key, 6)
        dim, hidden, rank = (256, 1024, 16)
        B, S = (4, 1024)
        x = jax.random.normal(ks[0], (B, S, dim), dtype=jnp.float32)
        w_fc = 0.02 * jax.random.normal(ks[1], (hidden, dim), dtype=jnp.float32)
        w_proj = 0.02 * jax.random.normal(ks[2], (dim, hidden), dtype=jnp.float32)
        u = 0.02 * jax.random.normal(ks[3], (hidden, rank), dtype=jnp.float32)
        v = 0.02 * jax.random.normal(ks[4], (rank, dim), dtype=jnp.float32)
        fast_b = jax.random.normal(ks[5], (rank, rank), dtype=jnp.float32)
        gate = jnp.float32(0.05)
        return {'x': x, 'fast_b': fast_b, 'w_fc': w_fc, 'w_proj': w_proj, 'u': u, 'v': v, 'gate': gate}
    _L1_ffn_all = _L1_ffn_setup()
    _L1_ffn_in = {k: v for k, v in _L1_ffn_all.items() if k in ('fast_b', 'w_fc', 'w_proj', 'u', 'v', 'gate')}
    del _L1_ffn_all

    def _L2_attn_setup():
        import jax, jax.numpy as jnp
        import numpy as np
        B, S, D = (4, 512, 256)
        KD, VD = (256, 256)
        key = jax.random.key(seed)
        ks = jax.random.split(key, 9)
        n = lambda k, shape: jax.random.normal(k, shape, jnp.float32) * 0.02
        return {'x': jax.random.normal(ks[0], (B, S, D), jnp.float32), 'Wq_w': n(ks[1], (KD, D)), 'Wq_b': n(ks[2], (KD,)), 'Wk_w': n(ks[3], (KD, D)), 'Wk_b': n(ks[4], (KD,)), 'Wv_w': n(ks[5], (VD, D)), 'Wv_b': n(ks[6], (VD,)), 'Wo_w': n(ks[7], (D, VD)), 'Wo_b': n(ks[8], (D,))}
    _L2_attn_all = _L2_attn_setup()
    _L2_attn_in = {k: v for k, v in _L2_attn_all.items() if k in ('Wq_w', 'Wq_b', 'Wk_w', 'Wk_b', 'Wv_w', 'Wv_b', 'Wo_w', 'Wo_b')}
    del _L2_attn_all

    def _L2_ffn_setup():
        import jax, jax.numpy as jnp
        import numpy as np
        B, S, H, F, G = (8, 512, 256, 1024, 128)
        EPS = 1e-05

        def _dequant(q, scales, g):
            K, N = q.shape
            w = (q.astype(jnp.float32) - 128.0).reshape(K // g, g, N) * scales[:, None, :]
            return w.reshape(K, N)
        key = jax.random.key(seed)
        ks = jax.random.split(key, 8)
        x = jax.random.normal(ks[0], (B, S, H), dtype=jnp.float32)
        ln_gamma = jnp.ones((H,), jnp.float32)
        ln_beta = jnp.zeros((H,), jnp.float32)
        fc1_q = jax.random.randint(ks[1], (H, F), 0, 64, dtype=jnp.int32)
        fc2_q = jax.random.randint(ks[2], (F, H), 0, 64, dtype=jnp.int32)
        fc1_scales = jax.random.uniform(ks[3], (H // G, F), jnp.float32) * 0.02 + 0.001
        fc2_scales = jax.random.uniform(ks[4], (F // G, H), jnp.float32) * 0.02 + 0.001
        fc1_bias = jax.random.normal(ks[5], (F,), jnp.float32) * 0.02
        fc2_bias = jax.random.normal(ks[6], (H,), jnp.float32) * 0.02
        return {'x': x, 'ln_gamma': ln_gamma, 'ln_beta': ln_beta, 'fc1_q': fc1_q, 'fc1_scales': fc1_scales, 'fc1_bias': fc1_bias, 'fc2_q': fc2_q, 'fc2_scales': fc2_scales, 'fc2_bias': fc2_bias}
    _L2_ffn_all = _L2_ffn_setup()
    _L2_ffn_in = {k: v for k, v in _L2_ffn_all.items() if k in ('ln_gamma', 'ln_beta', 'fc1_q', 'fc1_scales', 'fc1_bias', 'fc2_q', 'fc2_scales', 'fc2_bias')}
    del _L2_ffn_all

    def _L3_attn_setup():
        import math
        import jax, jax.numpy as jnp
        import numpy as np
        D_MODEL = 256
        NUM_HEADS = 16
        D_HEAD = D_MODEL // NUM_HEADS
        K_S = 32
        B, N = (2, 512)

        def _attn(x, Wq, bq, Wk, bk, Wv, bv, Wo, bo):
            b, n, _ = x.shape
            q = (x @ Wq.T + bq).reshape(b, n, NUM_HEADS, D_HEAD).transpose(0, 2, 1, 3)
            k = (x @ Wk.T + bk).reshape(b, n, NUM_HEADS, D_HEAD).transpose(0, 2, 1, 3)
            v = (x @ Wv.T + bv).reshape(b, n, NUM_HEADS, D_HEAD).transpose(0, 2, 1, 3)
            scores = jnp.einsum('bhqd,bhkd->bhqk', q, k) / math.sqrt(D_HEAD)
            causal = jnp.triu(jnp.ones((n, n), dtype=bool), k=1)
            neg_inf = jnp.array(-jnp.inf, dtype=scores.dtype)
            scores = jnp.where(causal, neg_inf, scores)
            vals, idx = jax.lax.top_k(scores, K_S)
            masked = jnp.full_like(scores, -jnp.inf)
            masked = jnp.put_along_axis(masked, idx, vals, axis=-1, inplace=False)
            attn = jax.nn.softmax(masked, axis=-1)
            out = jnp.einsum('bhqk,bhkd->bhqd', attn, v)
            out = out.transpose(0, 2, 1, 3).reshape(b, n, D_MODEL)
            y = out @ Wo.T + bo
            return (y, attn.mean(axis=1))

        def _reference_tuple_inner(x, Wq, bq, Wk, bk, Wv, bv, Wo, bo):
            return _attn(x, Wq, bq, Wk, bk, Wv, bv, Wo, bo)
        key = jax.random.key(seed)
        ks = jax.random.split(key, 9)
        s = 1.0 / math.sqrt(D_MODEL)
        return {'x': jax.random.normal(ks[0], (B, N, D_MODEL), dtype=jnp.float32), 'Wq': jax.random.normal(ks[1], (D_MODEL, D_MODEL), dtype=jnp.float32) * s, 'bq': jnp.zeros((D_MODEL,), dtype=jnp.float32), 'Wk': jax.random.normal(ks[2], (D_MODEL, D_MODEL), dtype=jnp.float32) * s, 'bk': jnp.zeros((D_MODEL,), dtype=jnp.float32), 'Wv': jax.random.normal(ks[3], (D_MODEL, D_MODEL), dtype=jnp.float32) * s, 'bv': jnp.zeros((D_MODEL,), dtype=jnp.float32), 'Wo': jax.random.normal(ks[4], (D_MODEL, D_MODEL), dtype=jnp.float32) * s, 'bo': jnp.zeros((D_MODEL,), dtype=jnp.float32)}
    _L3_attn_all = _L3_attn_setup()
    _L3_attn_in = {k: v for k, v in _L3_attn_all.items() if k in ('Wq', 'bq', 'Wk', 'bk', 'Wv', 'bv', 'Wo', 'bo')}
    del _L3_attn_all

    def _L3_ffn_setup():
        import jax, jax.numpy as jnp
        import numpy as np
        TOP_K = 2
        key = jax.random.key(seed)
        k1, k2, k3, k4 = jax.random.split(key, 4)
        B, S, D = (2, 512, 256)
        E, W = (8, 256)
        x = jax.random.normal(k1, (B, S, D), dtype=jnp.float32)
        router_w = jax.random.normal(k2, (E, D), dtype=jnp.float32) * 0.02
        w1 = jax.random.normal(k3, (D, E * W), dtype=jnp.float32) * 0.02
        w2 = jax.random.normal(k4, (E * W, D), dtype=jnp.float32) * 0.02
        return {'x': x, 'router_w': router_w, 'w1': w1, 'w2': w2}
    _L3_ffn_all = _L3_ffn_setup()
    _L3_ffn_in = {k: v for k, v in _L3_ffn_all.items() if k in ('router_w', 'w1', 'w2')}
    del _L3_ffn_all
    return {'x': x, 'x_txt': x_txt, 'L0_tok_W': _L0_tok_in['W'], 'L0_tok_b': _L0_tok_in['b'], 'L0_tok_cls_token': _L0_tok_in['cls_token'], 'L0_tok_pos_embedding': _L0_tok_in['pos_embedding'], 'L0_txt_emb': _L0_txt_in['emb'], 'L0_txt_pos_emb': _L0_txt_in['pos_emb'], 'L0_txt_A_diag': _L0_txt_in['A_diag'], 'L0_txt_B': _L0_txt_in['B'], 'L0_txt_C': _L0_txt_in['C'], 'L0_txt_D': _L0_txt_in['D'], 'L0_txt_w1': _L0_txt_in['w1'], 'L0_txt_b1': _L0_txt_in['b1'], 'L0_txt_w2': _L0_txt_in['w2'], 'L0_txt_b2': _L0_txt_in['b2'], 'L0_txt_ln1_s': _L0_txt_in['ln1_s'], 'L0_txt_ln1_b': _L0_txt_in['ln1_b'], 'L0_txt_ln2_s': _L0_txt_in['ln2_s'], 'L0_txt_ln2_b': _L0_txt_in['ln2_b'], 'L0_txt_lnf_s': _L0_txt_in['lnf_s'], 'L0_txt_lnf_b': _L0_txt_in['lnf_b'], 'L0_attn_norm_w': _L0_attn_in['norm_w'], 'L0_attn_norm_b': _L0_attn_in['norm_b'], 'L0_attn_in_proj_w': _L0_attn_in['in_proj_w'], 'L0_attn_conv_w': _L0_attn_in['conv_w'], 'L0_attn_conv_b': _L0_attn_in['conv_b'], 'L0_attn_x_proj_w': _L0_attn_in['x_proj_w'], 'L0_attn_dt_w': _L0_attn_in['dt_w'], 'L0_attn_dt_b': _L0_attn_in['dt_b'], 'L0_attn_A_log': _L0_attn_in['A_log'], 'L0_attn_D_skip': _L0_attn_in['D_skip'], 'L0_attn_out_proj_w': _L0_attn_in['out_proj_w'], 'L0_ffn_router_w0': _L0_ffn_in['router_w0'], 'L0_ffn_wg0': _L0_ffn_in['wg0'], 'L0_ffn_wu0': _L0_ffn_in['wu0'], 'L0_ffn_wd0': _L0_ffn_in['wd0'], 'L0_ffn_router_w1': _L0_ffn_in['router_w1'], 'L0_ffn_wg1': _L0_ffn_in['wg1'], 'L0_ffn_wu1': _L0_ffn_in['wu1'], 'L0_ffn_wd1': _L0_ffn_in['wd1'], 'L1_attn_c_attn_w': _L1_attn_in['c_attn_w'], 'L1_attn_c_attn_b': _L1_attn_in['c_attn_b'], 'L1_attn_c_proj_w': _L1_attn_in['c_proj_w'], 'L1_attn_c_proj_b': _L1_attn_in['c_proj_b'], 'L1_ffn_fast_b': _L1_ffn_in['fast_b'], 'L1_ffn_w_fc': _L1_ffn_in['w_fc'], 'L1_ffn_w_proj': _L1_ffn_in['w_proj'], 'L1_ffn_u': _L1_ffn_in['u'], 'L1_ffn_v': _L1_ffn_in['v'], 'L1_ffn_gate': _L1_ffn_in['gate'], 'L2_attn_Wq_w': _L2_attn_in['Wq_w'], 'L2_attn_Wq_b': _L2_attn_in['Wq_b'], 'L2_attn_Wk_w': _L2_attn_in['Wk_w'], 'L2_attn_Wk_b': _L2_attn_in['Wk_b'], 'L2_attn_Wv_w': _L2_attn_in['Wv_w'], 'L2_attn_Wv_b': _L2_attn_in['Wv_b'], 'L2_attn_Wo_w': _L2_attn_in['Wo_w'], 'L2_attn_Wo_b': _L2_attn_in['Wo_b'], 'L2_ffn_ln_gamma': _L2_ffn_in['ln_gamma'], 'L2_ffn_ln_beta': _L2_ffn_in['ln_beta'], 'L2_ffn_fc1_q': _L2_ffn_in['fc1_q'], 'L2_ffn_fc1_scales': _L2_ffn_in['fc1_scales'], 'L2_ffn_fc1_bias': _L2_ffn_in['fc1_bias'], 'L2_ffn_fc2_q': _L2_ffn_in['fc2_q'], 'L2_ffn_fc2_scales': _L2_ffn_in['fc2_scales'], 'L2_ffn_fc2_bias': _L2_ffn_in['fc2_bias'], 'L3_attn_Wq': _L3_attn_in['Wq'], 'L3_attn_bq': _L3_attn_in['bq'], 'L3_attn_Wk': _L3_attn_in['Wk'], 'L3_attn_bk': _L3_attn_in['bk'], 'L3_attn_Wv': _L3_attn_in['Wv'], 'L3_attn_bv': _L3_attn_in['bv'], 'L3_attn_Wo': _L3_attn_in['Wo'], 'L3_attn_bo': _L3_attn_in['bo'], 'L3_ffn_router_w': _L3_ffn_in['router_w'], 'L3_ffn_w1': _L3_ffn_in['w1'], 'L3_ffn_w2': _L3_ffn_in['w2']}

def reference(x, x_txt, L0_tok_W, L0_tok_b, L0_tok_cls_token, L0_tok_pos_embedding, L0_txt_emb, L0_txt_pos_emb, L0_txt_A_diag, L0_txt_B, L0_txt_C, L0_txt_D, L0_txt_w1, L0_txt_b1, L0_txt_w2, L0_txt_b2, L0_txt_ln1_s, L0_txt_ln1_b, L0_txt_ln2_s, L0_txt_ln2_b, L0_txt_lnf_s, L0_txt_lnf_b, L0_attn_norm_w, L0_attn_norm_b, L0_attn_in_proj_w, L0_attn_conv_w, L0_attn_conv_b, L0_attn_x_proj_w, L0_attn_dt_w, L0_attn_dt_b, L0_attn_A_log, L0_attn_D_skip, L0_attn_out_proj_w, L0_ffn_router_w0, L0_ffn_wg0, L0_ffn_wu0, L0_ffn_wd0, L0_ffn_router_w1, L0_ffn_wg1, L0_ffn_wu1, L0_ffn_wd1, L1_attn_c_attn_w, L1_attn_c_attn_b, L1_attn_c_proj_w, L1_attn_c_proj_b, L1_ffn_fast_b, L1_ffn_w_fc, L1_ffn_w_proj, L1_ffn_u, L1_ffn_v, L1_ffn_gate, L2_attn_Wq_w, L2_attn_Wq_b, L2_attn_Wk_w, L2_attn_Wk_b, L2_attn_Wv_w, L2_attn_Wv_b, L2_attn_Wo_w, L2_attn_Wo_b, L2_ffn_ln_gamma, L2_ffn_ln_beta, L2_ffn_fc1_q, L2_ffn_fc1_scales, L2_ffn_fc1_bias, L2_ffn_fc2_q, L2_ffn_fc2_scales, L2_ffn_fc2_bias, L3_attn_Wq, L3_attn_bq, L3_attn_Wk, L3_attn_bk, L3_attn_Wv, L3_attn_bv, L3_attn_Wo, L3_attn_bo, L3_ffn_router_w, L3_ffn_w1, L3_ffn_w2):
    import jax
    import jax.numpy as jnp

    def _L0_tok_ref(x, W, b, cls_token, pos_embedding):
        import jax, jax.numpy as jnp
        import numpy as np
        B, C, H, Wd = (64, 3, 96, 96)
        PH, PW, D = (16, 16, 256)
        PATCH_DIM = C * PH * PW
        N_TOK = H // PH * (Wd // PW)
        Bc = x.shape[0]
        nh, nw = (H // PH, Wd // PW)
        patches = x.reshape(Bc, C, nh, PH, nw, PW)
        patches = patches.transpose(0, 2, 4, 1, 3, 5).reshape(Bc, nh * nw, PATCH_DIM)
        tokens = jnp.einsum('bnp,dp->bnd', patches, W) + b
        cls = jnp.broadcast_to(cls_token, (Bc, 1, D))
        tokens = jnp.concatenate([cls, tokens], axis=1)
        return tokens + pos_embedding

    def _L0_txt_ref(tokens, emb, pos_emb, A_diag, B, C, D, w1, b1, w2, b2, ln1_s, ln1_b, ln2_s, ln2_b, lnf_s, lnf_b):
        import jax, jax.numpy as jnp
        import numpy as np
        EPS = 1e-05

        def layernorm(x, s, b):
            m = jnp.mean(x, axis=-1, keepdims=True)
            v = jnp.mean(jnp.square(x - m), axis=-1, keepdims=True)
            return (x - m) * jax.lax.rsqrt(v + EPS) * s + b

        def ssm(x, a_diag, Bm, Cm, Dm):
            a = jax.nn.sigmoid(a_diag)
            u = jnp.einsum('btd,ds->bts', x, Bm)

            def step(h, u_t):
                h = a * h + u_t
                return (h, h)
            h0 = jnp.zeros((x.shape[0], a.shape[0]), x.dtype)
            _, H = jax.lax.scan(step, h0, jnp.swapaxes(u, 0, 1))
            H = jnp.swapaxes(H, 0, 1)
            return jnp.einsum('bts,sd->btd', H, Cm) + jnp.einsum('btd,de->bte', x, Dm)
        T = tokens.shape[1]
        x = emb[tokens] + pos_emb[:T][None]
        L = A_diag.shape[0]
        for l in range(L):
            x = x + ssm(layernorm(x, ln1_s[l], ln1_b[l]), A_diag[l], B[l], C[l], D[l])
            h = layernorm(x, ln2_s[l], ln2_b[l])
            h = jax.nn.gelu(jnp.einsum('btd,df->btf', h, w1[l]) + b1[l], approximate=False)
            x = x + jnp.einsum('btf,fd->btd', h, w2[l]) + b2[l]
        return layernorm(x, lnf_s, lnf_b)

    def _L0_attn_ref(x, norm_w, norm_b, in_proj_w, conv_w, conv_b, x_proj_w, dt_w, dt_b, A_log, D_skip, out_proj_w):
        import jax, jax.numpy as jnp
        import numpy as np
        from jax import lax
        DIM = 256
        DS = 16
        DC = 4
        EXP = 2
        DI = DIM * EXP
        B, L = (2, 256)

        def _ssm(x, x_proj_w, dt_w, dt_b, A_log, D_skip):
            xp = jnp.einsum('bli,pi->blp', x, x_proj_w)
            delta = jax.nn.softplus(xp[..., :1] * dt_w[:, 0] + dt_b)
            Bp = xp[..., 1:DS + 1]
            Cp = xp[..., DS + 1:]
            A = -jnp.exp(A_log)
            dA = jnp.exp(delta[..., None] * A)
            dB = delta[..., None] * Bp[:, :, None, :] * x[..., None]

            def step(h, inp):
                dA_t, dB_t, C_t = inp
                h = dA_t * h + dB_t
                return (h, jnp.einsum('bdn,bn->bd', h, C_t))
            h0 = jnp.zeros((x.shape[0], DI, DS), x.dtype)
            _, ys = lax.scan(step, h0, (jnp.swapaxes(dA, 0, 1), jnp.swapaxes(dB, 0, 1), jnp.swapaxes(Cp, 0, 1)))
            y = jnp.swapaxes(ys, 0, 1)
            return y + x * D_skip
        mu = x.mean(-1, keepdims=True)
        var = ((x - mu) ** 2).mean(-1, keepdims=True)
        xn = (x - mu) * lax.rsqrt(var + 1e-05) * norm_w + norm_b
        xz = jnp.einsum('bld,pd->blp', xn, in_proj_w)
        xi, z = (xz[..., :DI], xz[..., DI:])
        xc = lax.conv_general_dilated(jnp.swapaxes(xi, 1, 2), conv_w, (1,), [(DC - 1, 0)], feature_group_count=DI, dimension_numbers=('NCH', 'OIH', 'NCH'))
        xc = jnp.swapaxes(xc + conv_b[None, :, None], 1, 2)
        xc = jax.nn.silu(xc)
        y = _ssm(xc, x_proj_w, dt_w, dt_b, A_log, D_skip)
        y = y * jax.nn.silu(z)
        return x + jnp.einsum('bli,di->bld', y, out_proj_w)

    def _L0_ffn_ref(x, router_w0, wg0, wu0, wd0, router_w1, wg1, wu1, wd1):
        import jax, jax.numpy as jnp
        from jax import lax
        import numpy as np
        D_MODEL = 256
        HIDDEN = 128
        N_EXPERTS = 32
        TOP_K = 2
        B, S = (1, 1024)

        def _moe_group(x2, router_w, wg, wu, wd, top_k):
            T = x2.shape[0]
            n_experts = router_w.shape[1]
            logits = x2 @ router_w
            scores = jax.nn.softmax(logits, axis=-1)
            expert_weights, expert_indices = lax.top_k(scores, top_k)
            flat_e = expert_indices.reshape(-1)
            flat_w = expert_weights.reshape(-1)
            flat_t = jnp.repeat(jnp.arange(T), top_k)
            order = jnp.argsort(flat_e)
            tok = flat_t[order]
            xs = x2[tok]
            group_sizes = jnp.bincount(flat_e, length=n_experts).astype(jnp.int32)
            gate = lax.ragged_dot(xs, wg, group_sizes)
            up = lax.ragged_dot(xs, wu, group_sizes)
            ys = lax.ragged_dot(jax.nn.silu(gate) * up, wd, group_sizes)
            ys = ys * flat_w[order][:, None]
            return jnp.zeros_like(x2).at[tok].add(ys)
        b, s, d = x.shape
        x2 = x.reshape(-1, d)
        out0 = _moe_group(x2, router_w0, wg0, wu0, wd0, TOP_K)
        out1 = _moe_group(x2, router_w1, wg1, wu1, wd1, TOP_K)
        out = (out0 * TOP_K + out1 * TOP_K) / (TOP_K + TOP_K)
        return out.reshape(b, s, d)

    def _L1_attn_ref(hidden_states, c_attn_w, c_attn_b, c_proj_w, c_proj_b):
        import jax, jax.numpy as jnp
        import numpy as np
        BLOCK = 128
        NUM_GLOBAL = 16
        GBL = BLOCK // NUM_GLOBAL
        NEG = -10000.0
        E = 256
        H = 16

        def _sparse_attn(q, k, v, M):
            B, Hn, S, d = q.shape
            nb = S // BLOCK
            rem = S % BLOCK
            Lg = S - S % GBL
            ns = Lg // GBL
            scale = 1.0 / jnp.sqrt(jnp.asarray(d, q.dtype))
            k_str = k[:, :, :Lg].reshape(B, Hn, ns, GBL, d)[:, :, :, -1, :]
            v_str = v[:, :, :Lg].reshape(B, Hn, ns, GBL, d)[:, :, :, -1, :]
            outs = []
            if nb > 0:
                L = nb * BLOCK
                fq = q[:, :, :L].reshape(B, Hn, nb, BLOCK, d)
                fk_loc = k[:, :, :L].reshape(B, Hn, nb, BLOCK, d)
                fv_loc = v[:, :, :L].reshape(B, Hn, nb, BLOCK, d)
                mloc = M[..., :L, :L].reshape(1, 1, nb, BLOCK, nb, BLOCK)
                mloc = jnp.moveaxis(jnp.diagonal(mloc, axis1=2, axis2=4), -1, 2)
                mstr = M[..., :L, :Lg].reshape(1, 1, nb, BLOCK, ns, GBL)[..., -1]
                fmask = jnp.concatenate([mstr, mloc], axis=-1)
                fk = jnp.concatenate([jnp.broadcast_to(k_str[:, :, None], (B, Hn, nb, ns, d)), fk_loc], axis=-2)
                fv = jnp.concatenate([jnp.broadcast_to(v_str[:, :, None], (B, Hn, nb, ns, d)), fv_loc], axis=-2)
                w = jnp.einsum('bhnqd,bhnkd->bhnqk', fq, fk) * scale + fmask
                w = jax.nn.softmax(w, axis=-1)
                o1 = jnp.einsum('bhnqk,bhnkd->bhnqd', w, fv).reshape(B, Hn, L, d)
                outs.append(o1)
            if rem > 0:
                sq = q[:, :, -rem:]
                sk = jnp.concatenate([k_str, k[:, :, -rem:]], axis=2)
                sv = jnp.concatenate([v_str, v[:, :, -rem:]], axis=2)
                mstr2 = M[..., -rem:, :Lg].reshape(1, 1, rem, ns, GBL)[..., -1]
                smask = jnp.concatenate([mstr2, M[..., -rem:, -rem:]], axis=-1)
                w2 = jnp.einsum('bhqd,bhkd->bhqk', sq, sk) * scale + smask
                w2 = jax.nn.softmax(w2, axis=-1)
                o2 = jnp.einsum('bhqk,bhkd->bhqd', w2, sv)
                outs.append(o2)
            return jnp.concatenate(outs, axis=-2) if len(outs) > 1 else outs[0]
        B, S, Em = hidden_states.shape
        d = Em // H
        qkv = hidden_states @ c_attn_w + c_attn_b
        q, k, v = jnp.split(qkv, 3, axis=-1)

        def split_heads(t):
            return t.reshape(B, S, H, d).transpose(0, 2, 1, 3)
        q, k, v = (split_heads(q), split_heads(k), split_heads(v))
        causal = jnp.tril(jnp.ones((S, S), dtype=bool))
        M = jnp.where(causal, 0.0, NEG).astype(hidden_states.dtype)[None, None]
        attn_out = _sparse_attn(q, k, v, M)
        attn_out = attn_out.transpose(0, 2, 1, 3).reshape(B, S, Em)
        return attn_out @ c_proj_w + c_proj_b

    def _L1_ffn_ref(x, fast_b, w_fc, w_proj, u, v, gate):
        import jax, jax.numpy as jnp
        import numpy as np

        def _bitlinear(x, w_latent):
            scale = jax.lax.stop_gradient(jnp.clip(jnp.mean(jnp.abs(w_latent), axis=1, keepdims=True), 1e-05, None))
            tern = jnp.clip(jnp.round(w_latent / scale), -1.0, 1.0)
            w = w_latent + jax.lax.stop_gradient(tern - w_latent)
            return x @ (w * scale).T
        h = _bitlinear(x, w_fc) + gate * (x @ v.T @ fast_b.T @ u.T)
        r = jnp.maximum(h, 0.0)
        return _bitlinear(r * r, w_proj)

    def _L2_attn_ref(x, Wq_w, Wq_b, Wk_w, Wk_b, Wv_w, Wv_b, Wo_w, Wo_b):
        import jax, jax.numpy as jnp
        import numpy as np
        B, S, D = (4, 512, 256)
        KD, VD = (256, 256)
        q = x @ Wq_w.T + Wq_b
        k = x @ Wk_w.T + Wk_b
        v = x @ Wv_w.T + Wv_b
        key_dim = q.shape[-1]
        scores = jnp.einsum('bik,bjk->bij', q, k) / jnp.sqrt(jnp.float32(key_dim))
        sign = jnp.sign(scores)
        sign = sign + (sign == 0).astype(scores.dtype)
        seq = scores.shape[-1]
        upper = jnp.triu(jnp.ones((seq, seq), dtype=bool), 1)
        mask = jnp.where(upper, -jnp.inf, 1.0).astype(scores.dtype)
        masked = scores * sign * mask
        weights = jax.nn.softmax(masked, axis=-1)
        out = jnp.einsum('bij,bjd->bid', weights, v)
        return out @ Wo_w.T + Wo_b

    def _L2_ffn_ref(x, ln_gamma, ln_beta, fc1_q, fc1_scales, fc1_bias, fc2_q, fc2_scales, fc2_bias):
        import jax, jax.numpy as jnp
        import numpy as np
        B, S, H, F, G = (8, 512, 256, 1024, 128)
        EPS = 1e-05

        def _dequant(q, scales, g):
            K, N = q.shape
            w = (q.astype(jnp.float32) - 128.0).reshape(K // g, g, N) * scales[:, None, :]
            return w.reshape(K, N)
        residual = x
        mu = jnp.mean(x, axis=-1, keepdims=True)
        var = jnp.mean(jnp.square(x - mu), axis=-1, keepdims=True)
        h = (x - mu) * jax.lax.rsqrt(var + EPS) * ln_gamma + ln_beta
        hf = h.reshape(-1, H)
        w1 = _dequant(fc1_q, fc1_scales, G)
        y = hf @ w1 + fc1_bias
        y = jax.nn.silu(y)
        w2 = _dequant(fc2_q, fc2_scales, G)
        z = y @ w2 + fc2_bias
        return residual + 0.5 * z.reshape(residual.shape)

    def _L3_attn_ref(x, Wq, bq, Wk, bk, Wv, bv, Wo, bo):
        import math
        import jax, jax.numpy as jnp
        import numpy as np
        D_MODEL = 256
        NUM_HEADS = 16
        D_HEAD = D_MODEL // NUM_HEADS
        K_S = 32
        B, N = (2, 512)

        def _attn(x, Wq, bq, Wk, bk, Wv, bv, Wo, bo):
            b, n, _ = x.shape
            q = (x @ Wq.T + bq).reshape(b, n, NUM_HEADS, D_HEAD).transpose(0, 2, 1, 3)
            k = (x @ Wk.T + bk).reshape(b, n, NUM_HEADS, D_HEAD).transpose(0, 2, 1, 3)
            v = (x @ Wv.T + bv).reshape(b, n, NUM_HEADS, D_HEAD).transpose(0, 2, 1, 3)
            scores = jnp.einsum('bhqd,bhkd->bhqk', q, k) / math.sqrt(D_HEAD)
            causal = jnp.triu(jnp.ones((n, n), dtype=bool), k=1)
            neg_inf = jnp.array(-jnp.inf, dtype=scores.dtype)
            scores = jnp.where(causal, neg_inf, scores)
            vals, idx = jax.lax.top_k(scores, K_S)
            masked = jnp.full_like(scores, -jnp.inf)
            masked = jnp.put_along_axis(masked, idx, vals, axis=-1, inplace=False)
            attn = jax.nn.softmax(masked, axis=-1)
            out = jnp.einsum('bhqk,bhkd->bhqd', attn, v)
            out = out.transpose(0, 2, 1, 3).reshape(b, n, D_MODEL)
            y = out @ Wo.T + bo
            return (y, attn.mean(axis=1))

        def _reference_tuple_inner(x, Wq, bq, Wk, bk, Wv, bv, Wo, bo):
            return _attn(x, Wq, bq, Wk, bk, Wv, bv, Wo, bo)
        return _reference_tuple_inner(x, Wq, bq, Wk, bk, Wv, bv, Wo, bo)[0]

    def _L3_ffn_ref(x, router_w, w1, w2):
        import jax, jax.numpy as jnp
        import numpy as np
        TOP_K = 2
        B, S, D = x.shape
        E = router_w.shape[0]
        W = w1.shape[1] // E
        T = B * S
        xf = x.reshape(T, D)
        router_logits = jnp.einsum('td,ed->te', xf, router_w)
        router_probs = jax.nn.sigmoid(router_logits.astype(jnp.float32))
        top_w, sel = jax.lax.top_k(router_probs, TOP_K)
        top_w = top_w / (top_w.sum(axis=-1, keepdims=True) + 1e-20)
        top_w = top_w.astype(x.dtype)
        W1e = w1.reshape(D, E, W).transpose(1, 0, 2)
        W2e = w2.reshape(E, W, D)
        h = jnp.einsum('td,edw->etw', xf, W1e)
        a = jnp.square(jax.nn.relu(h))
        y = jnp.einsum('etw,ewd->etd', a, W2e)
        cw = jnp.zeros((T, E), dtype=x.dtype).at[jnp.arange(T)[:, None], sel].set(top_w)
        out = jnp.einsum('etd,te->td', y, cw)
        return out.reshape(B, S, D)
    h = _L0_tok_ref(x, L0_tok_W, L0_tok_b, L0_tok_cls_token, L0_tok_pos_embedding)
    h = jnp.concatenate([h, _L0_txt_ref(x_txt, L0_txt_emb, L0_txt_pos_emb, L0_txt_A_diag, L0_txt_B, L0_txt_C, L0_txt_D, L0_txt_w1, L0_txt_b1, L0_txt_w2, L0_txt_b2, L0_txt_ln1_s, L0_txt_ln1_b, L0_txt_ln2_s, L0_txt_ln2_b, L0_txt_lnf_s, L0_txt_lnf_b)], axis=1)
    h = h + _L0_attn_ref(_layernorm(h, axis=-1), L0_attn_norm_w, L0_attn_norm_b, L0_attn_in_proj_w, L0_attn_conv_w, L0_attn_conv_b, L0_attn_x_proj_w, L0_attn_dt_w, L0_attn_dt_b, L0_attn_A_log, L0_attn_D_skip, L0_attn_out_proj_w)
    h = h + _L0_ffn_ref(_layernorm(h, axis=-1), L0_ffn_router_w0, L0_ffn_wg0, L0_ffn_wu0, L0_ffn_wd0, L0_ffn_router_w1, L0_ffn_wg1, L0_ffn_wu1, L0_ffn_wd1)
    h = h + _L1_attn_ref(_layernorm(h, axis=-1), L1_attn_c_attn_w, L1_attn_c_attn_b, L1_attn_c_proj_w, L1_attn_c_proj_b)
    h = h + _L1_ffn_ref(_layernorm(h, axis=-1), L1_ffn_fast_b, L1_ffn_w_fc, L1_ffn_w_proj, L1_ffn_u, L1_ffn_v, L1_ffn_gate)
    h = h + _L2_attn_ref(_layernorm(h, axis=-1), L2_attn_Wq_w, L2_attn_Wq_b, L2_attn_Wk_w, L2_attn_Wk_b, L2_attn_Wv_w, L2_attn_Wv_b, L2_attn_Wo_w, L2_attn_Wo_b)
    h = h + _L2_ffn_ref(_layernorm(h, axis=-1), L2_ffn_ln_gamma, L2_ffn_ln_beta, L2_ffn_fc1_q, L2_ffn_fc1_scales, L2_ffn_fc1_bias, L2_ffn_fc2_q, L2_ffn_fc2_scales, L2_ffn_fc2_bias)
    h = h + _L3_attn_ref(_layernorm(h, axis=-1), L3_attn_Wq, L3_attn_bq, L3_attn_Wk, L3_attn_bk, L3_attn_Wv, L3_attn_bv, L3_attn_Wo, L3_attn_bo)
    h = h + _L3_ffn_ref(_layernorm(h, axis=-1), L3_ffn_router_w, L3_ffn_w1, L3_ffn_w2)
    return h

_drawn_inputs = setup_inputs


def setup_inputs(seed=0):
    import zlib

    import numpy as np

    out = dict(_drawn_inputs(seed))
    spreads = {'L0_txt_b1': (0.0, 0.295),
     'L0_txt_b2': (0.0, 0.1),
     'L0_txt_ln1_s': (1.0, 0.2),
     'L0_txt_ln1_b': (0.0, 0.1),
     'L0_txt_ln2_s': (1.0, 0.2),
     'L0_txt_ln2_b': (0.0, 0.273),
     'L0_txt_lnf_s': (1.0, 0.2),
     'L0_txt_lnf_b': (0.0, 0.1),
     'L0_attn_norm_w': (1.0, 0.2),
     'L0_attn_norm_b': (0.0, 0.1),
     'L0_attn_conv_b': (0.0, 0.1),
     'L0_attn_D_skip': (1.0, 0.535),
     'L1_attn_c_attn_b': (0.0, 0.724),
     'L1_attn_c_proj_b': (0.0, 0.311),
     'L2_ffn_ln_gamma': (1.0, 0.2),
     'L2_ffn_ln_beta': (0.0, 0.1),
     'L3_attn_bq': (0.0, 2.0),
     'L3_attn_bk': (0.0, 2.0),
     'L3_attn_bv': (0.0, 2.0),
     'L3_attn_bo': (0.0, 2.0)}
    factors = {'L0_tok_b': 3.506,
     'L0_tok_pos_embedding': 4.219,
     'L0_attn_dt_b': 64.0,
     'L0_ffn_router_w0': 8.0,
     'L0_ffn_wg0': 8.0,
     'L0_ffn_wu0': 8.0,
     'L0_ffn_wd0': 8.0,
     'L0_ffn_router_w1': 8.0,
     'L0_ffn_wg1': 8.0,
     'L0_ffn_wu1': 8.0,
     'L0_ffn_wd1': 8.0,
     'L1_attn_c_attn_w': 5.022,
     'L1_attn_c_proj_w': 3.676,
     'L1_ffn_fast_b': 8.0,
     'L1_ffn_w_fc': 6.94,
     'L1_ffn_w_proj': 4.078,
     'L1_ffn_u': 8.0,
     'L1_ffn_v': 8.0,
     'L2_attn_Wq_w': 8.0,
     'L2_attn_Wq_b': 50.217,
     'L2_attn_Wk_w': 8.0,
     'L2_attn_Wk_b': 42.156,
     'L2_attn_Wv_w': 4.314,
     'L2_attn_Wv_b': 60.529,
     'L2_attn_Wo_w': 5.064,
     'L2_attn_Wo_b': 41.815,
     'L2_ffn_fc1_bias': 64.0,
     'L2_ffn_fc2_bias': 64.0,
     'L3_attn_Wq': 8.0,
     'L3_attn_Wk': 8.0,
     'L3_attn_Wv': 8.0,
     'L3_attn_Wo': 8.0,
     'L3_ffn_router_w': 62.8,
     'L3_ffn_w1': 54.681,
     'L3_ffn_w2': 52.431}
    for name, (base, spread) in spreads.items():
        noise = np.random.default_rng([zlib.crc32(name.encode()), seed]).standard_normal(out[name].shape)
        drawn = base * np.exp(spread * noise) if base else spread * noise
        out[name] = jnp.asarray(drawn.astype(out[name].dtype))
    for name, factor in factors.items():
        out[name] = (out[name] * factor).astype(out[name].dtype)
    return out
```

```python
from contextlib import ExitStack, contextmanager

import numpy as np

import concourse.bass as bass
from concourse import mybir

ALU = mybir.AluOpType
ACT = mybir.ActivationFunctionType
F32 = mybir.dt.float32
BF16 = mybir.dt.bfloat16
I32 = mybir.dt.int32
AX_X = mybir.AxisListType.X

P = 128
D = 256
KD = D // P
BATCH = 16
PATCHES = 36
TEXT = 32
SEQ = 1 + PATCHES + TEXT
N = BATCH * SEQ
NCH = 3
CW = N // NCH
CHUNKS = [(c * CW, CW) for c in range(NCH)]
BANK = 512
VOCAB = 8000
LAYERS = 4
STATE = 64
FF = 1024
DI = 512
DS = 16
HEADS = 16
HD = D // HEADS
HPC = P // HD
QT = 112
NQT = 5
QPAD = QT * NQT
EPS = 1e-5
NEG = -1e30
TAKEN = -3e38
GATHER_SEM = 109
SEM0 = 110
TOPK = 32
ROWT = 92
NROWT = N // ROWT
E0, E3 = 32, 8

VEC = {}
for _name, _n in (
    ("tok_b", 2), ("cls", 2), ("lnf_s", 2), ("lnf_b", 2), ("norm_w", 2), ("norm_b", 2), ("conv_b", 4),
    ("dt_w", 4), ("dt_b", 4), ("D_skip", 4), ("conv_w", 16), ("A_log", 64), ("c_attn_b", 6), ("c_proj_b", 2),
    ("gate", 1), ("Wq_b", 2), ("Wk_b", 2), ("Wv_b", 2), ("Wo_b", 2), ("gamma", 2), ("beta", 2), ("fc1_b", 8),
    ("fc2_b", 2), ("bq", 2), ("bk", 2), ("bv", 2), ("bo", 2),
):
    VEC[_name] = (sum(n for _, n in VEC.values()), _n)
NVEC = sum(n for _, n in VEC.values())
LVEC = {"ln1_s": 0, "ln1_b": 2, "ln2_s": 4, "ln2_b": 6, "b1": 8, "b2": 16, "A": 18}
NLVEC = 19


@contextmanager
def stage(nc, *names):
    with ExitStack() as held:
        sems = [held.enter_context(nc.semaphore(name=n, num=SEM0 + i)) for i, n in enumerate(names)]
        with nc.Block() as block:
            yield (block, *sems)
        nc.all_engine_barrier(sems_to_clear=range(SEM0, SEM0 + len(names)))


def linker(eng, sem, start=0):
    count = [0]

    def link(ins):
        count[0] += 1
        ins.then_inc(sem, 1)
        eng.wait_ge(sem, start + count[0])

    return link


class Mem:

    def __init__(self, nc, dram):
        self.nc, self.dram = nc, dram
        sb = lambda name, shape, dt=F32: nc.alloc_sbuf_tensor(name, shape, dt)
        self.h = sb("h", [P, KD, N])
        self.xn = sb("xn", [P, KD, N])
        self.s1 = sb("s1", [P, KD, N])
        self.s2 = sb("s2", [P, KD, N])
        self.s3 = sb("s3", [P, KD, N])
        self.big1 = sb("big1", [P, 8, N])
        self.big2 = sb("big2", [P, 8, N])
        self.wa = sb("wa", [P, 8192])
        self.vec = sb("vec", [P, NVEC])
        self.lvec = sb("lvec", [P, NLVEC])
        self.mean_w = sb("mean_w", [P, P])
        self.ident = sb("ident", [P, P])
        self.small = sb("small", [P, 2048])
        self.parts = sb("parts", [P, 2, N], BF16)
        self.pick = sb("pick", [P, 32 * P], BF16)
        self.ident_bf = sb("ident_bf", [P, P], BF16)
        self.order = sb("order", [ROWT, E0])
        self.ps = nc.alloc_psum_tensor("ps", [P, 8 * BANK], F32)

        self.ps_bf = self.ps[:, :].bitcast(BF16)

    def v(self, name, k=0):
        c = VEC[name][0] + k
        return self.vec[:, c:c + 1]

    def bank(self, b, n=BANK, rows=P):
        return self.ps[0:rows, b * BANK:b * BANK + n]


def layernorm(nc, m, src, dst, chunks, gamma=None, beta=None, fold=None, work=None):
    cen, sq, std = work or (m.s1, m.s2, m.small)
    n_ch = len(chunks)
    with stage(nc, "mean_ready", "centred", "squared", "var_ready", "std_ready", "rstd_ready", "scaled") as (
            block, mean_ready, centred, squared, var_ready, std_ready, rstd_ready, scaled):

        @block.tensor
        def _(pe):
            for c, (o, n) in enumerate(chunks):
                for k in range(KD):
                    ins = nc.tensor.matmul(m.bank(c, n), m.mean_w[:, :], src(k, o, n), start=k == 0, stop=k == KD - 1)
                ins.then_inc(mean_ready, 1)
            for c, (o, n) in enumerate(chunks):
                pe.wait_ge(squared, KD * (c + 1))
                for k in range(KD):
                    ins = nc.tensor.matmul(m.bank(4 + c, n), m.mean_w[:, :], sq[:, k, o:o + n],
                                           start=k == 0, stop=k == KD - 1)
                ins.then_inc(var_ready, 1)

        @block.scalar
        def _(act):
            for c, (o, n) in enumerate(chunks):
                for k in range(KD):
                    act.wait_ge(centred, KD * c + k + 1)
                    nc.scalar.activation(sq[:, k, o:o + n], cen[:, k, o:o + n], ACT.Square).then_inc(squared, 1)
            for c, (o, n) in enumerate(chunks):
                act.wait_ge(var_ready, c + 1)
                nc.scalar.activation(std[:, o:o + n], m.bank(4 + c, n), ACT.Sqrt,
                                     bias=m.eps[:, 0:1]).then_inc(std_ready, 1)

        @block.vector
        def _(dve):
            for c, (o, n) in enumerate(chunks):
                dve.wait_ge(mean_ready, c + 1)
                for k in range(KD):
                    nc.vector.tensor_tensor(cen[:, k, o:o + n], src(k, o, n), m.bank(c, n),
                                            ALU.subtract).then_inc(centred, 1)
            done = 0
            for c, (o, n) in enumerate(chunks):
                dve.wait_ge(std_ready, c + 1)
                nc.vector.reciprocal(m.bank(4 + c, n), std[:, o:o + n]).then_inc(rstd_ready, 1)
                dve.wait_ge(rstd_ready, c + 1)
                for k in range(KD):
                    a, r, out = cen[:, k, o:o + n], m.bank(4 + c, n), dst(k, o, n)
                    if gamma is not None:
                        nc.vector.tensor_tensor(a, a, r, ALU.mult).then_inc(scaled, 1)
                        done += 1
                        dve.wait_ge(scaled, done)
                        if fold:
                            a = a.rearrange("p (b t) -> p b t", t=fold)
                        nc.vector.tensor_scalar(out, a, gamma(k), beta(k), ALU.mult, ALU.add)
                    else:
                        nc.vector.tensor_tensor(out, a, r, ALU.mult)


def linear(nc, m, src, w, n_in, n_out, chunks, drain, on="scalar", rows=P):
    with stage(nc, "product_ready", "product_taken", "drain_step") as (block, product_ready, product_taken, drain_step):

        @block.tensor
        def _(pe):
            g = 0
            for j in range(n_out):
                for o, n in chunks:
                    if g >= 8:
                        pe.wait_ge(product_taken, g - 7)
                    for k in range(n_in):
                        ins = nc.tensor.matmul(m.bank(g % 8, n, rows), w(k, j), src(k, o, n), start=k == 0,
                                               stop=k == n_in - 1)
                    ins.then_inc(product_ready, 1)
                    g += 1

        def take(eng):
            link = linker(eng, drain_step)
            g = 0
            for j in range(n_out):
                for o, n in chunks:
                    eng.wait_ge(product_ready, g + 1)
                    drain(j, o, n, m.bank(g % 8, n, rows), link).then_inc(product_taken, 1)
                    g += 1

        (block.scalar if on == "scalar" else block.vector)(take)


def add_to(nc, m, dst, bias=None):
    def drain(j, o, n, acc, link):
        out = dst[:, j, o:o + n]
        if bias is None:
            return nc.vector.tensor_tensor(out, out, acc, ALU.add)
        return nc.vector.scalar_tensor_tensor(out=out, in0=acc, scalar=bias(j), in1=out, op0=ALU.add, op1=ALU.add)
    return drain


def load(nc, *pairs):
    with stage(nc, "landed_sp", "landed_act") as (block, landed_sp, landed_act):

        @block.sync
        def _(sp):
            for dst, src in pairs[0::2]:
                sp.dma_start(dst, src).then_inc(landed_sp, 16)
            sp.wait_ge(landed_sp, 16 * len(pairs[0::2]))

        @block.scalar
        def _(act):
            for dst, src in pairs[1::2]:
                act.dma_start(dst, src).then_inc(landed_act, 16)
            if pairs[1::2]:
                act.wait_ge(landed_act, 16 * len(pairs[1::2]))


def full(t):
    return lambda k, o, n: t[:, k, o:o + n]


def setup(nc, m, d):
    m.eps = nc.alloc_sbuf_tensor("eps", [P, 1], F32)
    pick = m.big1[:, :, :].rearrange("p a b -> p (a b)")[:, 0:32 * P]
    with stage(nc, "landed") as (block, landed):

        @block.sync
        def _(sp):
            sp.dma_start(m.vec[:, :], d["vec"]).then_inc(landed, 16)
            sp.dma_start(m.ident[:, :], d["ident"]).then_inc(landed, 16)
            sp.dma_start(pick, d["pick"]).then_inc(landed, 16)
            sp.dma_start(m.order[:, :], d["order"]).then_inc(landed, 16)
            sp.wait_ge(landed, 64)

        @block.vector
        def _(dve):
            dve.wait_ge(landed, 64)
            nc.vector.tensor_copy(m.pick[:, :], pick)
            nc.vector.tensor_copy(m.ident_bf[:, :], m.ident[:, :])

        @block.gpsimd
        def _(pool):
            nc.gpsimd.memset(m.eps[:, :], EPS)
            nc.gpsimd.memset(m.mean_w[:, :], 1.0 / D)


def patch_tokens(nc, m, d):
    kin = 6
    w = m.wa[:, 0:kin * D].rearrange("p (k n) -> p k n", k=kin)
    patches = m.big1[:, :, :].rearrange("p a b -> p (a b)")[:, 0:kin * BATCH * PATCHES].rearrange(
        "p (k n) -> p k n", k=kin)
    pos = m.small[:, 0:KD * 37].rearrange("p (k t) -> p k t", k=KD)
    load(nc, (patches, d["patches"]), (w, d["tok_w"]), (pos, d["tok_pos"]))
    h4 = m.h[:, :, :].rearrange("p k (b t) -> p k b t", t=SEQ)
    half = BATCH // 2
    with stage(nc, "product_ready", "pos_ready", "step") as (block, product_ready, pos_ready, step):

        @block.tensor
        def _(pe):
            for j in range(KD):
                for c in range(2):
                    for k in range(kin):
                        ins = nc.tensor.matmul(m.bank(2 * j + c, half * PATCHES), w[:, k, j * P:j * P + P],
                                               patches[:, k, c * half * PATCHES:(c + 1) * half * PATCHES],
                                               start=k == 0, stop=k == kin - 1)
                    ins.then_inc(product_ready, 1)

        @block.vector
        def _(dve):
            for k in range(KD):
                nc.vector.tensor_scalar(pos[:, k, 1:37], pos[:, k, 1:37], m.v("tok_b", k), None,
                                        ALU.add).then_inc(pos_ready, 1)
                nc.vector.tensor_scalar(pos[:, k, 0:1], pos[:, k, 0:1], m.v("cls", k), None,
                                        ALU.add).then_inc(pos_ready, 1)
            dve.wait_ge(pos_ready, 2 * KD)
            for k in range(KD):
                nc.vector.tensor_copy(h4[:, k, :, 0:1], pos[:, k, 0:1].unsqueeze(1).broadcast_to([P, BATCH, 1]))
            for j in range(KD):
                for c in range(2):
                    dve.wait_ge(product_ready, 2 * j + c + 1)
                    nc.vector.tensor_tensor(
                        h4[:, j, c * half:(c + 1) * half, 1:37],
                        m.bank(2 * j + c, half * PATCHES).rearrange("p (b t) -> p b t", t=PATCHES),
                        pos[:, j:j + 1, 1:37].broadcast_to([P, half, PATCHES]), ALU.add)


def text_encoder(nc, m, d):
    nt = BATCH * TEXT
    flat1 = m.big1[:, :, :].rearrange("p a b -> p (a b)")
    x = flat1[:, 0:KD * nt].rearrange("p (k n) -> p k n", k=KD)
    xn = flat1[:, KD * nt:2 * KD * nt].rearrange("p (k n) -> p k n", k=KD)
    cen = flat1[:, 2 * KD * nt:3 * KD * nt].rearrange("p (k n) -> p k n", k=KD)
    sq = flat1[:, 3 * KD * nt:4 * KD * nt].rearrange("p (k n) -> p k n", k=KD)
    rows = flat1[:, 4 * KD * nt:6 * KD * nt].rearrange("p (j n) -> p j n", j=8)[:, 0:4, :]
    hid = m.big2[:, :, :].rearrange("p a b -> p (a b)")[:, 0:8 * nt].rearrange("p (k n) -> p k n", k=8)
    work = (cen, sq, m.small)
    idx = nc.alloc_sbuf_tensor("idx", [P, 4], I32)
    wrapped = nc.alloc_sbuf_tensor("wrapped", [P, 4], I32)
    pos = m.xn[:, 0, 0:KD * TEXT].rearrange("p (k t) -> p k t", k=KD)
    fresh = m.s1[0:STATE, 0, 0:nt]
    load(nc, (idx[:, :], d["tokens"]), (pos, d["txt_pos"]), (fresh, d["fresh"]))
    gathered = nc.alloc_semaphore("gathered", num=GATHER_SEM)
    with stage(nc, "index_step", "turned") as (block, index_step, turned):

        @block.vector
        def _(dve):
            link = linker(dve, index_step)
            link(nc.vector.tensor_scalar(wrapped[:, :], idx[:, :], 0.0, float(VOCAB), ALU.is_lt, ALU.mult))
            link(nc.vector.tensor_tensor(idx[:, :], idx[:, :], wrapped[:, :], ALU.add))
            nc.vector.tensor_scalar(idx[:, :], idx[:, :], 0.0, float(VOCAB - 1), ALU.max,
                                    ALU.min).then_inc(index_step, 1)
            for k in range(KD):
                dve.wait_ge(turned, k + 1)
                nc.vector.tensor_tensor(
                    x[:, k, :].rearrange("p (b t) -> p b t", t=TEXT),
                    m.bank(k).rearrange("p (b t) -> p b t", t=TEXT),
                    pos[:, k:k + 1, :].broadcast_to([P, BATCH, TEXT]), ALU.add)

        @block.gpsimd
        def _(pool):
            pool.wait_ge(index_step, 3)
            for j in range(4):
                pool.indirect_dma_start(
                    rows[:, j, :], None, d["emb"], bass.IndirectOffsetOnAxis(ap=idx[:, j:j + 1], axis=0),
                ).then_inc(gathered, 16)

        @block.tensor
        def _(pe):
            pe.wait_ge(gathered, 64)
            for k in range(KD):
                for j in range(4):
                    ins = nc.tensor.transpose(m.bank(k)[:, j * P:j * P + P], rows[:, j, k * P:k * P + P],
                                              m.ident[:, :])
                ins.then_inc(turned, 1)

    wB = m.wa[:, 0:KD * STATE].rearrange("p (k n) -> p k n", k=KD)
    wD = m.wa[:, 128:128 + KD * D].rearrange("p (k n) -> p k n", k=KD)
    wC = m.wa[0:STATE, 640:640 + D]
    w1 = m.wa[:, 1024:1024 + KD * FF].rearrange("p (k n) -> p k n", k=KD)
    w2 = m.wa[:, 4096:4096 + 8 * D].rearrange("p (k n) -> p k n", k=8)
    decay = m.s2[0:STATE, 0, 0:nt]
    states = m.s2[0:STATE, 1, 0:nt]
    a = m.s1[0:STATE, 1, 0:1]
    L = LVEC
    lv = lambda name, k: m.lvec[:, L[name] + k:L[name] + k + 1]
    chunks = [(0, nt)]
    with nc.Fori(0, LAYERS) as layer:
        load(nc, (wB, d["B"][layer]), (wD, d["Dw"][layer]), (wC, d["C"][layer]), (w1, d["w1"][layer]),
             (m.lvec[:, :], d["lvec"][layer]), (w2, d["w2"][layer]))
        layernorm(nc, m, full(x), full(xn), chunks, lambda k: lv("ln1_s", k), lambda k: lv("ln1_b", k), work=work)
        with stage(nc, "input_ready", "decay_step", "scanned", "mixed") as (
                block, input_ready, decay_step, scanned, mixed):

            @block.scalar
            def _(act):
                nc.scalar.activation(a, m.lvec[0:STATE, L["A"]:L["A"] + 1], ACT.Sigmoid).then_inc(decay_step, 1)

            @block.tensor
            def _(pe):
                for k in range(KD):
                    ins = nc.tensor.matmul(m.bank(0, nt, STATE), wB[:, k, :], xn[:, k, :], start=k == 0,
                                           stop=k == KD - 1)
                ins.then_inc(input_ready, 1)
                for j in range(KD):
                    for k in range(KD):
                        nc.tensor.matmul(m.bank(1 + j, nt), wD[:, k, j * P:j * P + P], xn[:, k, :], start=k == 0,
                                         stop=False)
                    if j == 0:
                        pe.wait_ge(scanned, 1)
                    nc.tensor.matmul(m.bank(1 + j, nt), wC[:, j * P:j * P + P], states, start=False,
                                     stop=True).then_inc(mixed, 1)

            @block.vector
            def _(dve):
                dve.wait_ge(decay_step, 1)
                nc.vector.tensor_scalar(decay, fresh, a, None, ALU.mult).then_inc(decay_step, 1)
                dve.wait_ge(decay_step, 2)
                dve.wait_ge(input_ready, 1)
                nc.vector.tensor_tensor_scan(states, decay, m.bank(0, nt, STATE), 0.0, ALU.mult,
                                             ALU.add).then_inc(scanned, 1)
                for j in range(KD):
                    dve.wait_ge(mixed, j + 1)
                    nc.vector.tensor_tensor(x[:, j, :], x[:, j, :], m.bank(1 + j, nt), ALU.add)

        layernorm(nc, m, full(x), full(xn), chunks, lambda k: lv("ln2_s", k), lambda k: lv("ln2_b", k), work=work)
        linear(nc, m, full(xn), lambda k, j: w1[:, k, j * P:j * P + P], KD, 8, chunks,
               lambda j, o, n, acc, link: nc.scalar.activation(hid[:, j, o:o + n], acc, ACT.Gelu, bias=lv("b1", j)))
        linear(nc, m, full(hid), lambda k, j: w2[:, k, j * P:j * P + P], 8, KD, chunks,
               add_to(nc, m, x, lambda j: lv("b2", j)), on="vector")
    h4 = m.h[:, :, :].rearrange("p k (b t) -> p k b t", t=SEQ)
    layernorm(nc, m, full(x), lambda k, o, n: h4[:, k, o // TEXT:(o + n) // TEXT, 1 + PATCHES:SEQ], chunks,
              lambda k: m.v("lnf_s", k), lambda k: m.v("lnf_b", k), fold=TEXT, work=work)


def pieces(base, n):
    at = base
    while at < base + n:
        k = min(base + n, (at // BANK + 1) * BANK) - at
        yield at, at - base, k
        at += k


def selective_scan(nc, m, d):
    x2 = m.big2[:, 0:KD, :]
    xi, z = m.big1[:, 0:4, :], m.big1[:, 4:8, :]
    xc, delta = m.big2[:, 0:4, :], m.big2[:, 4:8, :]
    w_in = m.wa[:, 0:2048].rearrange("p (k n) -> p k n", k=KD)
    w_dt = m.wa[:, 2048:2560].rearrange("p (k n) -> p k n", k=4)
    w_bc = m.wa[:, 2560:3072].rearrange("p (k n) -> p k n", k=4)
    w_out = m.wa[:, 3072:4096].rearrange("p (k n) -> p k n", k=4)
    neg_a = m.small[:, 1200:1264]
    load(nc, (w_in, d["in_proj"]), (w_dt, d["dt_rows"]), (w_bc, d["bc_rows"]), (w_out, d["out_proj"]))
    layernorm(nc, m, full(m.h), full(m.xn), CHUNKS)
    layernorm(nc, m, full(m.xn), full(x2), CHUNKS, lambda k: m.v("norm_w", k), lambda k: m.v("norm_b", k))
    linear(nc, m, full(x2), lambda k, j: w_in[:, k, j * P:j * P + P], KD, 8, CHUNKS,
           lambda j, o, n, acc, link: nc.scalar.copy(m.big1[:, j, o:o + n], acc))

    with stage(nc, "conv_step", "conv_ready", "rates_ready") as (block, conv_step, conv_ready, rates_ready):
        @block.vector
        def _(dve):
            link = linker(dve, conv_step)
            for k in range(4):
                link(nc.vector.tensor_scalar(xc[:, k, :], xi[:, k, :], m.v("conv_w", 4 * k + 3), m.v("conv_b", k),
                                             ALU.mult, ALU.add))
                to = xc[:, k, :].rearrange("p (b t) -> p b t", t=SEQ)
                of = xi[:, k, :].rearrange("p (b t) -> p b t", t=SEQ)
                for back in (1, 2, 3):
                    ins = nc.vector.scalar_tensor_tensor(
                        out=to[:, :, back:], in0=of[:, :, :SEQ - back], scalar=m.v("conv_w", 4 * k + 3 - back),
                        in1=to[:, :, back:], op0=ALU.mult, op1=ALU.add)
                    link(ins)
                nc.vector.engine_nop().then_inc(conv_ready, 1)
            dve.wait_ge(rates_ready, 1)
            nc.vector.tensor_scalar(neg_a, neg_a, -1.0, None, ALU.mult)

        @block.scalar
        def _(act):
            c = VEC["A_log"][0]
            nc.scalar.activation(neg_a, m.vec[:, c:c + 64], ACT.Exp).then_inc(rates_ready, 1)
            for k in range(4):
                act.wait_ge(conv_ready, k + 1)
                nc.scalar.activation(xc[:, k, :], xc[:, k, :], ACT.Silu)
            for k in range(4):
                nc.scalar.activation(z[:, k, :], z[:, k, :], ACT.Silu)

    with stage(nc, "dt_ready", "dt_step", "log_ready", "dt_taken", "relu_ready") as (
            block, dt_ready, dt_step, log_ready, dt_taken, relu_ready):
        @block.tensor
        def _(pe):
            for c, (o, n) in enumerate(CHUNKS):
                for k in range(4):
                    ins = nc.tensor.matmul(m.bank(c, n), w_dt[:, k, :], xc[:, k, o:o + n], start=k == 0, stop=k == 3)
                ins.then_inc(dt_ready, 1)

        @block.scalar
        def _(act):
            link = linker(act, dt_step)
            for c, (o, n) in enumerate(CHUNKS):
                act.wait_ge(dt_ready, c + 1)
                for k in range(4):
                    ins = nc.scalar.activation(delta[:, k, o:o + n], m.bank(c, n), ACT.Identity,
                                               scale=m.v("dt_w", k), bias=m.v("dt_b", k))
            link(ins)
            for k in range(4):
                t = m.s1[:, k % 2, :]
                if k >= 2:
                    act.wait_ge(dt_taken, k - 1)
                link(nc.scalar.activation(t, delta[:, k, :], ACT.Abs))
                link(nc.scalar.activation(t, t, ACT.Exp, scale=-1.0))
                nc.scalar.activation(t, t, ACT.Ln, bias=1.0).then_inc(log_ready, 1)

        @block.vector
        def _(dve):
            for k in range(4):
                dve.wait_ge(log_ready, k + 1)
                nc.vector.scalar_tensor_tensor(out=delta[:, k, :], in0=delta[:, k, :], scalar=0.0,
                                               in1=m.s1[:, k % 2, :], op0=ALU.max, op1=ALU.add).then_inc(dt_taken, 1)
            dve.wait_ge(dt_taken, 4)
            for k in range(4):
                nc.vector.tensor_tensor(xi[:, k, :], delta[:, k, :], xc[:, k, :], ALU.mult)

    def split(j, o, n, acc, link):
        t1, r, t2 = m.parts[:, 0, o:o + n], m.s1[:, 0, o:o + n], m.parts[:, 1, o:o + n]
        link(nc.vector.tensor_copy(t1, acc))
        link(nc.vector.tensor_tensor(r, acc, t1, ALU.subtract))
        link(nc.vector.tensor_copy(t2, r))
        link(nc.vector.tensor_copy(t1[32:64, :], t2[32:64, :]))
        link(nc.vector.tensor_tensor(r, r, t2, ALU.subtract))
        return nc.vector.tensor_copy(t1[64:96, :], r[64:96, :])
    linear(nc, m, full(xc), lambda k, j: w_bc[:, k, :], 4, 1, CHUNKS, split, on="vector")

    decay = [m.s1[:, i, :] for i in range(2)]
    state = [m.s2[:, i, :] for i in range(2)]
    c_row = [m.s3[:, i, :] for i in range(2)]
    inflow, seen, skip = m.wa[:, 4096:4096 + N], [m.wa[:, 4096 + i * N:4096 + (i + 1) * N] for i in (1, 2)], \
        m.small[:, 0:N]
    tokens = lambda a: a.rearrange("p (b t) -> p b t", t=SEQ)
    Y, B = 0, 3 * BANK
    NQ, QW = 4, N // 4
    for k in range(4):
        u = xi[:, k, :]
        with stage(nc, "cleared", "skip_ready", "b_ready", "c_ready", "c_taken", "summed", "decay_ready",
                   "inflow_ready", "scanned", "seen_ready") as (
                block, cleared, skip_ready, b_ready, c_ready, c_taken, summed, decay_ready, inflow_ready, scanned,
                seen_ready):

            @block.tensor
            def _(pe):
                def spread_b(row):
                    for at, o, n in pieces(B, N):
                        ins = nc.tensor.matmul(m.ps[:, at:at + n], m.pick[:, bass.ds(row * P, P)],
                                               m.parts[:, 0, o:o + n], start=True, stop=True)
                    ins.then_inc(b_ready, 1)

                def spread_c(i, peeled=False):
                    for q in range(NQ):
                        if not peeled or q >= 2:
                            pe.wait_ge(c_taken, i * NQ + (q - 1))
                        nc.tensor.matmul(m.bank(6 + q % 2, QW), m.pick[:, bass.ds((i + DS) * P, P)],
                                         m.parts[:, 0, q * QW:(q + 1) * QW], start=True, stop=True).then_inc(c_ready, 1)

                def add_y(what, first):
                    for at, o, n in pieces(Y, N):
                        ins = nc.tensor.matmul(m.ps[:, at:at + n], m.ident[:, :], what[:, o:o + n], start=first,
                                               stop=False, skip_group_check=True)
                    return ins

                spread_b(0)
                pe.wait_ge(skip_ready, 1)
                add_y(skip, True)
                spread_c(0, True)
                pe.wait_ge(inflow_ready, 1)
                spread_b(1)
                spread_c(1)
                pe.wait_ge(seen_ready, 1)
                add_y(seen[0], False).then_inc(summed, 1)
                with pe.Fori(0, DS // 2 - 1) as pair:
                    for s in range(2):
                        i = pair * 2 + 1
                        pe.wait_ge(inflow_ready, i + (s + 1))
                        spread_b(i + (s + 1))
                        spread_c(i + (s + 1))
                        pe.wait_ge(seen_ready, i + (s + 1))
                        add_y(seen[(s + 1) % 2], False).then_inc(summed, 1)
                pe.wait_ge(seen_ready, DS)
                add_y(seen[1], False).then_inc(summed, 1)

            @block.scalar
            def _(act):
                act.wait_ge(cleared, 1)

                def rates(i, s, peeled=False):
                    if not peeled:
                        act.wait_ge(scanned, i + (s - 1))
                    nc.scalar.activation(
                        tokens(decay[s])[:, :, 1:], tokens(delta[:, k, :])[:, :, 1:], ACT.Exp,
                        scale=m.small[:, bass.ds(i + (1200 + k * DS + s), 1)]).then_inc(decay_ready, 1)
                    for q in range(NQ):
                        act.wait_ge(c_ready, i * NQ + (s * NQ + q + 1))
                        if q == 0 and not peeled:
                            act.wait_ge(seen_ready, i + (s - 1))
                        nc.scalar.copy(c_row[s][:, q * QW:(q + 1) * QW], m.bank(6 + q % 2, QW)).then_inc(c_taken, 1)

                for s in range(2):
                    rates(0, s, True)
                with act.Fori(1, DS // 2) as pair:
                    for s in range(2):
                        rates(pair * 2, s)

            @block.gpsimd
            def _(pool):
                def see(i, s, peeled=False):
                    pool.wait_ge(scanned, i + (s + 1))
                    pool.wait_ge(c_taken, i * NQ + (s + 1) * NQ)
                    if not peeled:
                        pool.wait_ge(summed, i + (s - 1))
                    nc.gpsimd.tensor_tensor(seen[s], state[s], c_row[s], ALU.mult).then_inc(seen_ready, 1)

                for s in range(2):
                    see(0, s, True)
                with pool.Fori(1, DS // 2) as pair:
                    for s in range(2):
                        see(pair * 2, s)

            @block.vector
            def _(dve):
                nc.vector.tensor_scalar(skip, xc[:, k, :], m.v("D_skip", k), None, ALU.mult).then_inc(skip_ready, 1)
                nc.vector.memset(tokens(decay[0])[:, :, 0:1], 0.0)
                nc.vector.memset(tokens(decay[1])[:, :, 0:1], 0.0).then_inc(cleared, 1)
                dve.wait_ge(cleared, 1)

                def step(i, s, peeled=False):
                    dve.wait_ge(b_ready, i + (s + 1))
                    if not peeled or s:
                        dve.wait_ge(scanned, i + s)
                    nc.vector.tensor_tensor(inflow, u, m.ps[:, B:B + N], ALU.mult).then_inc(inflow_ready, 1)
                    dve.wait_ge(inflow_ready, i + (s + 1))
                    dve.wait_ge(decay_ready, i + (s + 1))
                    if not peeled:
                        dve.wait_ge(seen_ready, i + (s - 1))
                    nc.vector.tensor_tensor_scan(state[s], decay[s], inflow, 0.0, ALU.mult,
                                                 ALU.add).then_inc(scanned, 1)

                for s in range(2):
                    step(0, s, True)
                with dve.Fori(1, DS // 2) as pair:
                    for s in range(2):
                        step(pair * 2, s)
                dve.wait_ge(summed, DS)
                nc.vector.tensor_tensor(z[:, k, :], z[:, k, :], m.ps[:, Y:Y + N], ALU.mult)

    def residual(j, o, n, acc, link):
        out = m.h[:, j, o:o + n]
        link(nc.vector.tensor_tensor(out, out, acc, ALU.add))
        return nc.vector.tensor_tensor(out, out, m.xn[:, j, o:o + n], ALU.add)
    linear(nc, m, full(z), lambda k, j: w_out[:, k, j * P:j * P + P], 4, KD, CHUNKS, residual, on="vector")


def route(nc, m, groups, experts, w, sigmoid):
    g_all = NROWT * groups
    ne = groups * experts
    cols_ = g_all * experts
    flat = m.big1[:, :, :].rearrange("p a b -> p (a b)")
    tile3 = lambda i, e=experts: flat[0:ROWT, i * 768:i * 768 + g_all * e].rearrange("p (g e) -> p g e", e=e)
    sc, key, one, two, tmp = (tile3(i) for i in range(5))
    order = m.order[0:ROWT, E0 - experts:E0].unsqueeze(1).broadcast_to([ROWT, g_all, experts])
    red = [m.small[0:ROWT, 32 * i:32 * i + g_all].unsqueeze(2) for i in range(4)]
    wide = lambda a: a.broadcast_to([ROWT, g_all, experts])
    parts = m.big2[:, :, :].rearrange("p a b -> p (a b)")[0:ROWT, 0:g_all * 64].bitcast(BF16).rearrange(
        "p (g s) -> p g s", s=P)
    half = NROWT // 2
    with stage(nc, "logits_ready", "logits_taken", "exp_ready", "route_step", "parts_ready", "turned",
               "turned_taken") as (
            block, logits_ready, logits_taken, exp_ready, route_step, parts_ready, turned, turned_taken):

        @block.tensor
        def _(pe):
            for t in range(NROWT):
                at = (t // half) * BANK + (t % half) * ne
                for k in range(KD):
                    ins = nc.tensor.matmul(m.ps[0:ROWT, at:at + ne], m.xn[:, k, t * ROWT:(t + 1) * ROWT],
                                           w[:, k, :], start=k == 0, stop=k == KD - 1)
            ins.then_inc(logits_ready, 1)
            pe.wait_ge(parts_ready, 1)
            for g in range(groups):
                for t in range(NROWT):
                    at = (2 + 2 * g) * 2 * BANK + (t // 11) * 2 * BANK + (t % 11) * ROWT
                    ins = nc.tensor.transpose(m.ps_bf[:, at:at + ROWT], parts[:, t * groups + g, :],
                                              m.ident_bf[0:ROWT, 0:ROWT])
                ins.then_inc(turned, 1)

        @block.scalar
        def _(act):
            act.wait_ge(logits_taken, 1)
            nc.scalar.activation(sc, sc, ACT.Exp, scale=-1.0 if sigmoid else 1.0).then_inc(exp_ready, 1)
            for g in range(groups):
                act.wait_ge(turned, g + 1)
                base = (2 + 2 * g) * 2 * BANK
                nc.scalar.copy(m.parts[:, g, 0:11 * ROWT], m.ps_bf[:, base:base + 11 * ROWT])
                nc.scalar.copy(m.parts[:, g, 11 * ROWT:N], m.ps_bf[:, base + 2 * BANK:base + 2 * BANK + ROWT])

        @block.vector
        def _(dve):
            link = linker(dve, route_step)
            tt, ts = nc.vector.tensor_tensor, nc.vector.tensor_scalar
            link(nc.vector.memset(parts, 0.0))
            dve.wait_ge(logits_ready, 1)
            for b in range(2):
                link(nc.vector.tensor_copy(sc[:, b * (g_all // 2):(b + 1) * (g_all // 2), :],
                                           m.ps[0:ROWT, b * BANK:b * BANK + cols_ // 2].rearrange(
                                               "p (g e) -> p g e", e=experts)))
            if sigmoid:
                nc.vector.engine_nop().then_inc(logits_taken, 1)
                dve.wait_ge(exp_ready, 1)
                link(ts(sc, sc, 1.0, None, ALU.add))
                link(nc.vector.reciprocal(sc, sc))
            else:
                link(nc.vector.tensor_reduce(red[0].squeeze(2), sc, AX_X, ALU.max))
                tt(sc, sc, wide(red[0]), ALU.subtract).then_inc(logits_taken, 1)
                dve.wait_ge(exp_ready, 1)
                link(nc.vector.tensor_reduce(red[0].squeeze(2), sc, AX_X, ALU.add))
                link(nc.vector.reciprocal(red[0], red[0]))
                link(tt(sc, sc, wide(red[0]), ALU.mult))

            def first_of_max(of, best, out):
                link(nc.vector.tensor_reduce(best.squeeze(2), of, AX_X, ALU.max))
                link(tt(key, of, wide(best), ALU.is_equal))
                link(tt(key, key, order, ALU.mult))
                link(nc.vector.tensor_reduce(red[3].squeeze(2), key, AX_X, ALU.max))
                link(tt(out, order, wide(red[3]), ALU.is_equal))

            first_of_max(sc, red[0], one)
            link(nc.vector.scalar_tensor_tensor(out=tmp, in0=one, scalar=-4.0, in1=sc, op0=ALU.mult, op1=ALU.add))
            first_of_max(tmp, red[1], two)
            link(tt(one, one, wide(red[0]), ALU.mult))
            link(tt(two, two, wide(red[1]), ALU.mult))
            link(tt(one, one, two, ALU.add))
            if sigmoid:
                link(tt(red[0], red[0], red[1], ALU.add))
                link(ts(red[0], red[0], 1e-20, None, ALU.add))
                link(nc.vector.reciprocal(red[0], red[0]))
                link(tt(one, one, wide(red[0]), ALU.mult))
            else:
                link(ts(one, one, 0.5, None, ALU.mult))
            for p in range(3):
                part = parts[:, :, 32 * p:32 * p + experts]
                link(nc.vector.tensor_copy(part, one))
                if p < 2:
                    link(tt(one, one, part, ALU.subtract))
            nc.vector.engine_nop().then_inc(parts_ready, 1)


def mixture0(nc, m, d):
    wr = m.small[:, 1200:1200 + KD * 2 * E0].rearrange("p (k n) -> p k n", k=KD)
    load(nc, (wr, d["router"]))
    layernorm(nc, m, full(m.h), full(m.xn), CHUNKS)
    route(nc, m, 2, E0, wr, False)
    per, groups = 4, 2
    span = per * 768
    units = [(g, c, e) for g in range(groups) for c in range(NCH) for e in range(per)]
    nu = len(units)
    w = [m.big1[:, :, :].rearrange("p a b -> p (a b)")[:, g * span:(g + 1) * span].rearrange(
        "p (e n) -> p e n", e=per) for g in range(groups)]
    flat2 = m.big2[:, :, :].rearrange("p a b -> p (a b)")
    gated = [flat2[:, i * CW:(i + 1) * CW] for i in range(2)]
    hidden = [flat2[:, (2 + i) * CW:(3 + i) * CW] for i in range(2)]
    iters = E0 // per
    with stage(nc, "weights_0", "weights_1", "gate_ready", "up_ready", "silu_ready", "hidden_step", "down_ready",
               "sum_taken", "group_done") as (
            block, weights_0, weights_1, gate_ready, up_ready, silu_ready, hidden_step, down_ready, sum_taken,
            group_done):
        weights = (weights_0, weights_1)

        @block.sync
        def _(sp):
            for g in range(groups):
                sp.dma_start(w[g].rearrange("p e n -> p (e n)"), d["experts"][0, g]).then_inc(weights[g], 16)
            with sp.Fori(1, iters) as i:
                for g in range(groups):
                    sp.wait_ge(group_done, groups * (i - 1) + g + 1)
                    sp.dma_start(w[g].rearrange("p e n -> p (e n)"), d["experts"][i, g]).then_inc(weights[g], 16)

        @block.tensor
        def _(pe):
            def first(i, u):
                g, c, e = units[u]
                o = c * CW
                if c == 0 and e == 0:
                    pe.wait_ge(weights[g], 16 * (i + 1))
                if u >= 2:
                    pe.wait_ge(hidden_step, 2 * (nu * i + u - 1))
                b = u % 2
                for k in range(KD):
                    ins = nc.tensor.matmul(m.bank(b, CW), w[g][:, e, k * P:k * P + P], m.xn[:, k, o:o + CW],
                                           start=k == 0, stop=k == KD - 1)
                ins.then_inc(gate_ready, 1)
                for k in range(KD):
                    nc.tensor.matmul(m.bank(2 + b, CW), w[g][:, e, 256 + k * P:256 + k * P + P],
                                     m.xn[:, k, o:o + CW], start=k == 0, stop=k == KD - 1)
                nc.tensor.matmul(m.bank(4 + b, CW), m.pick[:, bass.ds((i * per + e) * P, P)],
                                 m.parts[:, g, o:o + CW], start=True, stop=True).then_inc(up_ready, 1)

            def down(i, u):
                g, c, e = units[u]
                pe.wait_ge(hidden_step, 2 * (nu * i + u + 1))
                if e == 0 and not (isinstance(i, int) and u == 0):
                    pe.wait_ge(sum_taken, KD * (nu // per) * i + KD * (u // per))
                for j in range(KD):
                    ins = nc.tensor.matmul(m.bank(6 + j, CW), w[g][:, e, 512 + j * P:512 + j * P + P],
                                           hidden[u % 2], start=e == 0, stop=e == per - 1)
                if e == per - 1:
                    ins.then_inc(down_ready, 1)
                    if c == NCH - 1:
                        pe.wait_ge(down_ready, nu // per * i + u // per + 1)
                        pe.sem_inc(group_done, 1)

            def experts_of(i):
                first(i, 0)
                for u in range(nu):
                    if u + 1 < nu:
                        first(i, u + 1)
                    down(i, u)

            experts_of(0)
            with pe.Fori(1, iters) as i:
                experts_of(i)

        @block.scalar
        def _(act):
            with act.Fori(0, iters) as i:
                for u in range(nu):
                    act.wait_ge(gate_ready, nu * i + u + 1)
                    if u >= 2:
                        act.wait_ge(hidden_step, 2 * (nu * i + u - 1))
                    nc.scalar.activation(gated[u % 2], m.bank(u % 2, CW), ACT.Silu).then_inc(silu_ready, 1)

        @block.vector
        def _(dve):
            def take_sum(i, s):
                g, c, _ = units[s * per]
                dve.wait_ge(down_ready, nu // per * i + s + 1)
                for j in range(KD):
                    out = m.h[:, j, c * CW:(c + 1) * CW]
                    nc.vector.tensor_tensor(out, out, m.bank(6 + j, CW), ALU.add).then_inc(sum_taken, 1)

            with dve.Fori(0, iters) as i:
                for u in range(nu):
                    g, c, e = units[u]
                    dve.wait_ge(silu_ready, nu * i + u + 1)
                    dve.wait_ge(up_ready, nu * i + u + 1)
                    nc.vector.tensor_tensor(gated[u % 2], gated[u % 2], m.bank(2 + u % 2, CW),
                                            ALU.mult).then_inc(hidden_step, 1)
                    dve.wait_ge(hidden_step, 2 * (nu * i + u) + 1)
                    nc.vector.tensor_tensor(hidden[u % 2], gated[u % 2], m.bank(4 + u % 2, CW),
                                            ALU.mult).then_inc(hidden_step, 1)
                    if e == 0 and u:
                        take_sum(i, u // per - 1)
                take_sum(i, nu // per - 1)
                dve.wait_ge(sum_taken, KD * (nu // per) * (i + 1))


def value_rows(nc, m, w_v, v):
    with stage(nc, "rows_ready", "rows_taken") as (block, rows_ready, rows_taken):

        @block.tensor
        def _(pe):
            for b in range(BATCH):
                if b >= 4:
                    pe.wait_ge(rows_taken, b - 3)
                for k in range(KD):
                    ins = nc.tensor.matmul(m.bank(b % 4, D, SEQ), m.xn[:, k, b * SEQ:(b + 1) * SEQ], w_v(k),
                                           start=k == 0, stop=k == KD - 1)
                ins.then_inc(rows_ready, 1)

        @block.scalar
        def _(act):
            for b in range(BATCH):
                act.wait_ge(rows_ready, b + 1)
                nc.scalar.copy(v[:, b, :], m.bank(b % 4, D, SEQ)).then_inc(rows_taken, 1)


def attend(nc, m, mask_dram, v_bias, topk):
    q, k = m.big1[:, 0:2, :], m.big1[:, 2:4, :]
    flat1 = m.big1[:, :, :].rearrange("p a b -> p (a b)")
    v = flat1[0:SEQ, 4 * N:4 * N + BATCH * D].rearrange("p (b n) -> p b n", b=BATCH)
    flat2 = m.big2[:, :, :].rearrange("p a b -> p (a b)")
    q_out = [flat2[:, c * QPAD:(c + 1) * QPAD] for c in range(2)]
    v_out = [flat2[0:SEQ, 1200 + c * HPC * P:1200 + (c + 1) * HPC * P] for c in range(2)]
    turned_sb = [flat2[0:SEQ, 3300 + c * QPAD:3300 + (c + 1) * QPAD] for c in range(2)]
    score = [flat2[0:QT, 4500 + c * NQT * SEQ:4500 + (c + 1) * NQT * SEQ] for c in range(2)]
    left = [flat2[0:QT, 5200 + c * NQT * SEQ:5200 + (c + 1) * NQT * SEQ] for c in range(2)]
    mask = flat2[0:QT, 5900:5900 + NQT * SEQ]
    head_of = flat2[:, 6300:6300 + HPC]
    top8 = [flat2[0:QT, 6320 + c * 160:6320 + (c + 1) * 160].rearrange("p (j r e) -> p j r e", j=NQT, r=4)
            for c in range(2)]
    row_max = [flat2[0:QT, 6700 + c * 8:6700 + c * 8 + NQT] for c in range(2)]
    row_sum = [flat2[0:QT, 6720 + c * 8:6720 + c * 8 + NQT] for c in range(2)]
    att = m.s3
    tile3 = lambda a: a.rearrange("p (j n) -> p j n", j=NQT)
    wide = lambda a: a.unsqueeze(2).broadcast_to([QT, NQT, SEQ])
    load(nc, (mask, mask_dram), (head_of, m.dram["head_of"]))
    with stage(nc, "cleared", "q_out_ready", "v_out_ready", "scores_ready", "scores_taken", "shifted", "exp_ready",
               "weights_ready", "turned", "turned_taken", "out_ready", "out_taken", "shift_step",
               "divide_step") as (
            block, cleared, q_out_ready, v_out_ready, scores_ready, scores_taken, shifted, exp_ready, weights_ready,
            turned, turned_taken, out_ready, out_taken, shift_step, divide_step):

        @block.gpsimd
        def _(pool):
            for c in range(2):
                nc.gpsimd.memset(q_out[c], 0.0)
                nc.gpsimd.memset(v_out[c], 0.0).then_inc(cleared, 1)
            pool.wait_ge(cleared, 2)

            def set_out(b, c, peeled=False):
                if not peeled:
                    pool.wait_ge(scores_ready, b * 2 + (c - 1))
                nc.gpsimd.tensor_tensor(
                    q_out[c][:, 0:HPC * SEQ].rearrange("p (h t) -> p h t", h=HPC),
                    q[:, c:c + 1, bass.ds(b * SEQ, SEQ)].broadcast_to([P, HPC, SEQ]),
                    head_of.unsqueeze(2).broadcast_to([P, HPC, SEQ]), ALU.mult).then_inc(q_out_ready, 1)
                if not peeled:
                    pool.wait_ge(out_ready, b * 2 + (c - 1))
                blocks = v_out[c][:, :].rearrange("p (h n) -> p h n", h=HPC)
                for h in range(HPC):
                    ins = nc.gpsimd.tensor_copy(blocks[:, h, h * HD:(h + 1) * HD],
                                                v[:, bass.ds(b, 1), c * P + h * HD:c * P + (h + 1) * HD].squeeze(1))
                ins.then_inc(v_out_ready, 1)

            for c in range(2):
                set_out(0, c, True)
            with pool.Fori(1, BATCH) as b:
                for c in range(2):
                    set_out(b, c)

        @block.tensor
        def _(pe):
            def scores(b, c, peeled=False):
                pe.wait_ge(q_out_ready, b * 2 + (c + 1))
                if not peeled:
                    pe.wait_ge(scores_taken, b * 2 + (c - 1))
                for j in range(NQT):
                    ins = nc.tensor.matmul(m.ps[0:QT, c * BANK + j * SEQ:c * BANK + (j + 1) * SEQ],
                                           q_out[c][:, j * QT:(j + 1) * QT],
                                           k[:, c, bass.ds(b * SEQ, SEQ)], start=True, stop=True)
                ins.then_inc(scores_ready, 1)

            def weigh(b, c, peeled=False):
                pe.wait_ge(weights_ready, b * 2 + (c + 1))
                if not peeled:
                    pe.wait_ge(turned_taken, b * 2 + (c - 1))
                at = (2 + 2 * c) * BANK
                for j in range(NQT):
                    to = at + (j * QT if j < 4 else BANK)
                    ins = nc.tensor.transpose(m.ps[0:SEQ, to:to + QT], score[c][:, j * SEQ:(j + 1) * SEQ],
                                              m.ident[0:QT, 0:QT])
                ins.then_inc(turned, 1)
                pe.wait_ge(turned_taken, b * 2 + (c + 1))
                pe.wait_ge(v_out_ready, b * 2 + (c + 1))
                if not peeled:
                    pe.wait_ge(out_taken, b * 2 + (c - 1))
                for h in range(HPC):
                    ins = nc.tensor.matmul(m.bank(6 + c, SEQ), v_out[c][:, h * P:(h + 1) * P],
                                           turned_sb[c][:, h * SEQ:(h + 1) * SEQ], start=h == 0, stop=h == HPC - 1)
                ins.then_inc(out_ready, 1)

            scores(0, 0, True)
            scores(0, 1, True)
            weigh(0, 0, True)
            scores(1, 0)
            weigh(0, 1, True)
            with pe.Fori(1, BATCH - 1) as b:
                scores(b, 1)
                weigh(b, 0)
                scores(b + 1, 0)
                weigh(b, 1)
            scores(BATCH - 1, 1)
            weigh(BATCH - 1, 0)
            weigh(BATCH - 1, 1)

        @block.scalar
        def _(act):
            def exp(b, c):
                act.wait_ge(shifted, b * 2 + (c + 1))
                nc.scalar.activation(score[c], score[c], ACT.Exp).then_inc(exp_ready, 1)

            def take(b, c, peeled=False):
                act.wait_ge(turned, b * 2 + (c + 1))
                at = (2 + 2 * c) * BANK
                if not peeled:
                    act.wait_ge(out_ready, b * 2 + (c - 1))
                nc.scalar.copy(turned_sb[c][:, 0:4 * QT], m.ps[0:SEQ, at:at + 4 * QT])
                nc.scalar.copy(turned_sb[c][:, 4 * QT:QPAD], m.ps[0:SEQ, at + BANK:at + BANK + QT]).then_inc(
                    turned_taken, 1)
                act.wait_ge(out_ready, b * 2 + (c + 1))
                nc.scalar.activation(att[:, c, bass.ds(b * SEQ, SEQ)], m.bank(6 + c, SEQ), ACT.Identity,
                                     bias=v_bias(c)).then_inc(out_taken, 1)

            exp(0, 0)
            exp(0, 1)
            take(0, 0, True)
            exp(1, 0)
            take(0, 1, True)
            with act.Fori(1, BATCH - 1) as b:
                exp(b, 1)
                take(b, 0)
                exp(b + 1, 0)
                take(b, 1)
            exp(BATCH - 1, 1)
            take(BATCH - 1, 0)
            take(BATCH - 1, 1)

        @block.vector
        def _(dve):
            shift_steps = 1
            divide_steps = 3 if topk else 2

            def shift(b, c, peeled=False):
                link = linker(dve, shift_step, b * (2 * shift_steps) + c * shift_steps)
                dve.wait_ge(scores_ready, b * 2 + (c + 1))
                if not peeled:
                    dve.wait_ge(turned, b * 2 + (c - 1))
                s = tile3(score[c])
                nc.vector.tensor_tensor(score[c], m.ps[0:QT, c * BANK:c * BANK + NQT * SEQ], mask,
                                        ALU.add).then_inc(scores_taken, 1)
                dve.wait_ge(scores_taken, b * 2 + (c + 1))
                if topk:
                    nc.vector.tensor_copy(left[c], score[c])
                    nc.vector.drain()
                    for r in range(TOPK // 8):
                        for j in range(NQT):
                            nc.vector.max(top8[c][:, j, r, :], left[c][:, j * SEQ:(j + 1) * SEQ])
                        nc.vector.drain()
                        for j in range(NQT):
                            part = left[c][:, j * SEQ:(j + 1) * SEQ]
                            nc.vector.match_replace(part, top8[c][:, j, r, :], part, TAKEN)
                        nc.vector.drain()
                    link(nc.vector.tensor_scalar(left[c], left[c], -1e35, None, ALU.is_lt))
                    high = top8[c][:, :, 0, 0]
                else:
                    high = row_max[c]
                    link(nc.vector.tensor_reduce(high, s, AX_X, ALU.max))
                nc.vector.tensor_tensor(s, s, wide(high), ALU.subtract).then_inc(shifted, 1)

            def divide(b, c):
                link = linker(dve, divide_step, b * (2 * divide_steps) + c * divide_steps)
                dve.wait_ge(exp_ready, b * 2 + (c + 1))
                s = tile3(score[c])
                if topk:
                    link(nc.vector.tensor_tensor(score[c], score[c], left[c], ALU.mult))
                link(nc.vector.tensor_reduce(row_sum[c], s, AX_X, ALU.add))
                link(nc.vector.reciprocal(row_sum[c], row_sum[c]))
                nc.vector.tensor_tensor(s, s, wide(row_sum[c]), ALU.mult).then_inc(weights_ready, 1)

            shift(0, 0, True)
            shift(0, 1, True)
            divide(0, 0)
            shift(1, 0)
            divide(0, 1)
            with dve.Fori(1, BATCH - 1) as b:
                shift(b, 1)
                divide(b, 0)
                shift(b + 1, 0)
                divide(b, 1)
            shift(BATCH - 1, 1)
            divide(BATCH - 1, 0)
            divide(BATCH - 1, 1)


def project(nc, m, w_out, bias):
    linear(nc, m, full(m.s3), lambda k, j: w_out[:, k, j * P:j * P + P], KD, KD, CHUNKS, add_to(nc, m, m.h, bias),
           on="vector")


def queries_and_keys(nc, m, w_q, w_k, b_q, b_k, scale):
    def drain(j, o, n, acc, link):
        out = m.big1[:, j, o:o + n]
        if j < KD:
            return nc.vector.tensor_scalar(out, acc, b_q(j), scale, ALU.add, ALU.mult)
        return nc.vector.tensor_scalar(out, acc, b_k(j - KD), None, ALU.add)
    linear(nc, m, full(m.xn), lambda k, j: w_q(k, j) if j < KD else w_k(k, j - KD), KD, 2 * KD, CHUNKS, drain,
           on="vector")


def attention1(nc, m, d):
    w = m.wa[:, 0:KD * 3 * D].rearrange("p (k n) -> p k n", k=KD)
    w_o = m.wa[:, 1536:2048].rearrange("p (k n) -> p k n", k=KD)
    load(nc, (w, d["c_attn"]), (w_o, d["c_proj"]))
    layernorm(nc, m, full(m.h), full(m.xn), CHUNKS)
    queries_and_keys(nc, m, lambda k, j: w[:, k, j * P:j * P + P], lambda k, j: w[:, k, D + j * P:D + j * P + P],
                     lambda j: m.v("c_attn_b", j), lambda j: m.v("c_attn_b", 2 + j), HD ** -0.5)
    v = m.big1[:, :, :].rearrange("p a b -> p (a b)")[0:SEQ, 4 * N:4 * N + BATCH * D].rearrange(
        "p (b n) -> p b n", b=BATCH)
    value_rows(nc, m, lambda k: w[:, k, 2 * D:3 * D], v)
    attend(nc, m, d["mask1"], lambda c: m.v("c_attn_b", 4 + c), False)
    project(nc, m, w_o, lambda j: m.v("c_proj_b", j))


def load_qkvo(nc, m, d, of):
    w = [m.wa[:, i * 512:(i + 1) * 512].rearrange("p (k n) -> p k n", k=KD) for i in range(4)]
    load(nc, *[(w[i], d[of + name]) for i, name in enumerate(("Wq", "Wk", "Wv", "Wo"))])
    return w


def attention3(nc, m, d):
    w_q, w_k, w_v, w_o = load_qkvo(nc, m, d, "L3")
    layernorm(nc, m, full(m.h), full(m.xn), CHUNKS)
    queries_and_keys(nc, m, lambda k, j: w_q[:, k, j * P:j * P + P], lambda k, j: w_k[:, k, j * P:j * P + P],
                     lambda j: m.v("bq", j), lambda j: m.v("bk", j), HD ** -0.5)
    v = m.big1[:, :, :].rearrange("p a b -> p (a b)")[0:SEQ, 4 * N:4 * N + BATCH * D].rearrange(
        "p (b n) -> p b n", b=BATCH)
    value_rows(nc, m, lambda k: w_v[:, k, :], v)
    attend(nc, m, d["mask3"], lambda c: m.v("bv", c), True)
    project(nc, m, w_o, lambda j: m.v("bo", j))


def attention2(nc, m, d):
    w_q, w_k, w_v, w_o = load_qkvo(nc, m, d, "L2")
    layernorm(nc, m, full(m.h), full(m.xn), CHUNKS)
    queries_and_keys(nc, m, lambda k, j: w_q[:, k, j * P:j * P + P], lambda k, j: w_k[:, k, j * P:j * P + P],
                     lambda j: m.v("Wq_b", j), lambda j: m.v("Wk_b", j), D ** -0.5)
    flat1 = m.big1[:, :, :].rearrange("p a b -> p (a b)")
    v = flat1[0:SEQ, 4 * N:4 * N + BATCH * D].rearrange("p (b n) -> p b n", b=BATCH)
    value_rows(nc, m, lambda k: w_v[:, k, :], v)
    q, k = m.big1[:, 0:2, :], m.big1[:, 2:4, :]
    flat2 = m.big2[:, :, :].rearrange("p a b -> p (a b)")
    G = 4
    W = G * SEQ
    score = [flat2[0:SEQ, g * W:(g + 1) * W] for g in range(BATCH // G)]
    turned_sb = [flat2[0:SEQ, 1200 + g * W:1200 + (g + 1) * W] for g in range(BATCH // G)]
    mask = flat2[0:SEQ, 2400:2400 + SEQ]
    red = [flat2[0:SEQ, 2500 + 8 * g:2500 + 8 * g + G] for g in range(BATCH // G)]
    att = m.s3
    load(nc, (mask, d["mask2"]))
    with stage(nc, "scores_ready", "abs_ready", "step", "shifted", "exp_ready", "weights_ready", "turned",
               "turned_taken", "out_ready", "out_taken") as (
            block, scores_ready, abs_ready, step, shifted, exp_ready, weights_ready, turned, turned_taken, out_ready, out_taken):
        wide = lambda a: a.unsqueeze(2).broadcast_to([SEQ, G, SEQ])
        tiles = range(BATCH // G)

        @block.tensor
        def _(pe):
            for g in tiles:
                for i in range(G):
                    o = (g * G + i) * SEQ
                    for c in range(KD):
                        ins = nc.tensor.matmul(m.ps[0:SEQ, g * BANK + i * SEQ:g * BANK + (i + 1) * SEQ],
                                               q[:, c, o:o + SEQ], k[:, c, o:o + SEQ], start=c == 0, stop=c == KD - 1)
                ins.then_inc(scores_ready, 1)
            for g in tiles:
                pe.wait_ge(weights_ready, g + 1)
                if g >= 2:
                    pe.wait_ge(turned_taken, g - 1)
                b4 = 4 + g % 2
                for i in range(G):
                    ins = nc.tensor.transpose(m.ps[0:SEQ, b4 * BANK + i * SEQ:b4 * BANK + (i + 1) * SEQ],
                                              score[g][:, i * SEQ:(i + 1) * SEQ], m.ident[0:SEQ, 0:SEQ])
                ins.then_inc(turned, 1)
                pe.wait_ge(turned_taken, g + 1)
                if g >= 1:
                    pe.wait_ge(out_taken, 2 * g)
                for c in range(KD):
                    for i in range(G):
                        ins = nc.tensor.matmul(m.ps[:, (6 + c) * BANK + i * SEQ:(6 + c) * BANK + (i + 1) * SEQ],
                                               v[:, g * G + i, c * P:(c + 1) * P],
                                               turned_sb[g][:, i * SEQ:(i + 1) * SEQ], start=True, stop=True)
                    ins.then_inc(out_ready, 1)

        @block.scalar
        def _(act):
            for g in tiles:
                act.wait_ge(scores_ready, g + 1)
                nc.scalar.activation(score[g], m.bank(g, W, SEQ), ACT.Abs).then_inc(abs_ready, 1)
            for g in tiles:
                act.wait_ge(shifted, g + 1)
                nc.scalar.activation(score[g], score[g], ACT.Exp).then_inc(exp_ready, 1)
            for g in tiles:
                act.wait_ge(turned, g + 1)
                nc.scalar.copy(turned_sb[g], m.bank(4 + g % 2, W, SEQ)).then_inc(turned_taken, 1)
                for c in range(KD):
                    act.wait_ge(out_ready, 2 * g + c + 1)
                    nc.scalar.activation(att[:, c, g * W:(g + 1) * W], m.bank(6 + c, W), ACT.Identity,
                                         bias=m.v("Wv_b", c)).then_inc(out_taken, 1)

        @block.vector
        def _(dve):
            link = linker(dve, step)
            for g in tiles:
                dve.wait_ge(abs_ready, g + 1)
                s = score[g].rearrange("p (i n) -> p i n", i=G)
                link(nc.vector.tensor_tensor(s, s, mask.unsqueeze(1).broadcast_to([SEQ, G, SEQ]), ALU.add))
                link(nc.vector.tensor_reduce(red[g], s, AX_X, ALU.max))
                nc.vector.tensor_tensor(s, s, wide(red[g]), ALU.subtract).then_inc(shifted, 1)
            for g in tiles:
                dve.wait_ge(exp_ready, g + 1)
                s = score[g].rearrange("p (i n) -> p i n", i=G)
                link(nc.vector.tensor_reduce(red[g], s, AX_X, ALU.add))
                link(nc.vector.reciprocal(red[g], red[g]))
                nc.vector.tensor_tensor(s, s, wide(red[g]), ALU.mult).then_inc(weights_ready, 1)
    project(nc, m, w_o, lambda j: m.v("Wo_b", j))


MAGIC = 1.5 * 2.0 ** 23


def ternary(nc, m, w, tmp, scale, width):
    tiles = w.shape[1]
    wide = lambda a: a.unsqueeze(2).broadcast_to([P, tiles, width])
    inv = scale[:, tiles:2 * tiles]
    sc = scale[:, 0:tiles]
    with stage(nc, "step") as (block, step):
        @block.vector
        def _(dve):
            link = linker(dve, step)
            link(nc.vector.tensor_reduce(sc, w, AX_X, ALU.add, apply_absolute_value=True))
            link(nc.vector.tensor_scalar(sc, sc, 1.0 / width, 1e-5, ALU.mult, ALU.max))
            link(nc.vector.reciprocal(inv, sc))
            link(nc.vector.tensor_tensor(tmp, w, wide(inv), ALU.mult))
            link(nc.vector.tensor_scalar(tmp, tmp, MAGIC, -MAGIC, ALU.add, ALU.add))
            link(nc.vector.tensor_scalar(tmp, tmp, -1.0, 1.0, ALU.max, ALU.min))
            link(nc.vector.tensor_tensor(tmp, tmp, w, ALU.subtract))
            link(nc.vector.tensor_tensor(tmp, w, tmp, ALU.add))
            link(nc.vector.tensor_tensor(tmp, tmp, wide(sc), ALU.mult))


def mlp(nc, m, x, w1, w2, activate, add):
    linear(nc, m, full(x), lambda k, j: w1[:, k, j * P:j * P + P], KD, 8, CHUNKS, activate)
    linear(nc, m, full(m.big2), lambda k, j: w2[:, k, j * P:j * P + P], 8, KD, CHUNKS, add, on="vector")


def ternary_mlp(nc, m, d):
    flat1 = m.big1[:, :, :].rearrange("p a b -> p (a b)")
    fc = flat1[:, 0:2048].rearrange("p (k n) -> p k n", k=8)
    proj = flat1[:, 2048:4096].rearrange("p (k n) -> p k n", k=2)
    tmp_fc = flat1[:, 4096:6144].rearrange("p (k n) -> p k n", k=8)
    tmp_proj = flat1[:, 6144:8192].rearrange("p (k n) -> p k n", k=2)
    fast_b, u, v = flat1[0:16, 8192:8208], m.s1[0:16, 0, 0:FF], flat1[0:16, 8208:8464]
    mid = m.s1[0:16, 1, 0:FF]
    scale_fc, scale_proj = flat1[:, 8500:8516], flat1[:, 8520:8524]
    w1 = m.wa[:, 0:2048].rearrange("p (k n) -> p k n", k=KD)
    w2 = m.wa[:, 2048:4096].rearrange("p (k n) -> p k n", k=8)
    load(nc, (fc, d["w_fc"]), (proj, d["w_proj"]), (fast_b, d["fast_b"]), (u, d["uT"]), (v, d["v"]))
    ternary(nc, m, fc, tmp_fc, scale_fc, D)
    ternary(nc, m, proj, tmp_proj, scale_proj, FF)
    with stage(nc, "mid_ready", "mid_taken", "turned", "turned_taken") as (
            block, mid_ready, mid_taken, turned, turned_taken):

        @block.tensor
        def _(pe):
            for c in range(2):
                nc.tensor.matmul(m.bank(c, BANK, 16), fast_b, u[:, c * BANK:(c + 1) * BANK], start=True,
                                 stop=True).then_inc(mid_ready, 1)
            pe.wait_ge(mid_taken, 2)
            for k in range(KD):
                for c in range(2):
                    b = 2 + 2 * k + c
                    for i in range(4):
                        j = 4 * c + i
                        to = m.ps[:, b * BANK + i * P:b * BANK + (i + 1) * P]
                        nc.tensor.matmul(to, tmp_fc[:, j, k * P:(k + 1) * P], m.ident[:, :], start=True, stop=False)
                        ins = nc.tensor.matmul(to, v[:, k * P:(k + 1) * P], mid[:, j * P:(j + 1) * P], start=False,
                                               stop=True)
                    ins.then_inc(turned, 1)
            for g in range(4):
                b = 2 + g
                pe.wait_ge(turned_taken, g + 1)
                for i in range(2):
                    for j in range(2):
                        k = 2 * g + i
                        to = m.ps[:, b * BANK + (2 * i + j) * P:b * BANK + (2 * i + j + 1) * P]
                        ins = nc.tensor.transpose(to, tmp_proj[:, j, k * P:(k + 1) * P], m.ident[:, :])
                ins.then_inc(turned, 1)

        @block.vector
        def _(dve):
            for c in range(2):
                dve.wait_ge(mid_ready, c + 1)
                nc.vector.tensor_scalar(mid[:, c * BANK:(c + 1) * BANK], m.bank(c, BANK, 16),
                                        m.vec[0:16, VEC["gate"][0]:VEC["gate"][0] + 1], None,
                                        ALU.mult).then_inc(mid_taken, 1)
            for g in range(4):
                dve.wait_ge(turned, g + 1)
                k, c = divmod(g, 2)
                nc.vector.tensor_copy(w1[:, k, c * BANK:(c + 1) * BANK], m.bank(2 + g)).then_inc(turned_taken, 1)
            for g in range(4):
                dve.wait_ge(turned, 5 + g)
                nc.vector.tensor_copy(w2[:, 2 * g:2 * g + 2, :].rearrange("p k n -> p (k n)"), m.bank(2 + g))
    layernorm(nc, m, full(m.h), full(m.xn), CHUNKS)

    def relu_squared(j, o, n, acc, link):
        out = m.big2[:, j, o:o + n]
        link(nc.scalar.activation(out, acc, ACT.Relu))
        return nc.scalar.activation(out, out, ACT.Square)
    mlp(nc, m, m.xn, w1, w2, relu_squared, add_to(nc, m, m.h))


def dequantised_mlp(nc, m, d):
    flat1 = m.big1[:, :, :].rearrange("p a b -> p (a b)")
    raw = [flat1[:, i * 2048:(i + 1) * 2048] for i in range(4)]
    w1, w2 = m.wa[:, 0:2048], m.wa[:, 2048:4096]
    load(nc, (raw[0].bitcast(I32), d["fc1_q"]), (raw[1].bitcast(I32), d["fc2_q"]),
         (raw[2].rearrange("p (k n) -> p k n", k=KD), d["fc1_s"].unsqueeze(0).broadcast_to([P, KD, FF])),
         (raw[3].rearrange("p (k n) -> p k n", k=8), d["fc2_s"].unsqueeze(0).broadcast_to([P, 8, D])))
    with stage(nc, "half_bias") as (block, half_bias):
        @block.vector
        def _(dve):
            for w, q, s in ((w1, raw[0], raw[2]), (w2, raw[1], raw[3])):
                nc.vector.scalar_tensor_tensor(out=w, in0=q.bitcast(I32), scalar=-128.0, in1=s, op0=ALU.add,
                                               op1=ALU.mult)
    w1 = w1.rearrange("p (k n) -> p k n", k=KD)
    w2 = w2.rearrange("p (k n) -> p k n", k=8)
    layernorm(nc, m, full(m.h), full(m.xn), CHUNKS)
    layernorm(nc, m, full(m.xn), full(m.s3), CHUNKS, lambda k: m.v("gamma", k), lambda k: m.v("beta", k))

    def half(j, o, n, acc, link):
        out, t = m.h[:, j, o:o + n], m.s1[:, j, o:o + n]
        link(nc.vector.tensor_tensor(out, out, m.xn[:, j, o:o + n], ALU.add))
        link(nc.vector.tensor_scalar(t, acc, m.v("fc2_b", j), 0.5, ALU.add, ALU.mult))
        return nc.vector.tensor_tensor(out, out, t, ALU.add)
    mlp(nc, m, m.s3, w1, w2, lambda j, o, n, acc, link: nc.scalar.activation(
        m.big2[:, j, o:o + n], acc, ACT.Silu, bias=m.v("fc1_b", j)), half)


def mixture3(nc, m, d):
    w3 = m.small[:, 1200:1216].rearrange("p (k n) -> p k n", k=KD)
    w1 = m.wa[:, 0:4096].rearrange("p (k n) -> p k n", k=KD)
    w2 = m.wa[:, 4096:8192].rearrange("p (k n) -> p k n", k=16)
    load(nc, (w3, d["router3"]), (w1, d["mw1"]), (w2, d["mw2"]))
    layernorm(nc, m, full(m.h), full(m.xn), CHUNKS)
    route(nc, m, 1, E3, w3, True)
    flat1 = m.big1[:, :, :].rearrange("p a b -> p (a b)")
    nf = 16
    units = [(c, f) for c in range(NCH) for f in range(nf)]
    squared = [flat1[:, i * CW:(i + 1) * CW] for i in range(2)]
    hidden = [flat1[:, (2 + i) * CW:(3 + i) * CW] for i in range(2)]
    with stage(nc, "up_ready", "spread", "relu_ready", "square_ready", "hidden_ready", "down_ready", "sum_taken") as (
            block, up_ready, spread, relu_ready, square_ready, hidden_ready, down_ready, sum_taken):

        @block.tensor
        def _(pe):
            def up(u):
                c, f = units[u]
                o = c * CW
                if u >= 2:
                    pe.wait_ge(hidden_ready, u - 1)
                if f % 2 == 0:
                    nc.tensor.matmul(m.bank(2 + (f // 2) % 2, CW), m.pick[:, (f // 2) * P:(f // 2 + 1) * P],
                                     m.parts[:, 0, o:o + CW], start=True, stop=True).then_inc(spread, 1)
                for k in range(KD):
                    ins = nc.tensor.matmul(m.bank(u % 2, CW), w1[:, k, f * P:(f + 1) * P], m.xn[:, k, o:o + CW],
                                           start=k == 0, stop=k == KD - 1)
                ins.then_inc(up_ready, 1)

            up(0)
            for u, (c, f) in enumerate(units):
                if u + 1 < len(units):
                    up(u + 1)
                pe.wait_ge(hidden_ready, u + 1)
                if f == 0 and c >= 2:
                    pe.wait_ge(sum_taken, KD * (c - 1))
                for j in range(KD):
                    ins = nc.tensor.matmul(m.bank(4 + 2 * (c % 2) + j, CW), w2[:, f, j * P:(j + 1) * P],
                                           hidden[u % 2], start=f == 0, stop=f == nf - 1)
                if f == nf - 1:
                    ins.then_inc(down_ready, 1)

        @block.scalar
        def _(act):
            for u in range(len(units)):
                act.wait_ge(up_ready, u + 1)
                if u >= 2:
                    act.wait_ge(hidden_ready, u - 1)
                nc.scalar.activation(squared[u % 2], m.bank(u % 2, CW), ACT.Relu).then_inc(relu_ready, 1)
                act.wait_ge(relu_ready, u + 1)
                nc.scalar.activation(squared[u % 2], squared[u % 2], ACT.Square).then_inc(square_ready, 1)

        @block.vector
        def _(dve):
            for u, (c, f) in enumerate(units):
                dve.wait_ge(square_ready, u + 1)
                dve.wait_ge(spread, u // 2 + 1)
                nc.vector.tensor_tensor(hidden[u % 2], squared[u % 2], m.bank(2 + (f // 2) % 2, CW),
                                        ALU.mult).then_inc(hidden_ready, 1)
                if f == nf - 1:
                    dve.wait_ge(down_ready, c + 1)
                    for j in range(KD):
                        out = m.h[:, j, c * CW:(c + 1) * CW]
                        nc.vector.tensor_tensor(out, out, m.bank(4 + 2 * (c % 2) + j, CW),
                                                ALU.add).then_inc(sum_taken, 1)


def cols(a, n):
    return np.ascontiguousarray(np.reshape(a, (n, P)).T)


def rows_to_partitions(w):
    k = w.shape[-2] // P
    return np.ascontiguousarray(np.moveaxis(w.reshape(w.shape[:-2] + (k, P, w.shape[-1])), -3, -2)).reshape(
        w.shape[:-2] + (P, -1))


def lay_out(i):
    f = np.float32
    t = lambda name: np.asarray(i[name])
    d = {}
    x = t("x").reshape(BATCH, 3, 6, 16, 6, 16).transpose(1, 3, 5, 0, 2, 4).reshape(768, BATCH * PATCHES)
    d["patches"] = rows_to_partitions(x)
    d["tok_w"] = rows_to_partitions(t("L0_tok_W").T)
    d["tok_pos"] = rows_to_partitions(t("L0_tok_pos_embedding")[0].T)
    d["tokens"] = np.ascontiguousarray(t("x_txt").reshape(4, P).T)
    d["emb"] = t("L0_txt_emb")
    d["txt_pos"] = rows_to_partitions(t("L0_txt_pos_emb")[:TEXT].T)
    fresh = np.ones((STATE, BATCH, TEXT), f)
    fresh[:, :, 0] = 0
    d["fresh"] = fresh.reshape(STATE, -1)
    d["B"] = rows_to_partitions(t("L0_txt_B"))
    d["C"] = t("L0_txt_C")
    d["Dw"] = rows_to_partitions(t("L0_txt_D"))
    d["w1"] = rows_to_partitions(t("L0_txt_w1"))
    d["w2"] = rows_to_partitions(t("L0_txt_w2"))
    lvec = np.zeros((LAYERS, P, NLVEC), f)
    for l in range(LAYERS):
        for name in ("ln1_s", "ln1_b", "ln2_s", "ln2_b", "b2"):
            lvec[l][:, LVEC[name]:LVEC[name] + 2] = cols(t("L0_txt_" + name)[l], 2)
        lvec[l][:, LVEC["b1"]:LVEC["b1"] + 8] = cols(t("L0_txt_b1")[l], 8)
        lvec[l][:STATE, LVEC["A"]] = t("L0_txt_A_diag")[l]
    d["lvec"] = lvec
    vec = np.zeros((P, NVEC), f)

    def put(name, a):
        c, n = VEC[name]
        vec[:, c:c + n] = a

    names = {
        "tok_b": "L0_tok_b", "cls": "L0_tok_cls_token", "lnf_s": "L0_txt_lnf_s", "lnf_b": "L0_txt_lnf_b",
        "norm_w": "L0_attn_norm_w", "norm_b": "L0_attn_norm_b", "conv_b": "L0_attn_conv_b", "dt_w": "L0_attn_dt_w",
        "dt_b": "L0_attn_dt_b", "D_skip": "L0_attn_D_skip", "c_attn_b": "L1_attn_c_attn_b",
        "c_proj_b": "L1_attn_c_proj_b", "Wq_b": "L2_attn_Wq_b", "Wk_b": "L2_attn_Wk_b", "Wv_b": "L2_attn_Wv_b",
        "Wo_b": "L2_attn_Wo_b", "gamma": "L2_ffn_ln_gamma", "beta": "L2_ffn_ln_beta", "fc1_b": "L2_ffn_fc1_bias",
        "fc2_b": "L2_ffn_fc2_bias", "bq": "L3_attn_bq", "bk": "L3_attn_bk", "bv": "L3_attn_bv", "bo": "L3_attn_bo"}
    for short, name in names.items():
        put(short, cols(t(name), VEC[short][1]))
    put("gate", np.broadcast_to(t("L1_ffn_gate"), (P, 1)))
    put("conv_w", t("L0_attn_conv_w").reshape(4, P, 4).transpose(1, 0, 2).reshape(P, 16))
    put("A_log", t("L0_attn_A_log").reshape(4, P, DS).transpose(1, 0, 2).reshape(P, 4 * DS))
    d["vec"] = vec
    d["ident"] = np.eye(P, dtype=f)

    d["in_proj"] = rows_to_partitions(t("L0_attn_in_proj_w").T)
    xp = t("L0_attn_x_proj_w")
    d["dt_rows"] = rows_to_partitions(np.broadcast_to(xp[0:1].T, (DI, P)))
    d["bc_rows"] = rows_to_partitions(np.concatenate([xp[1:].T] * 3 + [np.zeros((DI, 32), f)], axis=1))
    d["out_proj"] = rows_to_partitions(t("L0_attn_out_proj_w").T)
    pick = np.zeros((P, 32, P), np.float32)
    for part in range(3):
        for e in range(32):
            pick[32 * part + e, e, :] = 1
    d["pick"] = pick.reshape(P, -1)

    d["router"] = rows_to_partitions(np.concatenate([t("L0_ffn_router_w0"), t("L0_ffn_router_w1")], axis=1))
    experts = [np.concatenate([rows_to_partitions(t("L0_ffn_wg%d" % g)), rows_to_partitions(t("L0_ffn_wu%d" % g)),
                               t("L0_ffn_wd%d" % g)], axis=2) for g in range(2)]
    d["experts"] = np.ascontiguousarray(
        np.stack(experts).reshape(2, 8, 4, P, 768).transpose(1, 0, 3, 2, 4).reshape(8, 2, P, 4 * 768))
    order = np.tile(np.arange(E0, 0, -1, dtype=f), (ROWT, 1))
    d["order"] = order

    d["c_attn"] = rows_to_partitions(t("L1_attn_c_attn_w"))
    d["c_proj"] = rows_to_partitions(t("L1_attn_c_proj_w"))
    for name in ("Wq", "Wk", "Wv", "Wo"):
        d["L2" + name] = rows_to_partitions(t("L2_attn_%s_w" % name).T)
        d["L3" + name] = rows_to_partitions(t("L3_attn_%s" % name).T)
    r = np.minimum(np.arange(QPAD), HPC * SEQ - 1) % SEQ
    key = np.arange(SEQ)
    late = key[None, :] > r[:, None]
    twice = np.zeros(SEQ, f)
    twice[7:64:8] = np.log(2.0)
    d["mask1"] = np.ascontiguousarray((np.where(late, np.float32(-10000.0), np.float32(0)) + twice[None, :]).reshape(
        NQT, QT, SEQ).transpose(1, 0, 2).reshape(QT, -1)).astype(f)
    d["mask3"] = np.ascontiguousarray(np.where(late, NEG, 0.0).astype(f).reshape(NQT, QT, SEQ).transpose(
        1, 0, 2).reshape(QT, -1))
    d["mask2"] = np.where(key[None, :] > key[:, None], NEG, 0.0).astype(f)
    d["head_of"] = np.repeat(np.eye(HPC, dtype=f), HD, axis=0)

    d["w_fc"] = rows_to_partitions(t("L1_ffn_w_fc"))
    d["w_proj"] = rows_to_partitions(t("L1_ffn_w_proj"))
    d["fast_b"] = t("L1_ffn_fast_b")
    d["uT"] = np.ascontiguousarray(t("L1_ffn_u").T)
    d["v"] = t("L1_ffn_v")
    d["fc1_q"] = rows_to_partitions(t("L2_ffn_fc1_q"))
    d["fc2_q"] = rows_to_partitions(t("L2_ffn_fc2_q"))
    d["fc1_s"] = t("L2_ffn_fc1_scales")
    d["fc2_s"] = t("L2_ffn_fc2_scales")
    d["router3"] = rows_to_partitions(t("L3_ffn_router_w").T)
    d["mw1"] = rows_to_partitions(t("L3_ffn_w1"))
    d["mw2"] = rows_to_partitions(t("L3_ffn_w2"))
    return d


def store(nc, m, out):
    with stage(nc, "stored") as (block, stored):

        @block.sync
        def _(sp):
            sp.dma_start(out, m.h[:, :, :].rearrange("p k n -> p (k n)")).then_inc(stored, 16)
            sp.wait_ge(stored, 16)


STAGES = ["patch_tokens", "text_encoder", "selective_scan", "mixture0", "attention1", "ternary_mlp", "attention2",
          "dequantised_mlp", "attention3", "mixture3"]


def build(nc, d, out):
    m = Mem(nc, d)
    setup(nc, m, d)
    patch_tokens(nc, m, d)
    text_encoder(nc, m, d)
    selective_scan(nc, m, d)
    mixture0(nc, m, d)
    attention1(nc, m, d)
    ternary_mlp(nc, m, d)
    attention2(nc, m, d)
    dequantised_mlp(nc, m, d)
    attention3(nc, m, d)
    mixture3(nc, m, d)
    store(nc, m, out)


def kernel(**inputs):
    import concourse.bacc as bacc
    from concourse.bass_utils import run_bass_kernel_spmd

    arrays = lay_out(inputs)
    nc = bacc.Bacc("TRN2", target_bir_lowering=False, num_devices=1)
    d = {name: nc.dram_tensor("in_" + name, a.shape, mybir.dt.from_np(a.dtype), kind="ExternalInput").ap()
         for name, a in arrays.items()}
    out = nc.dram_tensor("out", (P, KD * N), F32, kind="ExternalOutput").ap()
    build(nc, d, out)
    r = run_bass_kernel_spmd(nc, [{"in_" + k: a for k, a in arrays.items()}], core_ids=[0])
    got = np.asarray(r.results[0]["out"]).reshape(P, KD, BATCH, SEQ)
    return np.ascontiguousarray(got.transpose(2, 3, 1, 0)).reshape(BATCH, SEQ, D)
```

```python
from contextlib import ExitStack, contextmanager

import numpy as np

import concourse.bass as bass
from concourse import mybir

ALU = mybir.AluOpType
ACT = mybir.ActivationFunctionType
F32 = mybir.dt.float32
BF16 = mybir.dt.bfloat16
I32 = mybir.dt.int32
AX_X = mybir.AxisListType.X

P = 128
D = 256
KD = D // P
BATCH = 16
PATCHES = 36
TEXT = 32
SEQ = 1 + PATCHES + TEXT
N = BATCH * SEQ
NCH = 3
CW = N // NCH
CHUNKS = [(c * CW, CW) for c in range(NCH)]
BANK = 512
VOCAB = 8000
LAYERS = 4
STATE = 64
FF = 1024
DI = 512
DS = 16
HEADS = 16
HD = D // HEADS
HPC = P // HD
EASY, HARD = 32, SEQ - 32
HARD_HEADS = [(0, 3), (3, 3), (6, 2)]
NHARD = len(HARD_HEADS)
NQT = 2 + NHARD
QAT = [0, P] + [HPC * EASY + h * HARD for h, _ in HARD_HEADS]
QSET = QAT[-1] + P
EPS = 1e-5
NEG = -1e30
TAKEN = -3e38
GATHER_SEM = 109
SEMS = 24
SEM0 = 110
TOPK = 32
ROWT = 92
NROWT = N // ROWT
MAX_BLOCKS = 98
MAX_ROUNDS = 25
TABLE = 4 * (MAX_ROUNDS + 1)
E0, E3 = 32, 8

ROUTE_AT = {"tri": (0, ROWT, ROWT), "ones": (96, P, P), "iota": (224, P, ROWT), "token": (352, NROWT, ROWT),
            "place": (364, 1, P)}
ROUTE_CONSTS = 365
VEC = {}
for _name, _n in (
    ("tok_b", 2), ("cls", 2), ("lnf_s", 2), ("lnf_b", 2), ("norm_w", 2), ("norm_b", 2), ("conv_b", 4),
    ("dt_w", 4), ("dt_b", 4), ("D_skip", 4), ("conv_w", 16), ("A_log", 64), ("c_attn_b", 6), ("c_proj_b", 2),
    ("gate", 1), ("Wq_b", 2), ("Wk_b", 2), ("Wv_b", 2), ("Wo_b", 2), ("gamma", 2), ("beta", 2), ("fc1_b", 8),
    ("fc2_b", 2), ("bq", 2), ("bk", 2), ("bv", 2), ("bo", 2),
):
    VEC[_name] = (sum(n for _, n in VEC.values()), _n)
NVEC = sum(n for _, n in VEC.values())
LVEC = {"ln1_s": 0, "ln1_b": 2, "ln2_s": 4, "ln2_b": 6, "b1": 8, "b2": 16, "A": 18}
NLVEC = 19


class Turn:
    now = 0


@contextmanager
def stage(nc, *names):
    base, other = SEM0 + SEMS * Turn.now, SEM0 + SEMS * (1 - Turn.now)
    Turn.now = 1 - Turn.now
    with ExitStack() as held:
        sems = [held.enter_context(nc.semaphore(name=n, num=base + i)) for i, n in enumerate(names)]
        with nc.Block() as block:
            nc.gpsimd.sem_clear(range(other, other + SEMS))
            yield (block, *sems)


def linker(eng, sem, start=0):
    count = [0]

    def link(ins):
        count[0] += 1
        ins.then_inc(sem, 1)
        eng.wait_ge(sem, start + count[0])

    return link


class Mem:

    def __init__(self, nc, dram):
        self.nc, self.dram = nc, dram
        sb = lambda name, shape, dt=F32: nc.alloc_sbuf_tensor(name, shape, dt)
        self.h = sb("h", [P, KD, N])
        self.xn = sb("xn", [P, KD, N])
        self.s1 = sb("s1", [P, KD, N])
        self.s2 = sb("s2", [P, KD, N])
        self.s3 = sb("s3", [P, KD, N])
        self.big1 = sb("big1", [P, 8, N])
        self.big2 = sb("big2", [P, 8, N])
        self.wa = sb("wa", [P, 8192])
        self.vec = sb("vec", [P, NVEC])
        self.lvec = sb("lvec", [P, NLVEC])
        self.mean_w = sb("mean_w", [P, P])
        self.ones = sb("ones", [P, P])
        self.ident = sb("ident", [P, P])
        self.small = sb("small", [P, 2048])
        self.parts = sb("parts", [P, 2, N], BF16)
        self.pick = sb("pick", [P, 32 * P], BF16)
        self.ident_bf = sb("ident_bf", [P, P], BF16)
        self.order = sb("order", [ROWT, E0])
        self.ps = nc.alloc_psum_tensor("ps", [P, 8 * BANK], F32)

        self.ps_bf = self.ps[:, :].bitcast(BF16)

    def v(self, name, k=0):
        c = VEC[name][0] + k
        return self.vec[:, c:c + 1]

    def bank(self, b, n=BANK, rows=P):
        return self.ps[0:rows, b * BANK:b * BANK + n]


def layernorm(nc, m, src, dst, chunks, gamma=None, beta=None, fold=None, work=None):
    cen, sq = work or (m.s1, m.s2)
    tiles = 4
    width = chunks[0][1] // tiles
    n_ch = len(chunks)
    std = m.small[0:width, 0:tiles * n_ch]
    inv = m.small[0:width, 16:16 + tiles * n_ch]
    diag = [m.small[0:width, 32 + i * width:32 + (i + 1) * width] for i in range(tiles)]
    with stage(nc, "mean_ready", "centred", "squared", "var_ready", "std_ready", "inv_ready", "diag_ready",
               "rstd_ready", "scaled") as (
            block, mean_ready, centred, squared, var_ready, std_ready, inv_ready, diag_ready, rstd_ready, scaled):

        @block.tensor
        def _(pe):
            def mean(c):
                o, n = chunks[c]
                for k in range(KD):
                    ins = nc.tensor.matmul(m.bank(c, n), m.mean_w[:, :], src(k, o, n), start=k == 0, stop=k == KD - 1)
                ins.then_inc(mean_ready, 1)

            def variance(c):
                o, n = chunks[c]
                pe.wait_ge(squared, KD * (c + 1))
                for t in range(tiles):
                    for k in range(KD):
                        ins = nc.tensor.matmul(m.ps[0:width, 6 * BANK + c * tiles + t:][:, 0:1],
                                               sq[:, k, o + t * width:o + (t + 1) * width], m.mean_w[:, 0:1],
                                               start=k == 0, stop=k == KD - 1)
                ins.then_inc(var_ready, 1)

            def spread(c):
                for t in range(tiles):
                    pe.wait_ge(diag_ready, tiles * c + t + 1)
                    ins = nc.tensor.matmul(m.ps[:, (3 + c) * BANK + t * width:(3 + c) * BANK + (t + 1) * width],
                                           m.ones[0:width, :], diag[t], start=True, stop=True)
                    ins.then_inc(rstd_ready, 1)

            for c in range(n_ch):
                mean(c)
            for c in range(n_ch):
                if c:
                    pe.wait_ge(std_ready, c)
                variance(c)
                spread(c)

        @block.scalar
        def _(act):
            for c, (o, n) in enumerate(chunks):
                for k in range(KD):
                    act.wait_ge(centred, KD * c + k + 1)
                    nc.scalar.activation(sq[:, k, o:o + n], cen[:, k, o:o + n], ACT.Square).then_inc(squared, 1)
                act.wait_ge(var_ready, c + 1)
                nc.scalar.activation(std[:, c * tiles:(c + 1) * tiles], m.ps[0:width, 6 * BANK + c * tiles:][:, 0:tiles],
                                     ACT.Sqrt, bias=m.eps[0:width, 0:1]).then_inc(std_ready, 1)

        @block.vector
        def _(dve):
            def centre(c):
                o, n = chunks[c]
                dve.wait_ge(mean_ready, c + 1)
                for k in range(KD):
                    nc.vector.tensor_tensor(cen[:, k, o:o + n], src(k, o, n), m.bank(c, n),
                                            ALU.subtract).then_inc(centred, 1)

            def invert(c):
                dve.wait_ge(std_ready, c + 1)
                at = slice(c * tiles, (c + 1) * tiles)
                nc.vector.reciprocal(inv[:, at], std[:, at]).then_inc(inv_ready, 1)
                dve.wait_ge(inv_ready, c + 1)
                for t in range(tiles):
                    if c:
                        dve.wait_ge(rstd_ready, tiles * (c - 1) + t + 1)
                    nc.vector.tensor_scalar(diag[t], m.ident[0:width, 0:width], inv[:, c * tiles + t:c * tiles + t + 1],
                                            None, ALU.mult).then_inc(diag_ready, 1)

            def scale(c):
                o, n = chunks[c]
                dve.wait_ge(rstd_ready, tiles * (c + 1))
                for k in range(KD):
                    a, r, out = cen[:, k, o:o + n], m.bank(3 + c, n), dst(k, o, n)
                    if gamma is None:
                        nc.vector.tensor_tensor(out, a, r, ALU.mult)
                    else:
                        nc.vector.tensor_tensor(a, a, r, ALU.mult).then_inc(scaled, 1)
                if gamma is not None:
                    dve.wait_ge(scaled, KD * (c + 1))
                    for k in range(KD):
                        a, out = cen[:, k, o:o + n], dst(k, o, n)
                        if fold:
                            a = a.rearrange("p (b t) -> p b t", t=fold)
                        nc.vector.tensor_scalar(out, a, gamma(k), beta(k), ALU.mult, ALU.add)

            for c in range(n_ch):
                centre(c)
            for c in range(n_ch):
                invert(c)
                if c:
                    scale(c - 1)
            scale(n_ch - 1)


def linear(nc, m, src, w, n_in, n_out, chunks, drain, on="scalar", rows=P):
    with stage(nc, "product_ready", "product_taken", "drain_step") as (block, product_ready, product_taken, drain_step):

        @block.tensor
        def _(pe):
            g = 0
            for j in range(n_out):
                for o, n in chunks:
                    if g >= 8:
                        pe.wait_ge(product_taken, g - 7)
                    for k in range(n_in):
                        ins = nc.tensor.matmul(m.bank(g % 8, n, rows), w(k, j), src(k, o, n), start=k == 0,
                                               stop=k == n_in - 1)
                    ins.then_inc(product_ready, 1)
                    g += 1

        def take(eng):
            link = linker(eng, drain_step)
            g = 0
            for j in range(n_out):
                for o, n in chunks:
                    eng.wait_ge(product_ready, g + 1)
                    drain(j, o, n, m.bank(g % 8, n, rows), link).then_inc(product_taken, 1)
                    g += 1

        (block.scalar if on == "scalar" else block.vector)(take)


def add_to(nc, m, dst, bias=None):
    def drain(j, o, n, acc, link):
        out = dst[:, j, o:o + n]
        if bias is None:
            return nc.vector.tensor_tensor(out, out, acc, ALU.add)
        return nc.vector.scalar_tensor_tensor(out=out, in0=acc, scalar=bias(j), in1=out, op0=ALU.add, op1=ALU.add)
    return drain


def load(nc, *pairs):
    with stage(nc, "landed_sp", "landed_act") as (block, landed_sp, landed_act):

        @block.sync
        def _(sp):
            for dst, src in pairs[0::2]:
                sp.dma_start(dst, src).then_inc(landed_sp, 16)
            sp.wait_ge(landed_sp, 16 * len(pairs[0::2]))

        @block.scalar
        def _(act):
            for dst, src in pairs[1::2]:
                act.dma_start(dst, src).then_inc(landed_act, 16)
            if pairs[1::2]:
                act.wait_ge(landed_act, 16 * len(pairs[1::2]))


def full(t):
    return lambda k, o, n: t[:, k, o:o + n]


def setup(nc, m, d):
    rc = nc.alloc_sbuf_tensor("route_consts", [P, ROUTE_CONSTS], F32)
    m.route_consts = {name: rc[0:rows, c:c + n] for name, (c, n, rows) in ROUTE_AT.items()}
    m.pair_idx = nc.alloc_sbuf_tensor("pair_idx", [ROWT, 4 * NROWT], I32)[:, :]
    m.slot_token = nc.alloc_sbuf_tensor("slot_token", [P, TABLE], I32)[:, :]
    m.block_expert = nc.alloc_sbuf_tensor("block_expert", [1, TABLE], I32)[:, :]
    m.rounds = nc.alloc_sbuf_tensor("rounds", [1, 1], I32)[:, :]
    m.block_idx = [nc.alloc_sbuf_tensor("block_idx%d" % i, [P, 1], I32)[:, :] for i in range(4)]
    m.idle = nc.alloc_sbuf_tensor("idle", [P, 1], F32)[:, :]
    m.zeros = nc.alloc_sbuf_tensor("zeros", [P, 4 * D], F32)
    m.x_rows = nc.dram_tensor("x_rows", (N, D), F32).ap()
    m.y_rows = nc.dram_tensor("y_rows", (TABLE * P, D), F32).ap()
    m.y_cleared = nc.alloc_semaphore("y_cleared", num=GATHER_SEM + 58)
    m.gathered = [nc.alloc_semaphore("gathered%d" % i, num=GATHER_SEM + 60 + i) for i in range(4)]
    m.fetched = [nc.alloc_semaphore("fetched%d" % i, num=GATHER_SEM + 70 + i) for i in range(16)]
    m.eps = nc.alloc_sbuf_tensor("eps", [P, 1], F32)
    pick = m.big1[:, :, :].rearrange("p a b -> p (a b)")[:, 0:32 * P]
    with stage(nc, "landed") as (block, landed):

        @block.sync
        def _(sp):
            sp.dma_start(m.vec[:, :], d["vec"]).then_inc(landed, 16)
            sp.dma_start(m.ident[:, :], d["ident"]).then_inc(landed, 16)
            sp.dma_start(pick, d["pick"]).then_inc(landed, 16)
            sp.dma_start(m.order[:, :], d["order"]).then_inc(landed, 16)
            sp.dma_start(rc[:, :], d["route_consts"]).then_inc(landed, 16)
            sp.wait_ge(landed, 80)

        @block.vector
        def _(dve):
            dve.wait_ge(landed, 80)
            nc.vector.tensor_copy(m.pick[:, :], pick)
            nc.vector.tensor_copy(m.ident_bf[:, :], m.ident[:, :])

        @block.gpsimd
        def _(pool):
            nc.gpsimd.memset(m.eps[:, :], EPS)
            nc.gpsimd.memset(m.idle, 0.0)
            nc.gpsimd.memset(m.ones[:, :], 1.0)
            nc.gpsimd.memset(m.mean_w[:, :], 1.0 / D)


def patch_tokens(nc, m, d):
    kin = 6
    w = m.wa[:, 0:kin * D].rearrange("p (k n) -> p k n", k=kin)
    patches = m.big1[:, :, :].rearrange("p a b -> p (a b)")[:, 0:kin * BATCH * PATCHES].rearrange(
        "p (k n) -> p k n", k=kin)
    pos = m.small[:, 0:KD * 37].rearrange("p (k t) -> p k t", k=KD)
    load(nc, (patches, d["patches"]), (w, d["tok_w"]), (pos, d["tok_pos"]))
    h4 = m.h[:, :, :].rearrange("p k (b t) -> p k b t", t=SEQ)
    half = BATCH // 2
    with stage(nc, "product_ready", "pos_ready", "step") as (block, product_ready, pos_ready, step):

        @block.tensor
        def _(pe):
            for j in range(KD):
                for c in range(2):
                    for k in range(kin):
                        ins = nc.tensor.matmul(m.bank(2 * j + c, half * PATCHES), w[:, k, j * P:j * P + P],
                                               patches[:, k, c * half * PATCHES:(c + 1) * half * PATCHES],
                                               start=k == 0, stop=k == kin - 1)
                    ins.then_inc(product_ready, 1)

        @block.vector
        def _(dve):
            for k in range(KD):
                nc.vector.tensor_scalar(pos[:, k, 1:37], pos[:, k, 1:37], m.v("tok_b", k), None,
                                        ALU.add).then_inc(pos_ready, 1)
                nc.vector.tensor_scalar(pos[:, k, 0:1], pos[:, k, 0:1], m.v("cls", k), None,
                                        ALU.add).then_inc(pos_ready, 1)
            dve.wait_ge(pos_ready, 2 * KD)
            for k in range(KD):
                nc.vector.tensor_copy(h4[:, k, :, 0:1], pos[:, k, 0:1].unsqueeze(1).broadcast_to([P, BATCH, 1]))
            for j in range(KD):
                for c in range(2):
                    dve.wait_ge(product_ready, 2 * j + c + 1)
                    nc.vector.tensor_tensor(
                        h4[:, j, c * half:(c + 1) * half, 1:37],
                        m.bank(2 * j + c, half * PATCHES).rearrange("p (b t) -> p b t", t=PATCHES),
                        pos[:, j:j + 1, 1:37].broadcast_to([P, half, PATCHES]), ALU.add)


def text_encoder(nc, m, d):
    nt = BATCH * TEXT
    flat1 = m.big1[:, :, :].rearrange("p a b -> p (a b)")
    x = flat1[:, 0:KD * nt].rearrange("p (k n) -> p k n", k=KD)
    xn = flat1[:, KD * nt:2 * KD * nt].rearrange("p (k n) -> p k n", k=KD)
    cen = flat1[:, 2 * KD * nt:3 * KD * nt].rearrange("p (k n) -> p k n", k=KD)
    sq = flat1[:, 3 * KD * nt:4 * KD * nt].rearrange("p (k n) -> p k n", k=KD)
    rows = flat1[:, 4 * KD * nt:6 * KD * nt].rearrange("p (j n) -> p j n", j=8)[:, 0:4, :]
    hid = m.big2[:, :, :].rearrange("p a b -> p (a b)")[:, 0:8 * nt].rearrange("p (k n) -> p k n", k=8)
    work = (cen, sq)
    halves = [(0, nt // 2), (nt // 2, nt // 2)]
    idx = nc.alloc_sbuf_tensor("idx", [P, 4], I32)
    wrapped = nc.alloc_sbuf_tensor("wrapped", [P, 4], I32)
    pos = m.xn[:, 0, 0:KD * TEXT].rearrange("p (k t) -> p k t", k=KD)
    fresh = m.s1[0:STATE, 0, 0:nt]
    load(nc, (idx[:, :], d["tokens"]), (pos, d["txt_pos"]), (fresh, d["fresh"]))
    gathered = nc.alloc_semaphore("gathered", num=GATHER_SEM)
    with stage(nc, "index_step", "turned") as (block, index_step, turned):

        @block.vector
        def _(dve):
            link = linker(dve, index_step)
            link(nc.vector.tensor_scalar(wrapped[:, :], idx[:, :], 0.0, float(VOCAB), ALU.is_lt, ALU.mult))
            link(nc.vector.tensor_tensor(idx[:, :], idx[:, :], wrapped[:, :], ALU.add))
            nc.vector.tensor_scalar(idx[:, :], idx[:, :], 0.0, float(VOCAB - 1), ALU.max,
                                    ALU.min).then_inc(index_step, 1)
            for k in range(KD):
                dve.wait_ge(turned, k + 1)
                nc.vector.tensor_tensor(
                    x[:, k, :].rearrange("p (b t) -> p b t", t=TEXT),
                    m.bank(k).rearrange("p (b t) -> p b t", t=TEXT),
                    pos[:, k:k + 1, :].broadcast_to([P, BATCH, TEXT]), ALU.add)

        @block.gpsimd
        def _(pool):
            pool.wait_ge(index_step, 3)
            for j in range(4):
                pool.indirect_dma_start(
                    rows[:, j, :], None, d["emb"], bass.IndirectOffsetOnAxis(ap=idx[:, j:j + 1], axis=0),
                ).then_inc(gathered, 16)

        @block.tensor
        def _(pe):
            pe.wait_ge(gathered, 64)
            for k in range(KD):
                for j in range(4):
                    ins = nc.tensor.transpose(m.bank(k)[:, j * P:j * P + P], rows[:, j, k * P:k * P + P],
                                              m.ident[:, :])
                ins.then_inc(turned, 1)

    wB = m.wa[:, 0:KD * STATE].rearrange("p (k n) -> p k n", k=KD)
    wD = m.wa[:, 128:128 + KD * D].rearrange("p (k n) -> p k n", k=KD)
    wC = m.wa[0:STATE, 640:640 + D]
    w1 = m.wa[:, 1024:1024 + KD * FF].rearrange("p (k n) -> p k n", k=KD)
    w2 = m.wa[:, 4096:4096 + 8 * D].rearrange("p (k n) -> p k n", k=8)
    decay = m.s2[0:STATE, 0, 0:nt]
    states = m.s2[0:STATE, 1, 0:nt]
    a = m.s1[0:STATE, 1, 0:1]
    L = LVEC
    lv = lambda name, k: m.lvec[:, L[name] + k:L[name] + k + 1]
    chunks = [(0, nt)]
    with nc.Fori(0, LAYERS) as layer:
        load(nc, (wB, d["B"][layer]), (wD, d["Dw"][layer]), (wC, d["C"][layer]), (w1, d["w1"][layer]),
             (m.lvec[:, :], d["lvec"][layer]), (w2, d["w2"][layer]))
        layernorm(nc, m, full(x), full(xn), halves, lambda k: lv("ln1_s", k), lambda k: lv("ln1_b", k), work=work)
        with stage(nc, "input_ready", "decay_step", "scanned", "mixed") as (
                block, input_ready, decay_step, scanned, mixed):

            @block.scalar
            def _(act):
                nc.scalar.activation(a, m.lvec[0:STATE, L["A"]:L["A"] + 1], ACT.Sigmoid).then_inc(decay_step, 1)

            @block.tensor
            def _(pe):
                for k in range(KD):
                    ins = nc.tensor.matmul(m.bank(0, nt, STATE), wB[:, k, :], xn[:, k, :], start=k == 0,
                                           stop=k == KD - 1)
                ins.then_inc(input_ready, 1)
                for j in range(KD):
                    for k in range(KD):
                        nc.tensor.matmul(m.bank(1 + j, nt), wD[:, k, j * P:j * P + P], xn[:, k, :], start=k == 0,
                                         stop=False)
                    if j == 0:
                        pe.wait_ge(scanned, 1)
                    nc.tensor.matmul(m.bank(1 + j, nt), wC[:, j * P:j * P + P], states, start=False,
                                     stop=True).then_inc(mixed, 1)

            @block.vector
            def _(dve):
                dve.wait_ge(decay_step, 1)
                nc.vector.tensor_scalar(decay, fresh, a, None, ALU.mult).then_inc(decay_step, 1)
                dve.wait_ge(decay_step, 2)
                dve.wait_ge(input_ready, 1)
                nc.vector.tensor_tensor_scan(states, decay, m.bank(0, nt, STATE), 0.0, ALU.mult,
                                             ALU.add).then_inc(scanned, 1)
                for j in range(KD):
                    dve.wait_ge(mixed, j + 1)
                    nc.vector.tensor_tensor(x[:, j, :], x[:, j, :], m.bank(1 + j, nt), ALU.add)

        layernorm(nc, m, full(x), full(xn), halves, lambda k: lv("ln2_s", k), lambda k: lv("ln2_b", k), work=work)
        linear(nc, m, full(xn), lambda k, j: w1[:, k, j * P:j * P + P], KD, 8, chunks,
               lambda j, o, n, acc, link: nc.scalar.activation(hid[:, j, o:o + n], acc, ACT.Gelu, bias=lv("b1", j)))
        linear(nc, m, full(hid), lambda k, j: w2[:, k, j * P:j * P + P], 8, KD, chunks,
               add_to(nc, m, x, lambda j: lv("b2", j)), on="vector")
    h4 = m.h[:, :, :].rearrange("p k (b t) -> p k b t", t=SEQ)
    layernorm(nc, m, full(x), lambda k, o, n: h4[:, k, o // TEXT:(o + n) // TEXT, 1 + PATCHES:SEQ], halves,
              lambda k: m.v("lnf_s", k), lambda k: m.v("lnf_b", k), fold=TEXT, work=work)


def pieces(base, n):
    at = base
    while at < base + n:
        k = min(base + n, (at // BANK + 1) * BANK) - at
        yield at, at - base, k
        at += k


def clear_results(nc, m):
    with stage(nc, "zeroed") as (block, zeroed):

        @block.vector
        def _(dve):
            nc.vector.memset(m.zeros[:, :], 0.0).then_inc(zeroed, 1)

        @block.sync
        def _(sp):
            sp.wait_ge(zeroed, 1)
            sp.dma_start(m.y_rows.rearrange("(p j r) n -> p j (r n)", p=P, r=4),
                         m.zeros[:, :].unsqueeze(1).broadcast_to([P, TABLE // 4, 4 * D])).then_inc(m.y_cleared, 16)


def selective_scan(nc, m, d):
    x2 = m.big2[:, 0:KD, :]
    xi, z = m.big1[:, 0:4, :], m.big1[:, 4:8, :]
    xc, delta = m.big2[:, 0:4, :], m.big2[:, 4:8, :]
    w_in = m.wa[:, 0:2048].rearrange("p (k n) -> p k n", k=KD)
    w_dt = m.wa[:, 2048:2560].rearrange("p (k n) -> p k n", k=4)
    w_bc = m.wa[:, 2560:3072].rearrange("p (k n) -> p k n", k=4)
    w_out = m.wa[:, 3072:4096].rearrange("p (k n) -> p k n", k=4)
    neg_a = m.small[:, 1200:1264]
    load(nc, (w_in, d["in_proj"]), (w_dt, d["dt_rows"]), (w_bc, d["bc_rows"]), (w_out, d["out_proj"]))
    layernorm(nc, m, full(m.h), full(m.xn), CHUNKS)
    layernorm(nc, m, full(m.xn), full(x2), CHUNKS, lambda k: m.v("norm_w", k), lambda k: m.v("norm_b", k))
    linear(nc, m, full(x2), lambda k, j: w_in[:, k, j * P:j * P + P], KD, 8, CHUNKS,
           lambda j, o, n, acc, link: nc.scalar.copy(m.big1[:, j, o:o + n], acc))

    with stage(nc, "conv_step", "conv_ready", "rates_ready") as (block, conv_step, conv_ready, rates_ready):
        @block.vector
        def _(dve):
            link = linker(dve, conv_step)
            for k in range(4):
                link(nc.vector.tensor_scalar(xc[:, k, :], xi[:, k, :], m.v("conv_w", 4 * k + 3), m.v("conv_b", k),
                                             ALU.mult, ALU.add))
                to = xc[:, k, :].rearrange("p (b t) -> p b t", t=SEQ)
                of = xi[:, k, :].rearrange("p (b t) -> p b t", t=SEQ)
                for back in (1, 2, 3):
                    ins = nc.vector.scalar_tensor_tensor(
                        out=to[:, :, back:], in0=of[:, :, :SEQ - back], scalar=m.v("conv_w", 4 * k + 3 - back),
                        in1=to[:, :, back:], op0=ALU.mult, op1=ALU.add)
                    link(ins)
                nc.vector.engine_nop().then_inc(conv_ready, 1)
            dve.wait_ge(rates_ready, 1)
            nc.vector.tensor_scalar(neg_a, neg_a, -1.0, None, ALU.mult)

        @block.scalar
        def _(act):
            c = VEC["A_log"][0]
            nc.scalar.activation(neg_a, m.vec[:, c:c + 64], ACT.Exp).then_inc(rates_ready, 1)
            for k in range(4):
                act.wait_ge(conv_ready, k + 1)
                nc.scalar.activation(xc[:, k, :], xc[:, k, :], ACT.Silu)
            for k in range(4):
                nc.scalar.activation(z[:, k, :], z[:, k, :], ACT.Silu)

    with stage(nc, "dt_ready", "dt_step", "log_ready", "dt_taken", "relu_ready") as (
            block, dt_ready, dt_step, log_ready, dt_taken, relu_ready):
        @block.tensor
        def _(pe):
            for c, (o, n) in enumerate(CHUNKS):
                for k in range(4):
                    ins = nc.tensor.matmul(m.bank(c, n), w_dt[:, k, :], xc[:, k, o:o + n], start=k == 0, stop=k == 3)
                ins.then_inc(dt_ready, 1)

        @block.scalar
        def _(act):
            link = linker(act, dt_step)
            for c, (o, n) in enumerate(CHUNKS):
                act.wait_ge(dt_ready, c + 1)
                for k in range(4):
                    ins = nc.scalar.activation(delta[:, k, o:o + n], m.bank(c, n), ACT.Identity,
                                               scale=m.v("dt_w", k), bias=m.v("dt_b", k))
            link(ins)
            for k in range(4):
                t = m.s1[:, k % 2, :]
                if k >= 2:
                    act.wait_ge(dt_taken, k - 1)
                link(nc.scalar.activation(t, delta[:, k, :], ACT.Abs))
                link(nc.scalar.activation(t, t, ACT.Exp, scale=-1.0))
                nc.scalar.activation(t, t, ACT.Ln, bias=1.0).then_inc(log_ready, 1)

        @block.vector
        def _(dve):
            for k in range(4):
                dve.wait_ge(log_ready, k + 1)
                nc.vector.scalar_tensor_tensor(out=delta[:, k, :], in0=delta[:, k, :], scalar=0.0,
                                               in1=m.s1[:, k % 2, :], op0=ALU.max, op1=ALU.add).then_inc(dt_taken, 1)
            dve.wait_ge(dt_taken, 4)
            for k in range(4):
                nc.vector.tensor_tensor(xi[:, k, :], delta[:, k, :], xc[:, k, :], ALU.mult)

    def split(j, o, n, acc, link):
        t1, r, t2 = m.parts[:, 0, o:o + n], m.s1[:, 0, o:o + n], m.parts[:, 1, o:o + n]
        link(nc.vector.tensor_copy(t1, acc))
        link(nc.vector.tensor_tensor(r, acc, t1, ALU.subtract))
        link(nc.vector.tensor_copy(t2, r))
        link(nc.vector.tensor_copy(t1[32:64, :], t2[32:64, :]))
        link(nc.vector.tensor_tensor(r, r, t2, ALU.subtract))
        return nc.vector.tensor_copy(t1[64:96, :], r[64:96, :])
    linear(nc, m, full(xc), lambda k, j: w_bc[:, k, :], 4, 1, CHUNKS, split, on="vector")

    decay = [m.s1[:, i, :] for i in range(2)]
    state = [m.s2[:, i, :] for i in range(2)]
    c_row = [m.s3[:, i, :] for i in range(2)]
    inflow, seen, skip = m.wa[:, 4096:4096 + N], [m.wa[:, 4096 + i * N:4096 + (i + 1) * N] for i in (1, 2)], \
        m.small[:, 0:N]
    tokens = lambda a: a.rearrange("p (b t) -> p b t", t=SEQ)
    Y, B = 0, 3 * BANK
    NQ, QW = 4, N // 4
    for k in range(4):
        u = xi[:, k, :]
        with stage(nc, "cleared", "skip_ready", "b_ready", "c_ready", "c_taken", "summed", "decay_ready",
                   "inflow_ready", "scanned", "seen_ready") as (
                block, cleared, skip_ready, b_ready, c_ready, c_taken, summed, decay_ready, inflow_ready, scanned,
                seen_ready):

            @block.tensor
            def _(pe):
                def spread_b(row):
                    for at, o, n in pieces(B, N):
                        ins = nc.tensor.matmul(m.ps[:, at:at + n], m.pick[:, bass.ds(row * P, P)],
                                               m.parts[:, 0, o:o + n], start=True, stop=True)
                    ins.then_inc(b_ready, 1)

                def spread_c(i, peeled=False):
                    for q in range(NQ):
                        if not peeled or q >= 2:
                            pe.wait_ge(c_taken, i * NQ + (q - 1))
                        nc.tensor.matmul(m.bank(6 + q % 2, QW), m.pick[:, bass.ds((i + DS) * P, P)],
                                         m.parts[:, 0, q * QW:(q + 1) * QW], start=True, stop=True).then_inc(c_ready, 1)

                def add_y(what, first):
                    for at, o, n in pieces(Y, N):
                        ins = nc.tensor.matmul(m.ps[:, at:at + n], m.ident[:, :], what[:, o:o + n], start=first,
                                               stop=False, skip_group_check=True)
                    return ins

                spread_b(0)
                pe.wait_ge(skip_ready, 1)
                add_y(skip, True)
                spread_c(0, True)
                pe.wait_ge(inflow_ready, 1)
                spread_b(1)
                spread_c(1)
                pe.wait_ge(seen_ready, 1)
                add_y(seen[0], False).then_inc(summed, 1)
                with pe.Fori(0, DS // 2 - 1) as pair:
                    for s in range(2):
                        i = pair * 2 + 1
                        pe.wait_ge(inflow_ready, i + (s + 1))
                        spread_b(i + (s + 1))
                        spread_c(i + (s + 1))
                        pe.wait_ge(seen_ready, i + (s + 1))
                        add_y(seen[(s + 1) % 2], False).then_inc(summed, 1)
                pe.wait_ge(seen_ready, DS)
                add_y(seen[1], False).then_inc(summed, 1)

            @block.scalar
            def _(act):
                act.wait_ge(cleared, 1)

                def rates(i, s, peeled=False):
                    if not peeled:
                        act.wait_ge(scanned, i + (s - 1))
                    nc.scalar.activation(
                        tokens(decay[s])[:, :, 1:], tokens(delta[:, k, :])[:, :, 1:], ACT.Exp,
                        scale=m.small[:, bass.ds(i + (1200 + k * DS + s), 1)]).then_inc(decay_ready, 1)
                    for q in range(NQ):
                        act.wait_ge(c_ready, i * NQ + (s * NQ + q + 1))
                        if q == 0 and not peeled:
                            act.wait_ge(seen_ready, i + (s - 1))
                        nc.scalar.copy(c_row[s][:, q * QW:(q + 1) * QW], m.bank(6 + q % 2, QW)).then_inc(c_taken, 1)

                for s in range(2):
                    rates(0, s, True)
                with act.Fori(1, DS // 2) as pair:
                    for s in range(2):
                        rates(pair * 2, s)

            @block.gpsimd
            def _(pool):
                def see(i, s, peeled=False):
                    pool.wait_ge(scanned, i + (s + 1))
                    pool.wait_ge(c_taken, i * NQ + (s + 1) * NQ)
                    if not peeled:
                        pool.wait_ge(summed, i + (s - 1))
                    nc.gpsimd.tensor_tensor(seen[s], state[s], c_row[s], ALU.mult).then_inc(seen_ready, 1)

                for s in range(2):
                    see(0, s, True)
                with pool.Fori(1, DS // 2) as pair:
                    for s in range(2):
                        see(pair * 2, s)

            @block.vector
            def _(dve):
                nc.vector.tensor_scalar(skip, xc[:, k, :], m.v("D_skip", k), None, ALU.mult).then_inc(skip_ready, 1)
                nc.vector.memset(tokens(decay[0])[:, :, 0:1], 0.0)
                nc.vector.memset(tokens(decay[1])[:, :, 0:1], 0.0).then_inc(cleared, 1)
                dve.wait_ge(cleared, 1)

                def step(i, s, peeled=False):
                    dve.wait_ge(b_ready, i + (s + 1))
                    if not peeled or s:
                        dve.wait_ge(scanned, i + s)
                    nc.vector.tensor_tensor(inflow, u, m.ps[:, B:B + N], ALU.mult).then_inc(inflow_ready, 1)
                    dve.wait_ge(inflow_ready, i + (s + 1))
                    dve.wait_ge(decay_ready, i + (s + 1))
                    if not peeled:
                        dve.wait_ge(seen_ready, i + (s - 1))
                    nc.vector.tensor_tensor_scan(state[s], decay[s], inflow, 0.0, ALU.mult,
                                                 ALU.add).then_inc(scanned, 1)

                for s in range(2):
                    step(0, s, True)
                with dve.Fori(1, DS // 2) as pair:
                    for s in range(2):
                        step(pair * 2, s)
                dve.wait_ge(summed, DS)
                nc.vector.tensor_tensor(z[:, k, :], z[:, k, :], m.ps[:, Y:Y + N], ALU.mult)

    def residual(j, o, n, acc, link):
        out = m.h[:, j, o:o + n]
        link(nc.vector.tensor_tensor(out, out, acc, ALU.add))
        return nc.vector.tensor_tensor(out, out, m.xn[:, j, o:o + n], ALU.add)
    linear(nc, m, full(z), lambda k, j: w_out[:, k, j * P:j * P + P], 4, KD, CHUNKS, residual, on="vector")


def route(nc, m, groups, experts, w, sigmoid):
    g_all = NROWT * groups
    ne = groups * experts
    cols_ = g_all * experts
    flat = m.big1[:, :, :].rearrange("p a b -> p (a b)")
    tile3 = lambda i, e=experts: flat[0:ROWT, i * 768:i * 768 + g_all * e].rearrange("p (g e) -> p g e", e=e)
    sc, key, one, two, tmp = (tile3(i) for i in range(5))
    order = m.order[0:ROWT, E0 - experts:E0].unsqueeze(1).broadcast_to([ROWT, g_all, experts])
    red = [m.small[0:ROWT, 32 * i:32 * i + g_all].unsqueeze(2) for i in range(4)]
    wide = lambda a: a.broadcast_to([ROWT, g_all, experts])
    parts = m.big2[:, :, :].rearrange("p a b -> p (a b)")[0:ROWT, 0:g_all * 64].bitcast(BF16).rearrange(
        "p (g s) -> p g s", s=P)
    half = NROWT // 2
    with stage(nc, "logits_ready", "logits_taken", "exp_ready", "route_step", "parts_ready", "turned",
               "turned_taken") as (
            block, logits_ready, logits_taken, exp_ready, route_step, parts_ready, turned, turned_taken):

        @block.tensor
        def _(pe):
            for t in range(NROWT):
                at = (t // half) * BANK + (t % half) * ne
                for k in range(KD):
                    ins = nc.tensor.matmul(m.ps[0:ROWT, at:at + ne], m.xn[:, k, t * ROWT:(t + 1) * ROWT],
                                           w[:, k, :], start=k == 0, stop=k == KD - 1)
            ins.then_inc(logits_ready, 1)
            if not sigmoid:
                return
            pe.wait_ge(parts_ready, 1)
            for g in range(groups):
                for t in range(NROWT):
                    at = (2 + 2 * g) * 2 * BANK + (t // 11) * 2 * BANK + (t % 11) * ROWT
                    ins = nc.tensor.transpose(m.ps_bf[:, at:at + ROWT], parts[:, t * groups + g, :],
                                              m.ident_bf[0:ROWT, 0:ROWT])
                ins.then_inc(turned, 1)

        @block.scalar
        def _(act):
            act.wait_ge(logits_taken, 1)
            nc.scalar.activation(sc, sc, ACT.Exp, scale=-1.0 if sigmoid else 1.0).then_inc(exp_ready, 1)
            if not sigmoid:
                return
            for g in range(groups):
                act.wait_ge(turned, g + 1)
                base = (2 + 2 * g) * 2 * BANK
                nc.scalar.copy(m.parts[:, g, 0:11 * ROWT], m.ps_bf[:, base:base + 11 * ROWT])
                nc.scalar.copy(m.parts[:, g, 11 * ROWT:N], m.ps_bf[:, base + 2 * BANK:base + 2 * BANK + ROWT])

        @block.vector
        def _(dve):
            link = linker(dve, route_step)
            tt, ts = nc.vector.tensor_tensor, nc.vector.tensor_scalar
            if sigmoid:
                link(nc.vector.memset(parts, 0.0))
            dve.wait_ge(logits_ready, 1)
            for b in range(2):
                link(nc.vector.tensor_copy(sc[:, b * (g_all // 2):(b + 1) * (g_all // 2), :],
                                           m.ps[0:ROWT, b * BANK:b * BANK + cols_ // 2].rearrange(
                                               "p (g e) -> p g e", e=experts)))
            if sigmoid:
                nc.vector.engine_nop().then_inc(logits_taken, 1)
                dve.wait_ge(exp_ready, 1)
                link(ts(sc, sc, 1.0, None, ALU.add))
                link(nc.vector.reciprocal(sc, sc))
            else:
                link(nc.vector.tensor_reduce(red[0].squeeze(2), sc, AX_X, ALU.max))
                tt(sc, sc, wide(red[0]), ALU.subtract).then_inc(logits_taken, 1)
                dve.wait_ge(exp_ready, 1)
                link(nc.vector.tensor_reduce(red[0].squeeze(2), sc, AX_X, ALU.add))
                link(nc.vector.reciprocal(red[0], red[0]))
                link(tt(sc, sc, wide(red[0]), ALU.mult))

            def first_of_max(of, best, out):
                link(nc.vector.tensor_reduce(best.squeeze(2), of, AX_X, ALU.max))
                link(tt(key, of, wide(best), ALU.is_equal))
                link(tt(key, key, order, ALU.mult))
                link(nc.vector.tensor_reduce(red[3].squeeze(2), key, AX_X, ALU.max))
                link(tt(out, order, wide(red[3]), ALU.is_equal))

            first_of_max(sc, red[0], one)
            link(nc.vector.scalar_tensor_tensor(out=tmp, in0=one, scalar=-4.0, in1=sc, op0=ALU.mult, op1=ALU.add))
            first_of_max(tmp, red[1], two)
            if not sigmoid:
                for r in red[0:2]:
                    ts(r, r, 0.5, None, ALU.mult)
                return
            link(tt(one, one, wide(red[0]), ALU.mult))
            link(tt(two, two, wide(red[1]), ALU.mult))
            link(tt(one, one, two, ALU.add))
            link(tt(red[0], red[0], red[1], ALU.add))
            link(ts(red[0], red[0], 1e-20, None, ALU.add))
            link(nc.vector.reciprocal(red[0], red[0]))
            link(tt(one, one, wide(red[0]), ALU.mult))
            for p in range(3):
                part = parts[:, :, 32 * p:32 * p + experts]
                link(nc.vector.tensor_copy(part, one))
                if p < 2:
                    link(tt(one, one, part, ALU.subtract))
            nc.vector.engine_nop().then_inc(parts_ready, 1)


FLOOR = 0.498046875
MAGIC = 1.5 * 2.0 ** 23


def mixture0(nc, m, d):
    wr = m.small[:, 1200:1200 + KD * 2 * E0].rearrange("p (k n) -> p k n", k=KD)
    load(nc, (wr, d["router"]))
    layernorm(nc, m, full(m.h), full(m.xn), CHUNKS)
    route(nc, m, 2, E0, wr, False)
    blocks = dispatch(nc, m, d)
    run_blocks(nc, m, d, blocks)
    combine(nc, m, blocks)


def dispatch(nc, m, d):
    ne = 2 * E0
    g_all = 2 * NROWT
    wide_n = g_all * E0
    flat1 = m.big1[:, :, :].rearrange("p a b -> p (a b)")
    flat2 = m.big2[:, :, :].rearrange("p a b -> p (a b)")
    tile = lambda i, rows=ROWT: flat1[0:rows, i * 768:(i + 1) * 768]
    one, two, both, slot, tmp = tile(2), tile(3), tile(1), tile(0), tile(4)
    by_expert = lambda a: a.rearrange("p (t e) -> p t e", e=ne)
    by_group = lambda a: a.rearrange("p (g e) -> p g e", e=E0)
    before = flat1[:, 3840:3840 + wide_n]
    c = m.route_consts
    tri, ones, iota, token, place = c["tri"], c["ones"], c["iota"], c["token"], c["place"]
    counts, n_blocks, ends, starts, hits = (flat1[:, 4700 + 64 * i:4764 + 64 * i] for i in range(5))
    pair_slot, pair_block, pair_place = (flat1[0:ROWT, 5100 + 48 * i:5148 + 48 * i] for i in range(3))
    expert_col = flat1[:, 5300:5301]
    rounds_f = flat1[0:1, 5302:5303]
    place_hot = [flat1[0:ROWT, 5400 + P * i:5400 + P * (i + 1)] for i in range(4)]
    block_hot = [flat1[0:ROWT, 6000 + TABLE * i:6000 + TABLE * (i + 1)] for i in range(4)]
    rows = flat2[0:ROWT, 0:NROWT * D].rearrange("p (t n) -> p t n", n=D)
    x_rows, y_rows = m.x_rows, m.y_rows
    pair_idx = m.pair_idx
    slot_token, block_expert, rounds = m.slot_token, m.block_expert, m.rounds
    half = wide_n // 2
    pairs = 2 * g_all
    with stage(nc, "both_ready", "sums_ready", "step", "pairs_ready", "hot_ready", "hot_used", "table_ready",
               "experts_ready", "experts_turned", "rows_turned", "rows_taken", "rows_stored") as (
            block, both_ready, sums_ready, step, pairs_ready, hot_ready, hot_used, table_ready, experts_ready,
            experts_turned, rows_turned, rows_taken, rows_stored):

        @block.tensor
        def _(pe):
            pe.wait_ge(both_ready, 1)
            for b in range(2):
                nc.tensor.matmul(m.bank(b, half, ROWT), tri[0:ROWT, 0:ROWT], both[:, b * half:(b + 1) * half],
                                 start=True, stop=True)
                ins = nc.tensor.matmul(m.bank(2 + b, half), ones[0:ROWT, :], both[:, b * half:(b + 1) * half],
                                       start=True, stop=True)
            ins.then_inc(sums_ready, 1)
            for t in range(NROWT):
                if t >= 2:
                    pe.wait_ge(rows_taken, t - 1)
                for k in range(KD):
                    ins = nc.tensor.transpose(m.ps[0:ROWT, (4 + t % 2) * BANK + k * P:(4 + t % 2) * BANK + (k + 1) * P],
                                              m.xn[:, k, t * ROWT:(t + 1) * ROWT], m.ident[:, :])
                ins.then_inc(rows_turned, 1)
            pe.wait_ge(experts_ready, 1)
            nc.tensor.transpose(m.ps[0:1, 7 * BANK:7 * BANK + TABLE], expert_col[0:TABLE, :],
                                m.ident[0:TABLE, 0:TABLE]).then_inc(experts_turned, 1)
            for a in range(pairs):
                pe.wait_ge(hot_ready, 2 * (a + 1))
                nc.tensor.matmul(m.ps[:, 6 * BANK:6 * BANK + TABLE], place_hot[a % 4], block_hot[a % 4],
                                 start=a == 0, stop=a == pairs - 1).then_inc(hot_used, 1)

        @block.scalar
        def _(act):
            for t in range(NROWT):
                act.wait_ge(rows_turned, t + 1)
                nc.scalar.copy(rows[:, t, :], m.bank(4 + t % 2, D, ROWT)).then_inc(rows_taken, 1)

        @block.sync
        def _(sp):
            sp.wait_ge(rows_taken, NROWT)
            sp.dma_start(x_rows.rearrange("(t p) n -> p t n", p=ROWT), rows).then_inc(rows_stored, 16)
            sp.wait_ge(rows_stored, 16)
            sp.wait_ge(m.y_cleared, 16)

        @block.vector
        def _(dve):
            link = linker(dve, step)
            tt, ts = nc.vector.tensor_tensor, nc.vector.tensor_scalar
            tt(both, one, two, ALU.add).then_inc(both_ready, 1)
            link(nc.vector.memset(before[:, 0:ne], 0.0))
            dve.wait_ge(sums_ready, 1)
            per_bank = NROWT // 2
            for t in range(NROWT):
                total = m.ps[:, (2 + t // per_bank) * BANK + (t % per_bank) * ne:][:, 0:ne]
                out = counts if t == NROWT - 1 else before[:, (t + 1) * ne:(t + 2) * ne]
                link(tt(out, before[:, t * ne:(t + 1) * ne], total, ALU.add))
            link(ts(n_blocks, counts, 1.0 / P, (P - 1.0) / P - FLOOR, ALU.mult, ALU.add))
            link(ts(n_blocks, n_blocks, MAGIC, -MAGIC, ALU.add, ALU.add))
            link(nc.vector.tensor_tensor_scan(ends, ones[:, 0:ne], n_blocks, 0.0, ALU.mult, ALU.add))
            link(tt(starts, ends, n_blocks, ALU.subtract))
            link(ts(hits, ends, place, None, ALU.is_le))
            link(nc.vector.tensor_reduce(expert_col, hits, AX_X, ALU.add))
            ts(expert_col, expert_col, ne - 1.0, None, ALU.min).then_inc(experts_ready, 1)
            link(ts(rounds_f, ends[0:1, ne - 1:ne], 0.25, 0.75 - 0.375, ALU.mult, ALU.add))
            link(ts(rounds_f, rounds_f, MAGIC, -MAGIC, ALU.add, ALU.add))
            link(nc.vector.tensor_copy(rounds, rounds_f))
            link(ts(starts, starts, float(P), None, ALU.mult))
            for b in range(2):
                link(tt(slot[:, b * half:(b + 1) * half], before[0:ROWT, b * half:(b + 1) * half],
                        m.bank(b, half, ROWT), ALU.add))
            link(tt(by_expert(slot), by_expert(slot),
                    starts[0:ROWT, :].unsqueeze(1).broadcast_to([ROWT, NROWT, ne]), ALU.add))
            for i, pick in enumerate((one, two)):
                link(tt(tmp, pick, slot, ALU.mult))
                link(nc.vector.tensor_reduce(pair_slot[:, i * g_all:(i + 1) * g_all], by_group(tmp), AX_X, ALU.add))
            link(nc.vector.tensor_copy(pair_idx, pair_slot))
            link(ts(pair_block, pair_slot, 1.0 / P, -FLOOR, ALU.mult, ALU.add))
            link(ts(pair_block, pair_block, MAGIC, -MAGIC, ALU.add, ALU.add))
            link(nc.vector.scalar_tensor_tensor(out=pair_place, in0=pair_block, scalar=-float(P), in1=pair_slot,
                                                op0=ALU.mult, op1=ALU.add))
            dve.wait_ge(experts_turned, 1)
            link(nc.vector.tensor_copy(block_expert, m.ps[0:1, 7 * BANK:7 * BANK + TABLE]))
            for a in range(pairs):
                if a >= 4:
                    dve.wait_ge(hot_used, a - 3)
                t = (a % g_all) // 2
                ts(place_hot[a % 4], iota[:, 0:P], pair_place[:, a:a + 1], None, ALU.is_equal).then_inc(hot_ready, 1)
                ts(block_hot[a % 4], iota[:, 0:TABLE], pair_block[:, a:a + 1], token[:, t:t + 1], ALU.is_equal,
                   ALU.mult).then_inc(hot_ready, 1)
            dve.wait_ge(hot_used, pairs)
            nc.vector.tensor_copy(slot_token, m.ps[:, 6 * BANK:6 * BANK + TABLE])
    return x_rows, y_rows, pair_idx, slot_token, block_expert, rounds


def run_blocks(nc, m, d, blocks):
    x_rows, y_rows, _, slot_token, block_expert, rounds = blocks
    ROUND = 4
    flat1 = m.big1[:, :, :].rearrange("p a b -> p (a b)")
    flat2 = m.big2[:, :, :].rearrange("p a b -> p (a b)")
    w = [flat1[:, i * 768:(i + 1) * 768] for i in range(ROUND)]
    xr = [flat1[:, 3072 + i * D:3072 + (i + 1) * D] for i in range(ROUND)]
    xt = [flat1[:, 4096 + i * D:4096 + (i + 1) * D] for i in range(ROUND)]
    gated = [flat2[:, i * P:(i + 1) * P] for i in range(ROUND)]
    hidden = [flat2[:, 512 + i * P:512 + (i + 1) * P] for i in range(ROUND)]
    y = [flat2[:, 1024 + i * D:1024 + (i + 1) * D] for i in range(ROUND)]
    idx = m.block_idx
    gathered = m.gathered
    experts = d["experts"].rearrange("e p n -> (e p) n")

    def value(i, r, more=0):
        return i * ROUND + (r + more)

    def wait(eng, sem, i, r, more):
        n = value(i, r, more)
        if not (isinstance(n, int) and n <= 0):
            eng.wait_ge(sem, n)

    def shifted_by(i, r, more):
        return i + (r + more) // ROUND, (r + more) % ROUND

    def all_rounds(eng, step, lead):
        for t in range(-lead, ROUND):
            step(t // ROUND, t % ROUND)
        n = eng.value_load(rounds, min_val=2, max_val=MAX_ROUNDS)
        with eng.Fori(1, n) as i:
            for r in range(ROUND):
                step(i, r)
        return n

    with stage(nc, "weights_0", "weights_1", "weights_2", "weights_3", "stored_0", "stored_1", "stored_2", "stored_3",
               "index_ready", "rows_turned", "xt_ready", "gate_ready", "silu_ready", "hidden_ready", "down_ready",
               "y_ready") as (
            block, weights_0, weights_1, weights_2, weights_3, stored_0, stored_1, stored_2, stored_3, index_ready,
            rows_turned, xt_ready, gate_ready, silu_ready, hidden_ready, down_ready, y_ready):
        weights = (weights_0, weights_1, weights_2, weights_3)
        stored = (stored_0, stored_1, stored_2, stored_3)

        @block.sync
        def _(sp):
            def cleared():
                sp.wait_ge(m.y_cleared, 16)

            def load_expert(i, r):
                e = sp.value_load(block_expert[0:1, bass.ds(value(i, r), 1)], min_val=0, max_val=2 * E0 - 1)
                at = sp.snap(e * P)
                wait(sp, down_ready, i, r, 1 - ROUND)
                cleared()
                sp.dma_start(w[r], experts[bass.ds(at, P), :]).then_inc(weights[r], 16)

            def step(i, r):
                n = value(i, r)
                if not isinstance(n, int) or n >= 0:
                    at = n * P if isinstance(n, int) else sp.snap(n * P)
                    wait(sp, y_ready, i, r, 1)
                    cleared()
                    sp.dma_start(y_rows[bass.ds(at, P), :], y[r]).then_inc(stored[r], 16)
                load_expert(*shifted_by(i, r, ROUND))
            all_rounds(sp, step, ROUND)

        @block.gpsimd
        def _(pool):
            def gather(i, r):
                wait(pool, rows_turned, i, r, 1 - ROUND)
                nc.gpsimd.tensor_copy(idx[r], slot_token[:, bass.ds(value(i, r), 1)]).then_inc(index_ready, 1)
                wait(pool, index_ready, i, r, 1)
                nc.gpsimd.tensor_tensor(m.idle, m.idle, m.idle, ALU.add)
                pool.indirect_dma_start(xr[r], None, x_rows, bass.IndirectOffsetOnAxis(ap=idx[r], axis=0)).then_inc(
                    gathered[r], 16)

            def step(i, r):
                gather(*shifted_by(i, r, ROUND))
            n = all_rounds(pool, step, ROUND)
            for r in range(ROUND):
                pool.wait_ge(gathered[r], n * 16 + 16)
                pool.wait_ge(weights[r], n * 16 + 16)
                pool.wait_ge(stored[r], n * 16)

        @block.tensor
        def _(pe):
            def turn(i, r):
                pe.wait_ge(gathered[r], i * 16 + 16)
                wait(pe, xt_ready, i, r, -1)
                for k in range(KD):
                    to = (r % 2) * BANK + k * P
                    ins = nc.tensor.transpose(m.ps[:, to:to + P], xr[r][:, k * P:(k + 1) * P], m.ident[:, :])
                ins.then_inc(rows_turned, 1)

            def gate_up(i, r):
                pe.wait_ge(weights[r], i * 16 + 16)
                wait(pe, xt_ready, i, r, 1)
                wait(pe, hidden_ready, i, r, -1)
                for half in range(2):
                    to = (2 + r % 2) * BANK + half * P
                    for k in range(KD):
                        ins = nc.tensor.matmul(m.ps[:, to:to + P], w[r][:, half * D + k * P:half * D + (k + 1) * P],
                                               xt[r][:, k * P:(k + 1) * P], start=k == 0, stop=k == KD - 1)
                ins.then_inc(gate_ready, 1)

            def down(i, r):
                wait(pe, hidden_ready, i, r, 1)
                wait(pe, y_ready, i, r, -1)
                nc.tensor.matmul(m.bank(4 + r % 2, D), hidden[r], w[r][:, 2 * D:3 * D], start=True,
                                 stop=True).then_inc(down_ready, 1)

            def step(i, r):
                turn(*shifted_by(i, r, 2))
                n = value(i, r, 1)
                if not isinstance(n, int) or n >= 0:
                    gate_up(*shifted_by(i, r, 1))
                n = value(i, r)
                if not isinstance(n, int) or n >= 0:
                    down(i, r)
            all_rounds(pe, step, 2)

        @block.scalar
        def _(act):
            def step(i, r):
                n = value(i, r, 1)
                if not isinstance(n, int) or n >= 0:
                    i1, r1 = shifted_by(i, r, 1)
                    wait(act, gate_ready, i1, r1, 1)
                    wait(act, hidden_ready, i1, r1, 1 - ROUND)
                    nc.scalar.activation(gated[r1], m.ps[:, (2 + r1 % 2) * BANK:(2 + r1 % 2) * BANK + P],
                                         ACT.Silu).then_inc(silu_ready, 1)
                n = value(i, r)
                if not isinstance(n, int) or n >= 0:
                    wait(act, down_ready, i, r, 1)
                    if not isinstance(i, int) or i >= 1:
                        act.wait_ge(stored[r], i * 16)
                    nc.scalar.copy(y[r], m.bank(4 + r % 2, D)).then_inc(y_ready, 1)
            all_rounds(act, step, 1)

        @block.vector
        def _(dve):
            def step(i, r):
                i2, r2 = shifted_by(i, r, 2)
                wait(dve, rows_turned, i2, r2, 1)
                wait(dve, gate_ready, i2, r2, 1 - ROUND)
                nc.vector.tensor_copy(xt[r2], m.bank(r2 % 2, D)).then_inc(xt_ready, 1)
                n = value(i, r, 1)
                if not isinstance(n, int) or n >= 0:
                    i1, r1 = shifted_by(i, r, 1)
                    wait(dve, silu_ready, i1, r1, 1)
                    wait(dve, down_ready, i1, r1, 1 - ROUND)
                    at = (2 + r1 % 2) * BANK + P
                    nc.vector.tensor_tensor(hidden[r1], gated[r1], m.ps[:, at:at + P], ALU.mult).then_inc(
                        hidden_ready, 1)
            all_rounds(dve, step, 2)


def combine(nc, m, blocks):
    _, y_rows, pair_idx, _, _, _ = blocks
    g_all = 2 * NROWT
    flat2 = m.big2[:, :, :].rearrange("p a b -> p (a b)")
    ring = 16
    got = [flat2[0:ROWT, i * D:(i + 1) * D] for i in range(ring)]
    diag = [flat2[0:ROWT, ring * D + i * P:ring * D + i * P + ROWT] for i in range(8)]
    weight = [m.small[0:ROWT, 32 * i:32 * i + g_all] for i in range(2)]
    order = [(t, choice * g_all + 2 * t + g) for t in range(NROWT) for choice in range(2) for g in range(2)]
    with stage(nc, "diag_ready", "used", "sum_taken") as (block, diag_ready, used, sum_taken):

        @block.gpsimd
        def _(pool):
            for n, (_, a) in enumerate(order):
                if n >= ring:
                    pool.wait_ge(used, n - ring + 1)
                pool.indirect_dma_start(got[n % ring], None, y_rows, bass.IndirectOffsetOnAxis(
                    ap=pair_idx[:, a:a + 1], axis=0)).then_inc(m.fetched[n % ring], 16)

        @block.vector
        def _(dve):
            def diagonal(n):
                a = order[n][1]
                if n >= 8:
                    dve.wait_ge(used, n - 7)
                nc.vector.tensor_scalar(diag[n % 8], m.ident[0:ROWT, 0:ROWT],
                                        weight[a // g_all][:, a % g_all:a % g_all + 1], None,
                                        ALU.mult).then_inc(diag_ready, 1)
            for n in range(4):
                diagonal(n)
            for t in range(NROWT):
                if t + 1 < NROWT:
                    for n in range(4 * t + 4, 4 * t + 8):
                        diagonal(n)
                dve.wait_ge(used, 4 * (t + 1))
                out = m.h[:, :, t * ROWT:(t + 1) * ROWT]
                nc.vector.tensor_tensor(out, out, m.ps[:, (t % 2) * BANK:(t % 2) * BANK + KD * ROWT].rearrange(
                    "p (k n) -> p k n", k=KD), ALU.add).then_inc(sum_taken, 1)

        @block.tensor
        def _(pe):
            for t in range(NROWT):
                if t >= 2:
                    pe.wait_ge(sum_taken, t - 1)
                for q in range(4):
                    n = 4 * t + q
                    pe.wait_ge(m.fetched[n % ring], 16 * (n // ring + 1))
                    pe.wait_ge(diag_ready, n + 1)
                    for k in range(KD):
                        to = (t % 2) * BANK + k * ROWT
                        ins = nc.tensor.matmul(m.ps[:, to:to + ROWT], got[n % ring][:, k * P:(k + 1) * P],
                                               diag[n % 8], start=q == 0 and k == 0, stop=q == 3,
                                               skip_group_check=True)
                    ins.then_inc(used, 1)


def value_rows(nc, m, w_v, v):
    with stage(nc, "rows_ready", "rows_taken") as (block, rows_ready, rows_taken):

        @block.tensor
        def _(pe):
            for b in range(BATCH):
                if b >= 4:
                    pe.wait_ge(rows_taken, b - 3)
                for k in range(KD):
                    ins = nc.tensor.matmul(m.bank(b % 4, D, SEQ), m.xn[:, k, b * SEQ:(b + 1) * SEQ], w_v(k),
                                           start=k == 0, stop=k == KD - 1)
                ins.then_inc(rows_ready, 1)

        @block.scalar
        def _(act):
            for b in range(BATCH):
                act.wait_ge(rows_ready, b + 1)
                nc.scalar.copy(v[:, b, :], m.bank(b % 4, D, SEQ)).then_inc(rows_taken, 1)


def attend(nc, m, mask_dram, v_bias, topk):
    q, k = m.big1[:, 0:2, :], m.big1[:, 2:4, :]
    flat1 = m.big1[:, :, :].rearrange("p a b -> p (a b)")
    v = flat1[0:SEQ, 4 * N:4 * N + BATCH * D].rearrange("p (b n) -> p b n", b=BATCH)
    flat2 = m.big2[:, :, :].rearrange("p a b -> p (a b)")
    used = [0]

    def room(rows, n, copies):
        start = used[0]
        used[0] += n * copies
        return [flat2[0:rows, start + i * n:start + (i + 1) * n] for i in range(copies)]

    q_out = room(P, QSET, 2)
    v_out = room(SEQ, HPC * (P + HD), 2)
    turned_sb = room(SEQ, HPC * SEQ, 2)
    score = room(P, NQT * SEQ, 4)
    left = room(P, NHARD * SEQ, 2)
    top8 = [a.rearrange("p (j r e) -> p j r e", j=NHARD, r=TOPK // 8) for a in room(P, NHARD * TOPK, 2)]
    mask, = room(P, NQT * SEQ, 1)
    head_of, = room(P, HPC, 1)
    row_max, row_sum = room(P, 8, 4), room(P, 8, 4)
    att = m.s3
    easy = 2 * SEQ
    tile3 = lambda a: a.rearrange("p (j n) -> p j n", n=SEQ)
    wide = lambda a: a.unsqueeze(2).broadcast_to([P, NQT, SEQ])
    load(nc, (mask, mask_dram), (head_of, m.dram["head_of"]))
    steps, ROUND = 2 * BATCH, 4

    def value(i, r, more=0):
        return i * ROUND + (r + more)

    def wait(eng, sem, i, r, more):
        n = value(i, r, more)
        if not (isinstance(n, int) and n <= 0):
            eng.wait_ge(sem, n)

    def batch(i, r):
        return bass.ds((i * 2 + r // 2) * SEQ, SEQ)

    def rounds(eng, step):
        for t in range(-2, ROUND):
            step(t // ROUND, t % ROUND)
        with eng.Fori(1, steps // ROUND - 1) as i:
            for r in range(ROUND):
                step(i, r)
        for t in range(steps - ROUND, steps + 1):
            step(t // ROUND, t % ROUND)

    def has(i, r, more):
        n = value(i, r, more)
        return not isinstance(n, int) or 0 <= n < steps

    def shifted_by(i, r, more):
        return i + (r + more) // ROUND, (r + more) % ROUND

    with stage(nc, "cleared", "q_out_ready", "v_out_ready", "scores_ready", "scores_taken", "shifted", "exp_ready",
               "weights_ready", "turned", "turned_taken", "out_ready", "out_taken", "shift_step",
               "divide_step") as (
            block, cleared, q_out_ready, v_out_ready, scores_ready, scores_taken, shifted, exp_ready, weights_ready,
            turned, turned_taken, out_ready, out_taken, shift_step, divide_step):

        @block.gpsimd
        def _(pool):
            for c in range(2):
                nc.gpsimd.memset(q_out[c], 0.0)
                nc.gpsimd.memset(v_out[c], 0.0).then_inc(cleared, 1)
            pool.wait_ge(cleared, 2)

            def set_out_queries(i, r):
                c = r % 2
                wait(pool, scores_ready, i, r, -1)
                for first, n, at in ((0, EASY, 0), (EASY, HARD, HPC * EASY)):
                    o = (i * 2 + r // 2) * SEQ + first
                    ins = nc.gpsimd.tensor_tensor(
                        q_out[c][:, at:at + HPC * n].rearrange("p (h t) -> p h t", h=HPC),
                        q[:, c:c + 1, bass.ds(o, n)].broadcast_to([P, HPC, n]),
                        head_of.unsqueeze(2).broadcast_to([P, HPC, n]), ALU.mult)
                ins.then_inc(q_out_ready, 1)

            def set_out_values(i, r):
                c = r % 2
                wait(pool, out_ready, i, r, -1)
                nc.gpsimd.tensor_copy(
                    v_out[c].rearrange("p (h n) -> p h n", h=HPC)[:, :, 0:HD],
                    v[:, bass.ds(i * 2 + r // 2, 1), c * P:(c + 1) * P].squeeze(1).rearrange(
                        "p (h n) -> p h n", h=HPC)).then_inc(v_out_ready, 1)

            def step(i, r):
                if has(i, r, 2):
                    set_out_queries(*shifted_by(i, r, 2))
                if has(i, r, 0):
                    set_out_values(i, r)
            rounds(pool, step)

        @block.tensor
        def _(pe):
            def scores(i, r):
                c = r % 2
                wait(pe, q_out_ready, i, r, 1)
                wait(pe, scores_taken, i, r, -1)
                for j in range(NQT):
                    ins = nc.tensor.matmul(m.ps[:, c * BANK + j * SEQ:c * BANK + (j + 1) * SEQ],
                                           q_out[c][:, QAT[j]:QAT[j] + P], k[:, c, batch(i, r)], start=True,
                                           stop=True)
                ins.then_inc(scores_ready, 1)

            def turn(i, r):
                wait(pe, weights_ready, i, r, 1)
                wait(pe, turned_taken, i, r, -1)
                for j in range(NQT):
                    to = (2 + 2 * (r % 2)) * BANK + j * P
                    ins = nc.tensor.transpose(m.ps[0:SEQ, to:to + P], score[r][:, j * SEQ:(j + 1) * SEQ],
                                              m.ident[:, :])
                ins.then_inc(turned, 1)

            def output(i, r):
                c = r % 2
                wait(pe, turned_taken, i, r, 1)
                wait(pe, v_out_ready, i, r, 1)
                wait(pe, out_taken, i, r, -1)
                for h in range(HPC):
                    ins = nc.tensor.matmul(m.bank(6 + c, SEQ), v_out[c][:, h * P:(h + 1) * P],
                                           turned_sb[c][:, h * SEQ:(h + 1) * SEQ], start=h == 0, stop=h == HPC - 1)
                ins.then_inc(out_ready, 1)

            def step(i, r):
                if has(i, r, 2):
                    scores(*shifted_by(i, r, 2))
                if has(i, r, 0):
                    turn(i, r)
                if has(i, r, -1):
                    output(*shifted_by(i, r, -1))
            rounds(pe, step)

        @block.scalar
        def _(act):
            def exp(i, r):
                wait(act, shifted, i, r, 1)
                nc.scalar.activation(score[r], score[r], ACT.Exp).then_inc(exp_ready, 1)

            def take_turned(i, r):
                wait(act, turned, i, r, 1)
                wait(act, out_ready, i, r, -1)
                at = (2 + 2 * (r % 2)) * BANK
                by_head = turned_sb[r % 2].rearrange("p (h n) -> p h n", h=HPC)
                nc.scalar.copy(by_head[:, :, 0:EASY],
                               m.ps[0:SEQ, at:at + 2 * P].rearrange("p (h n) -> p h n", h=HPC))
                for j, (h, n) in enumerate(HARD_HEADS):
                    o = at + (2 + j) * P
                    ins = nc.scalar.copy(by_head[:, h:h + n, EASY:SEQ],
                                         m.ps[0:SEQ, o:o + n * HARD].rearrange("p (h n) -> p h n", h=n))
                ins.then_inc(turned_taken, 1)

            def take_output(i, r):
                c = r % 2
                wait(act, out_ready, i, r, 1)
                nc.scalar.activation(att[:, c, batch(i, r)], m.bank(6 + c, SEQ), ACT.Identity,
                                     bias=v_bias(c)).then_inc(out_taken, 1)

            def step(i, r):
                if has(i, r, 1):
                    exp(*shifted_by(i, r, 1))
                if has(i, r, 0):
                    take_turned(i, r)
                if has(i, r, -1):
                    take_output(*shifted_by(i, r, -1))
            rounds(act, step)

        @block.vector
        def _(dve):
            divide_steps = 3 if topk else 2

            def shift(i, r):
                c = r % 2
                wait(dve, scores_ready, i, r, 1)
                wait(dve, turned, i, r, -3)
                s = tile3(score[r])
                nc.vector.tensor_tensor(score[r], m.ps[:, c * BANK:c * BANK + NQT * SEQ], mask,
                                        ALU.add).then_inc(scores_taken, 1)
                wait(dve, scores_taken, i, r, 1)
                high = row_max[r][:, 0:NQT]
                nc.vector.tensor_reduce(high, s, AX_X, ALU.max).then_inc(shift_step, 1)
                if topk:
                    nc.vector.tensor_copy(left[c], score[r][:, easy:])
                    nc.vector.drain()
                    for e in range(TOPK // 8):
                        for j in range(NHARD):
                            nc.vector.max(top8[c][:, j, e, :], left[c][:, j * SEQ:(j + 1) * SEQ])
                        nc.vector.drain()
                        for j in range(NHARD):
                            part = left[c][:, j * SEQ:(j + 1) * SEQ]
                            nc.vector.match_replace(part, top8[c][:, j, e, :], part, TAKEN)
                        nc.vector.drain()
                wait(dve, shift_step, i, r, 1)
                nc.vector.tensor_tensor(s, s, wide(high), ALU.subtract).then_inc(shifted, 1)

            def divide(i, r):
                link = linker(dve, divide_step, value(i, r) * divide_steps)
                wait(dve, exp_ready, i, r, 1)
                s = tile3(score[r])
                total = row_sum[r][:, 0:NQT]
                if topk:
                    hard = score[r][:, easy:]
                    link(nc.vector.scalar_tensor_tensor(out=hard, in0=left[r % 2], scalar=-1e35, in1=hard,
                                                        op0=ALU.is_lt, op1=ALU.mult))
                link(nc.vector.tensor_reduce(total, s, AX_X, ALU.add))
                link(nc.vector.reciprocal(total, total))
                nc.vector.tensor_tensor(s, s, wide(total), ALU.mult).then_inc(weights_ready, 1)

            def step(i, r):
                if has(i, r, 0):
                    divide(i, r)
                if has(i, r, 2):
                    shift(*shifted_by(i, r, 2))
            rounds(dve, step)


def project(nc, m, w_out, bias):
    linear(nc, m, full(m.s3), lambda k, j: w_out[:, k, j * P:j * P + P], KD, KD, CHUNKS, add_to(nc, m, m.h, bias),
           on="vector")


def queries_and_keys(nc, m, w_q, w_k, b_q, b_k, scale):
    def drain(j, o, n, acc, link):
        out = m.big1[:, j, o:o + n]
        if j < KD:
            return nc.vector.tensor_scalar(out, acc, b_q(j), scale, ALU.add, ALU.mult)
        return nc.vector.tensor_scalar(out, acc, b_k(j - KD), None, ALU.add)
    linear(nc, m, full(m.xn), lambda k, j: w_q(k, j) if j < KD else w_k(k, j - KD), KD, 2 * KD, CHUNKS, drain,
           on="vector")


def attention1(nc, m, d):
    w = m.wa[:, 0:KD * 3 * D].rearrange("p (k n) -> p k n", k=KD)
    w_o = m.wa[:, 1536:2048].rearrange("p (k n) -> p k n", k=KD)
    load(nc, (w, d["c_attn"]), (w_o, d["c_proj"]))
    layernorm(nc, m, full(m.h), full(m.xn), CHUNKS)
    queries_and_keys(nc, m, lambda k, j: w[:, k, j * P:j * P + P], lambda k, j: w[:, k, D + j * P:D + j * P + P],
                     lambda j: m.v("c_attn_b", j), lambda j: m.v("c_attn_b", 2 + j), HD ** -0.5)
    v = m.big1[:, :, :].rearrange("p a b -> p (a b)")[0:SEQ, 4 * N:4 * N + BATCH * D].rearrange(
        "p (b n) -> p b n", b=BATCH)
    value_rows(nc, m, lambda k: w[:, k, 2 * D:3 * D], v)
    attend(nc, m, d["mask1"], lambda c: m.v("c_attn_b", 4 + c), False)
    project(nc, m, w_o, lambda j: m.v("c_proj_b", j))


def load_qkvo(nc, m, d, of):
    w = [m.wa[:, i * 512:(i + 1) * 512].rearrange("p (k n) -> p k n", k=KD) for i in range(4)]
    load(nc, *[(w[i], d[of + name]) for i, name in enumerate(("Wq", "Wk", "Wv", "Wo"))])
    return w


def attention3(nc, m, d):
    w_q, w_k, w_v, w_o = load_qkvo(nc, m, d, "L3")
    layernorm(nc, m, full(m.h), full(m.xn), CHUNKS)
    queries_and_keys(nc, m, lambda k, j: w_q[:, k, j * P:j * P + P], lambda k, j: w_k[:, k, j * P:j * P + P],
                     lambda j: m.v("bq", j), lambda j: m.v("bk", j), HD ** -0.5)
    v = m.big1[:, :, :].rearrange("p a b -> p (a b)")[0:SEQ, 4 * N:4 * N + BATCH * D].rearrange(
        "p (b n) -> p b n", b=BATCH)
    value_rows(nc, m, lambda k: w_v[:, k, :], v)
    attend(nc, m, d["mask3"], lambda c: m.v("bv", c), True)
    project(nc, m, w_o, lambda j: m.v("bo", j))


def attention2(nc, m, d):
    w_q, w_k, w_v, w_o = load_qkvo(nc, m, d, "L2")
    layernorm(nc, m, full(m.h), full(m.xn), CHUNKS)
    queries_and_keys(nc, m, lambda k, j: w_q[:, k, j * P:j * P + P], lambda k, j: w_k[:, k, j * P:j * P + P],
                     lambda j: m.v("Wq_b", j), lambda j: m.v("Wk_b", j), D ** -0.5)
    flat1 = m.big1[:, :, :].rearrange("p a b -> p (a b)")
    v = flat1[0:SEQ, 4 * N:4 * N + BATCH * D].rearrange("p (b n) -> p b n", b=BATCH)
    value_rows(nc, m, lambda k: w_v[:, k, :], v)
    q, k = m.big1[:, 0:2, :], m.big1[:, 2:4, :]
    flat2 = m.big2[:, :, :].rearrange("p a b -> p (a b)")
    G = 4
    W = G * SEQ
    score = [flat2[0:SEQ, g * W:(g + 1) * W] for g in range(BATCH // G)]
    turned_sb = [flat2[0:SEQ, 1200 + g * W:1200 + (g + 1) * W] for g in range(BATCH // G)]
    mask = flat2[0:SEQ, 2400:2400 + SEQ]
    red = [flat2[0:SEQ, 2500 + 8 * g:2500 + 8 * g + G] for g in range(BATCH // G)]
    att = m.s3
    load(nc, (mask, d["mask2"]))
    with stage(nc, "scores_ready", "abs_ready", "step", "shifted", "exp_ready", "weights_ready", "turned",
               "turned_taken", "out_ready", "out_taken") as (
            block, scores_ready, abs_ready, step, shifted, exp_ready, weights_ready, turned, turned_taken, out_ready, out_taken):
        wide = lambda a: a.unsqueeze(2).broadcast_to([SEQ, G, SEQ])
        tiles = range(BATCH // G)

        @block.tensor
        def _(pe):
            for g in tiles:
                for i in range(G):
                    o = (g * G + i) * SEQ
                    for c in range(KD):
                        ins = nc.tensor.matmul(m.ps[0:SEQ, g * BANK + i * SEQ:g * BANK + (i + 1) * SEQ],
                                               q[:, c, o:o + SEQ], k[:, c, o:o + SEQ], start=c == 0, stop=c == KD - 1)
                ins.then_inc(scores_ready, 1)
            for g in tiles:
                pe.wait_ge(weights_ready, g + 1)
                if g >= 2:
                    pe.wait_ge(turned_taken, g - 1)
                b4 = 4 + g % 2
                for i in range(G):
                    ins = nc.tensor.transpose(m.ps[0:SEQ, b4 * BANK + i * SEQ:b4 * BANK + (i + 1) * SEQ],
                                              score[g][:, i * SEQ:(i + 1) * SEQ], m.ident[0:SEQ, 0:SEQ])
                ins.then_inc(turned, 1)
                pe.wait_ge(turned_taken, g + 1)
                if g >= 1:
                    pe.wait_ge(out_taken, 2 * g)
                for c in range(KD):
                    for i in range(G):
                        ins = nc.tensor.matmul(m.ps[:, (6 + c) * BANK + i * SEQ:(6 + c) * BANK + (i + 1) * SEQ],
                                               v[:, g * G + i, c * P:(c + 1) * P],
                                               turned_sb[g][:, i * SEQ:(i + 1) * SEQ], start=True, stop=True)
                    ins.then_inc(out_ready, 1)

        @block.scalar
        def _(act):
            for g in tiles:
                act.wait_ge(scores_ready, g + 1)
                nc.scalar.activation(score[g], m.bank(g, W, SEQ), ACT.Abs).then_inc(abs_ready, 1)
            for g in tiles:
                act.wait_ge(shifted, g + 1)
                nc.scalar.activation(score[g], score[g], ACT.Exp).then_inc(exp_ready, 1)
            for g in tiles:
                act.wait_ge(turned, g + 1)
                nc.scalar.copy(turned_sb[g], m.bank(4 + g % 2, W, SEQ)).then_inc(turned_taken, 1)
                for c in range(KD):
                    act.wait_ge(out_ready, 2 * g + c + 1)
                    nc.scalar.activation(att[:, c, g * W:(g + 1) * W], m.bank(6 + c, W), ACT.Identity,
                                         bias=m.v("Wv_b", c)).then_inc(out_taken, 1)

        @block.vector
        def _(dve):
            link = linker(dve, step)
            for g in tiles:
                dve.wait_ge(abs_ready, g + 1)
                s = score[g].rearrange("p (i n) -> p i n", i=G)
                link(nc.vector.tensor_tensor(s, s, mask.unsqueeze(1).broadcast_to([SEQ, G, SEQ]), ALU.add))
                link(nc.vector.tensor_reduce(red[g], s, AX_X, ALU.max))
                nc.vector.tensor_tensor(s, s, wide(red[g]), ALU.subtract).then_inc(shifted, 1)
            for g in tiles:
                dve.wait_ge(exp_ready, g + 1)
                s = score[g].rearrange("p (i n) -> p i n", i=G)
                link(nc.vector.tensor_reduce(red[g], s, AX_X, ALU.add))
                link(nc.vector.reciprocal(red[g], red[g]))
                nc.vector.tensor_tensor(s, s, wide(red[g]), ALU.mult).then_inc(weights_ready, 1)
    project(nc, m, w_o, lambda j: m.v("Wo_b", j))


def ternary(nc, m, w, tmp, scale, width):
    tiles = w.shape[1]
    wide = lambda a: a.unsqueeze(2).broadcast_to([P, tiles, width])
    inv = scale[:, tiles:2 * tiles]
    sc = scale[:, 0:tiles]
    with stage(nc, "step") as (block, step):
        @block.vector
        def _(dve):
            link = linker(dve, step)
            link(nc.vector.tensor_reduce(sc, w, AX_X, ALU.add, apply_absolute_value=True))
            link(nc.vector.tensor_scalar(sc, sc, 1.0 / width, 1e-5, ALU.mult, ALU.max))
            link(nc.vector.reciprocal(inv, sc))
            link(nc.vector.tensor_tensor(tmp, w, wide(inv), ALU.mult))
            link(nc.vector.tensor_scalar(tmp, tmp, MAGIC, -MAGIC, ALU.add, ALU.add))
            link(nc.vector.tensor_scalar(tmp, tmp, -1.0, 1.0, ALU.max, ALU.min))
            link(nc.vector.tensor_tensor(tmp, tmp, w, ALU.subtract))
            link(nc.vector.tensor_tensor(tmp, w, tmp, ALU.add))
            link(nc.vector.tensor_tensor(tmp, tmp, wide(sc), ALU.mult))


def mlp(nc, m, x, w1, w2, activate, add):
    linear(nc, m, full(x), lambda k, j: w1[:, k, j * P:j * P + P], KD, 8, CHUNKS, activate)
    linear(nc, m, full(m.big2), lambda k, j: w2[:, k, j * P:j * P + P], 8, KD, CHUNKS, add, on="vector")


def ternary_mlp(nc, m, d):
    flat1 = m.big1[:, :, :].rearrange("p a b -> p (a b)")
    fc = flat1[:, 0:2048].rearrange("p (k n) -> p k n", k=8)
    proj = flat1[:, 2048:4096].rearrange("p (k n) -> p k n", k=2)
    tmp_fc = flat1[:, 4096:6144].rearrange("p (k n) -> p k n", k=8)
    tmp_proj = flat1[:, 6144:8192].rearrange("p (k n) -> p k n", k=2)
    fast_b, u, v = flat1[0:16, 8192:8208], m.s1[0:16, 0, 0:FF], flat1[0:16, 8208:8464]
    mid = m.s1[0:16, 1, 0:FF]
    scale_fc, scale_proj = flat1[:, 8500:8516], flat1[:, 8520:8524]
    w1 = m.wa[:, 0:2048].rearrange("p (k n) -> p k n", k=KD)
    w2 = m.wa[:, 2048:4096].rearrange("p (k n) -> p k n", k=8)
    load(nc, (fc, d["w_fc"]), (proj, d["w_proj"]), (fast_b, d["fast_b"]), (u, d["uT"]), (v, d["v"]))
    ternary(nc, m, fc, tmp_fc, scale_fc, D)
    ternary(nc, m, proj, tmp_proj, scale_proj, FF)
    with stage(nc, "mid_ready", "mid_taken", "turned", "turned_taken") as (
            block, mid_ready, mid_taken, turned, turned_taken):

        @block.tensor
        def _(pe):
            for c in range(2):
                nc.tensor.matmul(m.bank(c, BANK, 16), fast_b, u[:, c * BANK:(c + 1) * BANK], start=True,
                                 stop=True).then_inc(mid_ready, 1)
            pe.wait_ge(mid_taken, 2)
            for k in range(KD):
                for c in range(2):
                    b = 2 + 2 * k + c
                    for i in range(4):
                        j = 4 * c + i
                        to = m.ps[:, b * BANK + i * P:b * BANK + (i + 1) * P]
                        nc.tensor.matmul(to, tmp_fc[:, j, k * P:(k + 1) * P], m.ident[:, :], start=True, stop=False)
                        ins = nc.tensor.matmul(to, v[:, k * P:(k + 1) * P], mid[:, j * P:(j + 1) * P], start=False,
                                               stop=True)
                    ins.then_inc(turned, 1)
            for g in range(4):
                b = 2 + g
                pe.wait_ge(turned_taken, g + 1)
                for i in range(2):
                    for j in range(2):
                        k = 2 * g + i
                        to = m.ps[:, b * BANK + (2 * i + j) * P:b * BANK + (2 * i + j + 1) * P]
                        ins = nc.tensor.transpose(to, tmp_proj[:, j, k * P:(k + 1) * P], m.ident[:, :])
                ins.then_inc(turned, 1)

        @block.vector
        def _(dve):
            for c in range(2):
                dve.wait_ge(mid_ready, c + 1)
                nc.vector.tensor_scalar(mid[:, c * BANK:(c + 1) * BANK], m.bank(c, BANK, 16),
                                        m.vec[0:16, VEC["gate"][0]:VEC["gate"][0] + 1], None,
                                        ALU.mult).then_inc(mid_taken, 1)
            for g in range(4):
                dve.wait_ge(turned, g + 1)
                k, c = divmod(g, 2)
                nc.vector.tensor_copy(w1[:, k, c * BANK:(c + 1) * BANK], m.bank(2 + g)).then_inc(turned_taken, 1)
            for g in range(4):
                dve.wait_ge(turned, 5 + g)
                nc.vector.tensor_copy(w2[:, 2 * g:2 * g + 2, :].rearrange("p k n -> p (k n)"), m.bank(2 + g))
    layernorm(nc, m, full(m.h), full(m.xn), CHUNKS)

    def relu_squared(j, o, n, acc, link):
        out = m.big2[:, j, o:o + n]
        link(nc.scalar.activation(out, acc, ACT.Relu))
        return nc.scalar.activation(out, out, ACT.Square)
    mlp(nc, m, m.xn, w1, w2, relu_squared, add_to(nc, m, m.h))


def dequantised_mlp(nc, m, d):
    flat1 = m.big1[:, :, :].rearrange("p a b -> p (a b)")
    raw = [flat1[:, i * 2048:(i + 1) * 2048] for i in range(4)]
    w1, w2 = m.wa[:, 0:2048], m.wa[:, 2048:4096]
    load(nc, (raw[0].bitcast(I32), d["fc1_q"]), (raw[1].bitcast(I32), d["fc2_q"]),
         (raw[2].rearrange("p (k n) -> p k n", k=KD), d["fc1_s"].unsqueeze(0).broadcast_to([P, KD, FF])),
         (raw[3].rearrange("p (k n) -> p k n", k=8), d["fc2_s"].unsqueeze(0).broadcast_to([P, 8, D])))
    with stage(nc, "half_bias") as (block, half_bias):
        @block.vector
        def _(dve):
            for w, q, s in ((w1, raw[0], raw[2]), (w2, raw[1], raw[3])):
                nc.vector.scalar_tensor_tensor(out=w, in0=q.bitcast(I32), scalar=-128.0, in1=s, op0=ALU.add,
                                               op1=ALU.mult)
    w1 = w1.rearrange("p (k n) -> p k n", k=KD)
    w2 = w2.rearrange("p (k n) -> p k n", k=8)
    layernorm(nc, m, full(m.h), full(m.xn), CHUNKS)
    layernorm(nc, m, full(m.xn), full(m.s3), CHUNKS, lambda k: m.v("gamma", k), lambda k: m.v("beta", k))

    def half(j, o, n, acc, link):
        out, t = m.h[:, j, o:o + n], m.s1[:, j, o:o + n]
        link(nc.vector.tensor_tensor(out, out, m.xn[:, j, o:o + n], ALU.add))
        link(nc.vector.tensor_scalar(t, acc, m.v("fc2_b", j), 0.5, ALU.add, ALU.mult))
        return nc.vector.tensor_tensor(out, out, t, ALU.add)
    mlp(nc, m, m.s3, w1, w2, lambda j, o, n, acc, link: nc.scalar.activation(
        m.big2[:, j, o:o + n], acc, ACT.Silu, bias=m.v("fc1_b", j)), half)


def mixture3(nc, m, d):
    w3 = m.small[:, 1200:1216].rearrange("p (k n) -> p k n", k=KD)
    w1 = m.wa[:, 0:4096].rearrange("p (k n) -> p k n", k=KD)
    w2 = m.wa[:, 4096:8192].rearrange("p (k n) -> p k n", k=16)
    load(nc, (w3, d["router3"]), (w1, d["mw1"]), (w2, d["mw2"]))
    layernorm(nc, m, full(m.h), full(m.xn), CHUNKS)
    route(nc, m, 1, E3, w3, True)
    flat1 = m.big1[:, :, :].rearrange("p a b -> p (a b)")
    nf = 16
    units = [(c, f) for c in range(NCH) for f in range(nf)]
    squared = [flat1[:, i * CW:(i + 1) * CW] for i in range(2)]
    hidden = [flat1[:, (2 + i) * CW:(3 + i) * CW] for i in range(2)]
    with stage(nc, "up_ready", "spread", "relu_ready", "square_ready", "hidden_ready", "down_ready", "sum_taken") as (
            block, up_ready, spread, relu_ready, square_ready, hidden_ready, down_ready, sum_taken):

        @block.tensor
        def _(pe):
            def up(u):
                c, f = units[u]
                o = c * CW
                if u >= 2:
                    pe.wait_ge(hidden_ready, u - 1)
                if f % 2 == 0:
                    nc.tensor.matmul(m.bank(2 + (f // 2) % 2, CW), m.pick[:, (f // 2) * P:(f // 2 + 1) * P],
                                     m.parts[:, 0, o:o + CW], start=True, stop=True).then_inc(spread, 1)
                for k in range(KD):
                    ins = nc.tensor.matmul(m.bank(u % 2, CW), w1[:, k, f * P:(f + 1) * P], m.xn[:, k, o:o + CW],
                                           start=k == 0, stop=k == KD - 1)
                ins.then_inc(up_ready, 1)

            up(0)
            for u, (c, f) in enumerate(units):
                if u + 1 < len(units):
                    up(u + 1)
                pe.wait_ge(hidden_ready, u + 1)
                if f == 0 and c >= 2:
                    pe.wait_ge(sum_taken, KD * (c - 1))
                for j in range(KD):
                    ins = nc.tensor.matmul(m.bank(4 + 2 * (c % 2) + j, CW), w2[:, f, j * P:(j + 1) * P],
                                           hidden[u % 2], start=f == 0, stop=f == nf - 1)
                if f == nf - 1:
                    ins.then_inc(down_ready, 1)

        @block.scalar
        def _(act):
            for u in range(len(units)):
                act.wait_ge(up_ready, u + 1)
                if u >= 2:
                    act.wait_ge(hidden_ready, u - 1)
                nc.scalar.activation(squared[u % 2], m.bank(u % 2, CW), ACT.Relu).then_inc(relu_ready, 1)
                act.wait_ge(relu_ready, u + 1)
                nc.scalar.activation(squared[u % 2], squared[u % 2], ACT.Square).then_inc(square_ready, 1)

        @block.vector
        def _(dve):
            for u, (c, f) in enumerate(units):
                dve.wait_ge(square_ready, u + 1)
                dve.wait_ge(spread, u // 2 + 1)
                nc.vector.tensor_tensor(hidden[u % 2], squared[u % 2], m.bank(2 + (f // 2) % 2, CW),
                                        ALU.mult).then_inc(hidden_ready, 1)
                if f == nf - 1:
                    dve.wait_ge(down_ready, c + 1)
                    for j in range(KD):
                        out = m.h[:, j, c * CW:(c + 1) * CW]
                        nc.vector.tensor_tensor(out, out, m.bank(4 + 2 * (c % 2) + j, CW),
                                                ALU.add).then_inc(sum_taken, 1)


def cols(a, n):
    return np.ascontiguousarray(np.reshape(a, (n, P)).T)


def rows_to_partitions(w):
    k = w.shape[-2] // P
    return np.ascontiguousarray(np.moveaxis(w.reshape(w.shape[:-2] + (k, P, w.shape[-1])), -3, -2)).reshape(
        w.shape[:-2] + (P, -1))


def lay_out(i):
    f = np.float32
    t = lambda name: np.asarray(i[name])
    d = {}
    x = t("x").reshape(BATCH, 3, 6, 16, 6, 16).transpose(1, 3, 5, 0, 2, 4).reshape(768, BATCH * PATCHES)
    d["patches"] = rows_to_partitions(x)
    d["tok_w"] = rows_to_partitions(t("L0_tok_W").T)
    d["tok_pos"] = rows_to_partitions(t("L0_tok_pos_embedding")[0].T)
    d["tokens"] = np.ascontiguousarray(t("x_txt").reshape(4, P).T)
    d["emb"] = t("L0_txt_emb")
    d["txt_pos"] = rows_to_partitions(t("L0_txt_pos_emb")[:TEXT].T)
    fresh = np.ones((STATE, BATCH, TEXT), f)
    fresh[:, :, 0] = 0
    d["fresh"] = fresh.reshape(STATE, -1)
    d["B"] = rows_to_partitions(t("L0_txt_B"))
    d["C"] = t("L0_txt_C")
    d["Dw"] = rows_to_partitions(t("L0_txt_D"))
    d["w1"] = rows_to_partitions(t("L0_txt_w1"))
    d["w2"] = rows_to_partitions(t("L0_txt_w2"))
    lvec = np.zeros((LAYERS, P, NLVEC), f)
    for l in range(LAYERS):
        for name in ("ln1_s", "ln1_b", "ln2_s", "ln2_b", "b2"):
            lvec[l][:, LVEC[name]:LVEC[name] + 2] = cols(t("L0_txt_" + name)[l], 2)
        lvec[l][:, LVEC["b1"]:LVEC["b1"] + 8] = cols(t("L0_txt_b1")[l], 8)
        lvec[l][:STATE, LVEC["A"]] = t("L0_txt_A_diag")[l]
    d["lvec"] = lvec
    vec = np.zeros((P, NVEC), f)

    def put(name, a):
        c, n = VEC[name]
        vec[:, c:c + n] = a

    names = {
        "tok_b": "L0_tok_b", "cls": "L0_tok_cls_token", "lnf_s": "L0_txt_lnf_s", "lnf_b": "L0_txt_lnf_b",
        "norm_w": "L0_attn_norm_w", "norm_b": "L0_attn_norm_b", "conv_b": "L0_attn_conv_b", "dt_w": "L0_attn_dt_w",
        "dt_b": "L0_attn_dt_b", "D_skip": "L0_attn_D_skip", "c_attn_b": "L1_attn_c_attn_b",
        "c_proj_b": "L1_attn_c_proj_b", "Wq_b": "L2_attn_Wq_b", "Wk_b": "L2_attn_Wk_b", "Wv_b": "L2_attn_Wv_b",
        "Wo_b": "L2_attn_Wo_b", "gamma": "L2_ffn_ln_gamma", "beta": "L2_ffn_ln_beta", "fc1_b": "L2_ffn_fc1_bias",
        "fc2_b": "L2_ffn_fc2_bias", "bq": "L3_attn_bq", "bk": "L3_attn_bk", "bv": "L3_attn_bv", "bo": "L3_attn_bo"}
    for short, name in names.items():
        put(short, cols(t(name), VEC[short][1]))
    put("gate", np.broadcast_to(t("L1_ffn_gate"), (P, 1)))
    put("conv_w", t("L0_attn_conv_w").reshape(4, P, 4).transpose(1, 0, 2).reshape(P, 16))
    put("A_log", t("L0_attn_A_log").reshape(4, P, DS).transpose(1, 0, 2).reshape(P, 4 * DS))
    d["vec"] = vec
    d["ident"] = np.eye(P, dtype=f)

    d["in_proj"] = rows_to_partitions(t("L0_attn_in_proj_w").T)
    xp = t("L0_attn_x_proj_w")
    d["dt_rows"] = rows_to_partitions(np.broadcast_to(xp[0:1].T, (DI, P)))
    d["bc_rows"] = rows_to_partitions(np.concatenate([xp[1:].T] * 3 + [np.zeros((DI, 32), f)], axis=1))
    d["out_proj"] = rows_to_partitions(t("L0_attn_out_proj_w").T)
    pick = np.zeros((P, 32, P), np.float32)
    for part in range(3):
        for e in range(32):
            pick[32 * part + e, e, :] = 1
    d["pick"] = pick.reshape(P, -1)

    d["router"] = rows_to_partitions(np.concatenate([t("L0_ffn_router_w0"), t("L0_ffn_router_w1")], axis=1))
    experts = [np.concatenate([rows_to_partitions(t("L0_ffn_wg%d" % g)), rows_to_partitions(t("L0_ffn_wu%d" % g)),
                               t("L0_ffn_wd%d" % g)], axis=2) for g in range(2)]
    d["experts"] = np.concatenate(experts, axis=0)
    rc = np.zeros((P, ROUTE_CONSTS), f)
    rc[:ROWT, 0:ROWT] = np.triu(np.ones((ROWT, ROWT), f), 1)
    rc[:, 96:224] = 1
    rc[:, 224:352] = np.arange(P)
    rc[:, 352:364] = np.arange(NROWT)[None, :] * ROWT + np.arange(P)[:, None]
    rc[:, 364] = np.arange(P)
    d["route_consts"] = rc
    order = np.tile(np.arange(E0, 0, -1, dtype=f), (ROWT, 1))
    d["order"] = order

    d["c_attn"] = rows_to_partitions(t("L1_attn_c_attn_w"))
    d["c_proj"] = rows_to_partitions(t("L1_attn_c_proj_w"))
    for name in ("Wq", "Wk", "Wv", "Wo"):
        d["L2" + name] = rows_to_partitions(t("L2_attn_%s_w" % name).T)
        d["L3" + name] = rows_to_partitions(t("L3_attn_%s" % name).T)
    query = np.concatenate([np.tile(np.arange(EASY), HPC), np.tile(np.arange(EASY, SEQ), HPC),
                            np.full(P, SEQ - 1)])
    query = np.stack([query[a:a + P] for a in QAT], axis=1)
    key = np.arange(SEQ)
    late = key > query[:, :, None]
    twice = np.zeros(SEQ, f)
    twice[7:64:8] = np.log(2.0)
    d["mask1"] = (np.where(late, np.float32(-10000.0), np.float32(0)) + twice).reshape(P, -1).astype(f)
    d["mask3"] = np.where(late, NEG, 0.0).reshape(P, -1).astype(f)
    d["mask2"] = np.where(key[None, :] > key[:, None], NEG, 0.0).astype(f)
    d["head_of"] = np.repeat(np.eye(HPC, dtype=f), HD, axis=0)

    d["w_fc"] = rows_to_partitions(t("L1_ffn_w_fc"))
    d["w_proj"] = rows_to_partitions(t("L1_ffn_w_proj"))
    d["fast_b"] = t("L1_ffn_fast_b")
    d["uT"] = np.ascontiguousarray(t("L1_ffn_u").T)
    d["v"] = t("L1_ffn_v")
    d["fc1_q"] = rows_to_partitions(t("L2_ffn_fc1_q"))
    d["fc2_q"] = rows_to_partitions(t("L2_ffn_fc2_q"))
    d["fc1_s"] = t("L2_ffn_fc1_scales")
    d["fc2_s"] = t("L2_ffn_fc2_scales")
    d["router3"] = rows_to_partitions(t("L3_ffn_router_w").T)
    d["mw1"] = rows_to_partitions(t("L3_ffn_w1"))
    d["mw2"] = rows_to_partitions(t("L3_ffn_w2"))
    return d


def store(nc, m, out):
    with stage(nc, "stored") as (block, stored):

        @block.sync
        def _(sp):
            sp.dma_start(out, m.h[:, :, :].rearrange("p k n -> p (k n)")).then_inc(stored, 16)
            sp.wait_ge(stored, 16)


STAGES = ["patch_tokens", "text_encoder", "selective_scan", "mixture0", "attention1", "ternary_mlp", "attention2",
          "dequantised_mlp", "attention3", "mixture3"]


def build(nc, d, out):
    m = Mem(nc, d)
    setup(nc, m, d)
    patch_tokens(nc, m, d)
    text_encoder(nc, m, d)
    clear_results(nc, m)
    selective_scan(nc, m, d)
    mixture0(nc, m, d)
    attention1(nc, m, d)
    ternary_mlp(nc, m, d)
    attention2(nc, m, d)
    dequantised_mlp(nc, m, d)
    attention3(nc, m, d)
    mixture3(nc, m, d)
    store(nc, m, out)


def kernel(**inputs):
    import concourse.bacc as bacc
    from concourse.bass_utils import run_bass_kernel_spmd

    arrays = lay_out(inputs)
    nc = bacc.Bacc("TRN2", target_bir_lowering=False, num_devices=1)
    d = {name: nc.dram_tensor("in_" + name, a.shape, mybir.dt.from_np(a.dtype), kind="ExternalInput").ap()
         for name, a in arrays.items()}
    out = nc.dram_tensor("out", (P, KD * N), F32, kind="ExternalOutput").ap()
    build(nc, d, out)
    r = run_bass_kernel_spmd(nc, [{"in_" + k: a for k, a in arrays.items()}], core_ids=[0])
    got = np.asarray(r.results[0]["out"]).reshape(P, KD, BATCH, SEQ)
    return np.ascontiguousarray(got.transpose(2, 3, 1, 0)).reshape(BATCH, SEQ, D)
```

```python
from contextlib import ExitStack, contextmanager

import numpy as np

import concourse.bass as bass
from concourse import mybir

ALU = mybir.AluOpType
ACT = mybir.ActivationFunctionType
F32 = mybir.dt.float32
BF16 = mybir.dt.bfloat16
I32 = mybir.dt.int32
AX_X = mybir.AxisListType.X

P = 128
D = 256
KD = D // P
BATCH = 16
PATCHES = 36
TEXT = 32
SEQ = 1 + PATCHES + TEXT
N = BATCH * SEQ
NCH = 3
CW = N // NCH
CHUNKS = [(c * CW, CW) for c in range(NCH)]
BANK = 512
VOCAB = 8000
LAYERS = 4
STATE = 64
FF = 1024
DI = 512
DS = 16
HEADS = 16
HD = D // HEADS
HPC = P // HD
EASY, HARD = 32, SEQ - 32
HARD_HEADS = [(0, 3), (3, 3), (6, 2)]
NHARD = len(HARD_HEADS)
NQT = 2 + NHARD
QAT = [0, P] + [HPC * EASY + h * HARD for h, _ in HARD_HEADS]
QSET = QAT[-1] + P
EPS = 1e-5
NEG = -1e30
TAKEN = -3e38
GATHER_SEM = 109
SEMS = 24
SEM0 = 110
TOPK = 32
ROWT = 92
NROWT = N // ROWT
MAX_BLOCKS = 98
MAX_ROUNDS = 25
TABLE = 4 * (MAX_ROUNDS + 1)
LANDED = ("patches", "text_input", "state_mix", "up", "down", "layer_vectors", "pick", "masks", "scan", "attention1",
          "ternary", "attention2", "dequantised", "attention3", "mixture3")
E0, E3 = 32, 8

ROUTE_AT = {"tri": (0, ROWT, ROWT), "ones": (96, P, P), "iota": (224, P, ROWT), "token": (352, NROWT, ROWT),
            "place": (364, 1, P)}
ROUTE_CONSTS = 365
VEC = {}
for _name, _n in (
    ("tok_b", 2), ("cls", 2), ("lnf_s", 2), ("lnf_b", 2), ("norm_w", 2), ("norm_b", 2), ("conv_b", 4),
    ("dt_w", 4), ("dt_b", 4), ("D_skip", 4), ("conv_w", 16), ("A_log", 64), ("c_attn_b", 6), ("c_proj_b", 2),
    ("gate", 1), ("Wq_b", 2), ("Wk_b", 2), ("Wv_b", 2), ("Wo_b", 2), ("gamma", 2), ("beta", 2), ("fc1_b", 8),
    ("fc2_b", 2), ("bq", 2), ("bk", 2), ("bv", 2), ("bo", 2),
):
    VEC[_name] = (sum(n for _, n in VEC.values()), _n)
NVEC = sum(n for _, n in VEC.values())
LVEC = {"ln1_s": 0, "ln1_b": 2, "ln2_s": 4, "ln2_b": 6, "b1": 8, "b2": 16, "A": 18}
NLVEC = 19


class Turn:
    now = 0


@contextmanager
def stage(nc, *names):
    base, other = SEM0 + SEMS * Turn.now, SEM0 + SEMS * (1 - Turn.now)
    Turn.now = 1 - Turn.now
    with ExitStack() as held:
        sems = [held.enter_context(nc.semaphore(name=n, num=base + i)) for i, n in enumerate(names)]
        with nc.Block() as block:
            nc.gpsimd.sem_clear(range(other, other + SEMS))
            yield (block, *sems)


def linker(eng, sem, start=0):
    count = [0]

    def link(ins):
        count[0] += 1
        ins.then_inc(sem, 1)
        eng.wait_ge(sem, start + count[0])

    return link


class Mem:

    def __init__(self, nc):
        sb = lambda name, shape, dt=F32: nc.alloc_sbuf_tensor(name, shape, dt)
        self.h = sb("h", [P, KD, N])
        self.xn = sb("xn", [P, KD, N])
        self.s1 = sb("s1", [P, KD, N])
        self.s2 = sb("s2", [P, KD, N])
        self.s3 = sb("s3", [P, KD, N])
        self.big1 = sb("big1", [P, 8, N])
        self.big2 = sb("big2", [P, 8, N])
        self.wa = sb("wa", [P, 8192])
        self.wb = sb("wb", [P, 6144])
        self.routers = sb("routers", [P, KD * (2 * E0 + E3)])
        self.mask1 = sb("mask1", [P, NQT * SEQ])
        self.mask2 = sb("mask2", [SEQ, SEQ])
        self.mask3 = sb("mask3", [P, NQT * SEQ])
        self.head_of = sb("head_of", [P, HPC])
        self.vec = sb("vec", [P, NVEC])
        self.lvec = sb("lvec", [P, NLVEC])
        self.mean_w = sb("mean_w", [P, P])
        self.ones = sb("ones", [P, P])
        self.ident = sb("ident", [P, P])
        self.small = sb("small", [P, 2048])
        self.parts = sb("parts", [P, 2, N], BF16)
        self.pick = sb("pick", [P, 32 * P], BF16)
        self.ident_bf = sb("ident_bf", [P, P], BF16)
        self.order = sb("order", [ROWT, E0])
        self.idx = sb("idx", [P, 4], I32)
        self.ps = nc.alloc_psum_tensor("ps", [P, 8 * BANK], F32)

        self.ps_bf = self.ps[:, :].bitcast(BF16)
        self.landed = {name: nc.alloc_semaphore("landed_" + name, num=GATHER_SEM + 86 + i)
                       for i, name in enumerate(LANDED)}

    def v(self, name, k=0):
        c = VEC[name][0] + k
        return self.vec[:, c:c + 1]

    def bank(self, b, n=BANK, rows=P):
        return self.ps[0:rows, b * BANK:b * BANK + n]


def fetch(sp, m, name, *pairs):
    for dst, src in pairs:
        sp.dma_start(dst, src).then_inc(m.landed[name], 16)


class Products:

    def __init__(self, w, n_out, drain, landed, on="scalar", hidden=None, second_w=None, second_drain=None,
                 second_landed=None, behind=None, beside=None):
        self.w, self.n_out, self.drain, self.landed, self.on = w, n_out, drain, landed, on
        self.hidden, self.second_w, self.second_drain = hidden, second_w, second_drain
        self.second_landed, self.behind, self.beside = second_landed, behind, beside


def keep_warm(nc, m, bank, products):
    for _ in range(products):
        nc.tensor.matmul(m.bank(bank), m.ident_bf[:, :], m.pick[:, 0:BANK], start=True, stop=True)


def layernorm(nc, m, src, dst, chunks, gamma=None, beta=None, fold=None, work=None, ahead=None, vectors=None,
              then=None, behind=None):
    cen, sq = work or (m.s1, m.s2)
    tiles = 4
    width = chunks[0][1] // tiles
    n_ch = len(chunks)
    std = m.small[0:width, 0:tiles * n_ch]
    inv = m.small[0:width, 16:16 + tiles * n_ch]
    diag = [m.small[0:width, 32 + i * width:32 + (i + 1) * width] for i in range(2 * tiles)]
    var = [m.ps[0:width, b * BANK:b * BANK + tiles] for b in (6, 7, 0)]
    last = n_ch - 1
    RING = (1, 2, 6, 7)
    PAIRS = ((3, 4), (5, 0), (3, 4))
    with stage(nc, "mean_ready", "centred", "squared", "squared_last", "var_ready", "std_ready", "inv_ready",
               "diag_ready", "rstd_ready", "scaled", "normed", "product_ready", "product_taken", "drain_step",
               "second_ready", "second_taken", "second_step", *(behind[0] if behind else ())) as (
            block, mean_ready, centred, squared, squared_last, var_ready, std_ready, inv_ready, diag_ready,
            rstd_ready, scaled, normed, product_ready, product_taken, drain_step, second_ready, second_taken,
            second_step, *behind_sems):

        def products(pe):
            def first(c):
                o, n = chunks[c]
                pe.wait_ge(normed, KD * (c + 1))
                for j in range(then.n_out):
                    g = c * then.n_out + j
                    if g >= 4:
                        pe.wait_ge(product_taken, g - 3)
                    for k in range(KD):
                        ins = nc.tensor.matmul(m.bank(RING[g % 4], n), then.w(k, j), dst(k, o, n), start=k == 0,
                                               stop=k == KD - 1)
                    ins.then_inc(product_ready, 1)

            def second(c):
                o, n = chunks[c]
                pe.wait_ge(product_taken, then.n_out * (c + 1))
                if c >= 2:
                    pe.wait_ge(second_taken, KD * (c - 1))
                for j in range(KD):
                    for k in range(then.n_out):
                        ins = nc.tensor.matmul(m.bank(PAIRS[c][j], n), then.second_w(k, j),
                                               then.hidden[:, k, o:o + n], start=k == 0, stop=k == then.n_out - 1)
                    ins.then_inc(second_ready, 1)

            keep_warm(nc, m, 0, 5)
            pe.wait_ge(*then.landed)
            if not then.second_w:
                for c in range(n_ch):
                    first(c)
                return
            first(0)
            pe.wait_ge(*then.second_landed)
            for c in range(1, n_ch):
                first(c)
                second(c - 1)
            second(last)

        @block.tensor
        def _(pe):
            def mean(c):
                o, n = chunks[c]
                for k in range(KD):
                    ins = nc.tensor.matmul(m.bank(c, n), m.mean_w[:, :], src(k, o, n), start=k == 0, stop=k == KD - 1)
                ins.then_inc(mean_ready, 1)

            def variance(c):
                o, n = chunks[c]
                pe.wait_ge(squared, min(KD * (c + 1), KD * n_ch - 1))
                if c == last:
                    pe.wait_ge(squared_last, 1)
                for t in range(tiles):
                    for k in range(KD):
                        ins = nc.tensor.matmul(var[c][:, t:t + 1], sq[:, k, o + t * width:o + (t + 1) * width],
                                               m.mean_w[:, 0:1], start=k == 0, stop=k == KD - 1)
                ins.then_inc(var_ready, 1)

            def spread(c):
                for t in range(tiles):
                    pe.wait_ge(diag_ready, tiles * c + t + 1)
                    ins = nc.tensor.matmul(m.ps[:, (3 + c) * BANK + t * width:(3 + c) * BANK + (t + 1) * width],
                                           m.ones[0:width, :], diag[(c % 2) * tiles + t], start=True, stop=True)
                    ins.then_inc(rstd_ready, 1)

            for c in range(n_ch):
                mean(c)
            for c in range(n_ch):
                keep_warm(nc, m, 5, 2 if c else 7)
                variance(c)
                if c:
                    keep_warm(nc, m, 5, 2)
                    spread(c - 1)
            keep_warm(nc, m, 5, 2)
            spread(last)
            if then:
                products(pe)
            if behind:
                behind[1](pe, normed, *behind_sems)

        if ahead or (then and then.behind):
            @block.sync
            def _(sp):
                if ahead:
                    ahead(sp)
                if then and then.behind:
                    sp.wait_ge(product_ready, then.n_out * n_ch)
                    then.behind(sp)

        def take_first(eng):
            link = linker(eng, drain_step)
            for c, (o, n) in enumerate(chunks):
                for j in range(then.n_out):
                    g = c * then.n_out + j
                    eng.wait_ge(product_ready, g + 1)
                    then.drain(j, o, n, m.bank(RING[g % 4], n), link).then_inc(product_taken, 1)

        @block.gpsimd
        def _(pool):
            for c, (o, n) in enumerate(chunks):
                for k in range(KD):
                    if (c, k) != (last, KD - 1):
                        pool.wait_ge(centred, KD * c + k + 1)
                        at = cen[:, k, o:o + n]
                        nc.gpsimd.tensor_tensor(sq[:, k, o:o + n], at, at, ALU.mult).then_inc(squared, 1)

        @block.scalar
        def _(act):
            for c in range(n_ch):
                act.wait_ge(var_ready, c + 1)
                nc.scalar.activation(std[:, c * tiles:(c + 1) * tiles], var[c], ACT.Sqrt,
                                     bias=m.eps[0:width, 0:1]).then_inc(std_ready, 1)
            if vectors:
                act.wait_ge(*vectors)
            for c, (o, n) in enumerate(chunks if gamma else ()):
                for k in range(KD):
                    act.wait_ge(scaled, KD * c + k + 1)
                    a, out = cen[:, k, o:o + n], dst(k, o, n)
                    if fold:
                        a = a.rearrange("p (b t) -> p b t", t=fold)
                    nc.scalar.activation(out, a, ACT.Identity, scale=gamma(k), bias=beta(k)).then_inc(normed, 1)
            if then and then.on == "scalar":
                take_first(act)
            if behind and behind[2]:
                behind[2](act, normed, *behind_sems)

        @block.vector
        def _(dve):
            def centre(c):
                o, n = chunks[c]
                dve.wait_ge(mean_ready, c + 1)
                for k in range(KD):
                    nc.vector.tensor_tensor(cen[:, k, o:o + n], src(k, o, n), m.bank(c, n),
                                            ALU.subtract).then_inc(centred, 1)

            def square_last():
                o, n = chunks[last]
                at = cen[:, KD - 1, o:o + n]
                dve.wait_ge(centred, KD * n_ch)
                nc.vector.tensor_tensor(sq[:, KD - 1, o:o + n], at, at, ALU.mult).then_inc(squared_last, 1)

            def invert(c):
                dve.wait_ge(std_ready, c + 1)
                at = slice(c * tiles, (c + 1) * tiles)
                nc.vector.reciprocal(inv[:, at], std[:, at]).then_inc(inv_ready, 1)
                dve.wait_ge(inv_ready, c + 1)
                for t in range(tiles):
                    if c >= 2:
                        dve.wait_ge(rstd_ready, tiles * (c - 2) + t + 1)
                    nc.vector.tensor_scalar(diag[(c % 2) * tiles + t], m.ident[0:width, 0:width],
                                            inv[:, c * tiles + t:c * tiles + t + 1], None,
                                            ALU.mult).then_inc(diag_ready, 1)

            def scale(c):
                o, n = chunks[c]
                dve.wait_ge(rstd_ready, tiles * (c + 1))
                for k in range(KD):
                    a, out = cen[:, k, o:o + n], dst(k, o, n)
                    ins = nc.vector.tensor_tensor(out if gamma is None else a, a, m.bank(3 + c, n), ALU.mult)
                    ins.then_inc(scaled if gamma else normed, 1)

            for c in range(n_ch):
                centre(c)
            square_last()
            for c in range(n_ch):
                invert(c)
                if c:
                    scale(c - 1)
            scale(last)
            if then and then.on == "vector":
                take_first(dve)
            if then and then.beside:
                dve.wait_ge(*then.beside[0])
                then.beside[1]()
            if behind and behind[3]:
                behind[3](dve, normed, *behind_sems)
            if then and then.second_w:
                link = linker(dve, second_step)
                for c, (o, n) in enumerate(chunks):
                    for j in range(KD):
                        dve.wait_ge(second_ready, KD * c + j + 1)
                        then.second_drain(j, o, n, m.bank(PAIRS[c][j], n), link).then_inc(second_taken, 1)


def linear(nc, m, src, w, n_in, n_out, chunks, drain, on="scalar", rows=P, weights=None, ahead=None):
    with stage(nc, "product_ready", "product_taken", "drain_step") as (block, product_ready, product_taken, drain_step):

        if ahead:
            @block.sync
            def _(sp):
                ahead(sp)

        @block.tensor
        def _(pe):
            if weights:
                pe.wait_ge(*weights)
            g = 0
            for j in range(n_out):
                for o, n in chunks:
                    if g >= 8:
                        pe.wait_ge(product_taken, g - 7)
                    for k in range(n_in):
                        ins = nc.tensor.matmul(m.bank(g % 8, n, rows), w(k, j), src(k, o, n), start=k == 0,
                                               stop=k == n_in - 1)
                    ins.then_inc(product_ready, 1)
                    g += 1

        def take(eng):
            link = linker(eng, drain_step)
            g = 0
            for j in range(n_out):
                for o, n in chunks:
                    eng.wait_ge(product_ready, g + 1)
                    drain(j, o, n, m.bank(g % 8, n, rows), link).then_inc(product_taken, 1)
                    g += 1

        (block.scalar if on == "scalar" else block.vector)(take)


def add_to(nc, m, dst, bias=None):
    def drain(j, o, n, acc, link):
        out = dst[:, j, o:o + n]
        if bias is None:
            return nc.vector.tensor_tensor(out, out, acc, ALU.add)
        return nc.vector.scalar_tensor_tensor(out=out, in0=acc, scalar=bias(j), in1=out, op0=ALU.add, op1=ALU.add)
    return drain


def full(t):
    return lambda k, o, n: t[:, k, o:o + n]


def setup(nc, m, d):
    rc = nc.alloc_sbuf_tensor("route_consts", [P, ROUTE_CONSTS], F32)
    m.route_consts = {name: rc[0:rows, c:c + n] for name, (c, n, rows) in ROUTE_AT.items()}
    m.pair_idx = nc.alloc_sbuf_tensor("pair_idx", [ROWT, 4 * NROWT], I32)[:, :]
    m.slot_token = nc.alloc_sbuf_tensor("slot_token", [P, TABLE], I32)[:, :]
    m.block_expert = nc.alloc_sbuf_tensor("block_expert", [1, TABLE], I32)[:, :]
    m.rounds = nc.alloc_sbuf_tensor("rounds", [1, 1], I32)[:, :]
    m.block_idx = [nc.alloc_sbuf_tensor("block_idx%d" % i, [P, 1], I32)[:, :] for i in range(4)]
    m.idle = nc.alloc_sbuf_tensor("idle", [P, 1], F32)[:, :]
    m.zeros = nc.alloc_sbuf_tensor("zeros", [P, 4 * D], F32)
    m.x_rows = nc.dram_tensor("x_rows", (N, D), F32).ap()
    m.y_rows = nc.dram_tensor("y_rows", (TABLE * P, D), F32).ap()
    m.y_cleared = nc.alloc_semaphore("y_cleared", num=GATHER_SEM + 58)
    m.gathered = [nc.alloc_semaphore("gathered%d" % i, num=GATHER_SEM + 60 + i) for i in range(4)]
    m.fetched = [nc.alloc_semaphore("fetched%d" % i, num=GATHER_SEM + 70 + i) for i in range(16)]
    m.eps = nc.alloc_sbuf_tensor("eps", [P, 1], F32)
    with stage(nc, "vectors_landed") as (block, vectors_landed):

        @block.sync
        def _(sp):
            sp.dma_start(m.vec[:, :], d["vec"]).then_inc(vectors_landed, 16)
            sp.dma_start(m.ident[:, :], d["ident"]).then_inc(vectors_landed, 16)
            fetch_patches(sp, m, d)
            fetch(sp, m, "pick", (m.wb[:, 1536:1536 + 32 * P], d["pick"]))
            fetch(sp, m, "masks", (m.order[:, :], d["order"]), (rc[:, :], d["route_consts"]),
                  (m.routers[:, :], d["routers"]), (m.mask1[:, :], d["mask1"]), (m.mask2[:, :], d["mask2"]),
                  (m.mask3[:, :], d["mask3"]), (m.head_of[:, :], d["head_of"]))
            sp.wait_ge(vectors_landed, 32)

        @block.vector
        def _(dve):
            dve.wait_ge(vectors_landed, 32)
            nc.vector.tensor_copy(m.ident_bf[:, :], m.ident[:, :])

        @block.gpsimd
        def _(pool):
            nc.gpsimd.memset(m.eps[:, :], EPS)
            nc.gpsimd.memset(m.idle, 0.0)
            nc.gpsimd.memset(m.ones[:, :], 1.0)
            nc.gpsimd.memset(m.mean_w[:, :], 1.0 / D)


def patch_input(m):
    kin = 6
    w = m.wb[:, 0:kin * D].rearrange("p (k n) -> p k n", k=kin)
    patches = m.big1[:, :, :].rearrange("p a b -> p (a b)")[:, 0:kin * BATCH * PATCHES].rearrange(
        "p (k n) -> p k n", k=kin)
    pos = m.small[:, 0:KD * 37].rearrange("p (k t) -> p k t", k=KD)
    return patches, w, pos


def fetch_patches(sp, m, d):
    patches, w, pos = patch_input(m)
    fetch(sp, m, "patches", (w, d["tok_w"]), (patches, d["patches"]), (pos, d["tok_pos"]))


def patch_tokens(nc, m, d):
    patches, w, pos = patch_input(m)
    kin = w.shape[1]
    text = text_input(m)
    h4 = m.h[:, :, :].rearrange("p k (b t) -> p k b t", t=SEQ)
    half = BATCH // 2
    with stage(nc, "product_ready", "pos_ready") as (block, product_ready, pos_ready):

        @block.sync
        def _(sp):
            fetch(sp, m, "text_input", *zip(text, (d["tokens"], d["txt_pos"], d["fresh"])))
            fetch_layer(sp, m, d, "layer_vectors", 0)
            fetch_layer(sp, m, d, "state_mix", 0)
            fetch_layer(sp, m, d, "up", 0)
            fetch_layer(sp, m, d, "down", 0)

        @block.scalar
        def _(act):
            act.wait_ge(m.landed["pick"], 16)
            nc.scalar.copy(m.pick[:, :], m.wb[:, 1536:1536 + 32 * P])

        @block.tensor
        def _(pe):
            pe.wait_ge(m.landed["patches"], 48)
            for j in range(KD):
                for c in range(2):
                    for k in range(kin):
                        ins = nc.tensor.matmul(m.bank(2 * j + c, half * PATCHES), w[:, k, j * P:j * P + P],
                                               patches[:, k, c * half * PATCHES:(c + 1) * half * PATCHES],
                                               start=k == 0, stop=k == kin - 1)
                    ins.then_inc(product_ready, 1)

        @block.vector
        def _(dve):
            dve.wait_ge(m.landed["patches"], 48)
            for k in range(KD):
                nc.vector.tensor_scalar(pos[:, k, 1:37], pos[:, k, 1:37], m.v("tok_b", k), None,
                                        ALU.add).then_inc(pos_ready, 1)
                nc.vector.tensor_scalar(pos[:, k, 0:1], pos[:, k, 0:1], m.v("cls", k), None,
                                        ALU.add).then_inc(pos_ready, 1)
            dve.wait_ge(pos_ready, 2 * KD)
            for k in range(KD):
                nc.vector.tensor_copy(h4[:, k, :, 0:1], pos[:, k, 0:1].unsqueeze(1).broadcast_to([P, BATCH, 1]))
            for j in range(KD):
                for c in range(2):
                    dve.wait_ge(product_ready, 2 * j + c + 1)
                    nc.vector.tensor_tensor(
                        h4[:, j, c * half:(c + 1) * half, 1:37],
                        m.bank(2 * j + c, half * PATCHES).rearrange("p (b t) -> p b t", t=PATCHES),
                        pos[:, j:j + 1, 1:37].broadcast_to([P, half, PATCHES]), ALU.add)


def text_input(m):
    pos = m.xn[:, 0, 0:KD * TEXT].rearrange("p (k t) -> p k t", k=KD)
    return m.idx[:, :], pos, m.s1[0:STATE, 0, 0:BATCH * TEXT]


def layer_weights(m):
    return {"B": m.wa[:, 0:KD * STATE].rearrange("p (k n) -> p k n", k=KD),
            "Dw": m.wa[:, 128:128 + KD * D].rearrange("p (k n) -> p k n", k=KD),
            "C": m.wa[0:STATE, 640:640 + D],
            "w1": m.wa[:, 1024:1024 + KD * FF].rearrange("p (k n) -> p k n", k=KD),
            "w2": m.wa[:, 3072:3072 + 8 * D].rearrange("p (k n) -> p k n", k=8), "lvec": m.lvec[:, :]}


FETCHED = {"layer_vectors": ("lvec",), "state_mix": ("B", "Dw", "C"), "up": ("w1",), "down": ("w2",)}


def fetch_layer(sp, m, d, name, layer):
    to = layer_weights(m)
    fetch(sp, m, name, *[(to[part], d[part][layer]) for part in FETCHED[name]])


def fetch_scan(sp, m, d):
    fetch(sp, m, "scan", (m.wb[:, 0:2048], d["in_proj"]), (m.wb[:, 2048:2560], d["dt_rows"]),
          (m.wb[:, 2560:3072], d["bc_rows"]), (m.wb[:, 3072:4096], d["out_proj"]))


def text_encoder(nc, m, d):
    nt = BATCH * TEXT
    flat1 = m.big1[:, :, :].rearrange("p a b -> p (a b)")
    x = flat1[:, 0:KD * nt].rearrange("p (k n) -> p k n", k=KD)
    xn = flat1[:, KD * nt:2 * KD * nt].rearrange("p (k n) -> p k n", k=KD)
    cen = flat1[:, 2 * KD * nt:3 * KD * nt].rearrange("p (k n) -> p k n", k=KD)
    sq = flat1[:, 3 * KD * nt:4 * KD * nt].rearrange("p (k n) -> p k n", k=KD)
    rows = flat1[:, 4 * KD * nt:6 * KD * nt].rearrange("p (j n) -> p j n", j=8)[:, 0:4, :]
    hid = m.big2[:, :, :].rearrange("p a b -> p (a b)")[:, 0:8 * nt].rearrange("p (k n) -> p k n", k=8)
    work = (cen, sq)
    halves = [(0, nt // 2), (nt // 2, nt // 2)]
    idx, pos, fresh = text_input(m)
    wrapped = nc.alloc_sbuf_tensor("wrapped", [P, 4], I32)
    gathered = nc.alloc_semaphore("gathered", num=GATHER_SEM)
    with stage(nc, "index_step", "turned") as (block, index_step, turned):

        @block.vector
        def _(dve):
            link = linker(dve, index_step)
            dve.wait_ge(m.landed["text_input"], 48)
            link(nc.vector.tensor_scalar(wrapped[:, :], idx, 0.0, float(VOCAB), ALU.is_lt, ALU.mult))
            link(nc.vector.tensor_tensor(idx, idx, wrapped[:, :], ALU.add))
            nc.vector.tensor_scalar(idx, idx, 0.0, float(VOCAB - 1), ALU.max,
                                    ALU.min).then_inc(index_step, 1)
            for k in range(KD):
                dve.wait_ge(turned, k + 1)
                nc.vector.tensor_tensor(
                    x[:, k, :].rearrange("p (b t) -> p b t", t=TEXT),
                    m.bank(k).rearrange("p (b t) -> p b t", t=TEXT),
                    pos[:, k:k + 1, :].broadcast_to([P, BATCH, TEXT]), ALU.add)

        @block.gpsimd
        def _(pool):
            pool.wait_ge(index_step, 3)
            for j in range(4):
                pool.indirect_dma_start(
                    rows[:, j, :], None, d["emb"], bass.IndirectOffsetOnAxis(ap=idx[:, j:j + 1], axis=0),
                ).then_inc(gathered, 16)

        @block.tensor
        def _(pe):
            pe.wait_ge(gathered, 64)
            for k in range(KD):
                for j in range(4):
                    ins = nc.tensor.transpose(m.bank(k)[:, j * P:j * P + P], rows[:, j, k * P:k * P + P],
                                              m.ident[:, :])
                ins.then_inc(turned, 1)

    wB, wD, wC, w1, w2 = (layer_weights(m)[name] for name in ("B", "Dw", "C", "w1", "w2"))
    decay = m.s2[0:STATE, 0, 0:nt]
    states = m.s2[0:STATE, 1, 0:nt]
    a = m.s1[0:STATE, 1, 0:1]
    L = LVEC
    lv = lambda name, k: m.lvec[:, L[name] + k:L[name] + k + 1]
    chunks = [(0, nt)]

    def encoder_layer(layer, first_ahead, last=False):
        def landed(name):
            loads = 16 * len(FETCHED[name])
            return m.landed[name], layer * loads + loads

        def mix(pe, normed, input_ready, decay_step, scanned, mixed):
            pe.wait_ge(*landed("state_mix"))
            pe.wait_ge(normed, KD * len(halves))
            for k in range(KD):
                ins = nc.tensor.matmul(m.bank(1, nt, STATE), wB[:, k, :], xn[:, k, :], start=k == 0, stop=k == KD - 1)
            ins.then_inc(input_ready, 1)
            for j in range(KD):
                for k in range(KD):
                    nc.tensor.matmul(m.bank((2, 7)[j], nt), wD[:, k, j * P:j * P + P], xn[:, k, :], start=k == 0,
                                     stop=False)
            pe.wait_ge(scanned, 1)
            for j in range(KD):
                nc.tensor.matmul(m.bank((2, 7)[j], nt), wC[:, j * P:j * P + P], states, start=False,
                                 stop=True).then_inc(mixed, 1)

        def rate(act, normed, input_ready, decay_step, scanned, mixed):
            nc.scalar.activation(a, m.lvec[0:STATE, L["A"]:L["A"] + 1], ACT.Sigmoid).then_inc(decay_step, 1)

        def scan(dve, normed, input_ready, decay_step, scanned, mixed):
            dve.wait_ge(decay_step, 1)
            nc.vector.tensor_scalar(decay, fresh, a, None, ALU.mult).then_inc(decay_step, 1)
            dve.wait_ge(decay_step, 2)
            dve.wait_ge(input_ready, 1)
            nc.vector.tensor_tensor_scan(states, decay, m.bank(1, nt, STATE), 0.0, ALU.mult,
                                         ALU.add).then_inc(scanned, 1)
            for j in range(KD):
                dve.wait_ge(mixed, j + 1)
                nc.vector.tensor_tensor(x[:, j, :], x[:, j, :], m.bank((2, 7)[j], nt), ALU.add)

        layernorm(nc, m, full(x), full(xn), halves, lambda k: lv("ln1_s", k), lambda k: lv("ln1_b", k), work=work,
                  vectors=landed("layer_vectors"), ahead=first_ahead,
                  behind=(("input_ready", "decay_step", "scanned", "mixed"), mix, rate, scan))
        layernorm(nc, m, full(x), full(xn), halves, lambda k: lv("ln2_s", k), lambda k: lv("ln2_b", k), work=work,
                  ahead=None if last else lambda sp: fetch_layer(sp, m, d, "state_mix", layer + 1),
                  then=Products(
                      lambda k, j: w1[:, k, j * P:j * P + P], 8,
                      lambda j, o, n, acc, link: nc.scalar.activation(hid[:, j, o:o + n], acc, ACT.Gelu,
                                                                      bias=lv("b1", j)),
                      landed("up"), hidden=hid, second_w=lambda k, j: w2[:, k, j * P:j * P + P],
                      second_drain=add_to(nc, m, x, lambda j: lv("b2", j)), second_landed=landed("down"),
                      behind=None if last else lambda sp: fetch_layer(sp, m, d, "up", layer + 1)))

    def start_ahead(layer):
        def ahead(sp):
            fetch_layer(sp, m, d, "layer_vectors", layer)
            fetch_layer(sp, m, d, "down", layer)
        return ahead

    encoder_layer(0, lambda sp: fetch_scan(sp, m, d))
    with nc.Fori(1, LAYERS - 1) as layer:
        encoder_layer(layer, start_ahead(layer))
    encoder_layer(LAYERS - 1, start_ahead(LAYERS - 1), True)
    h4 = m.h[:, :, :].rearrange("p k (b t) -> p k b t", t=SEQ)
    layernorm(nc, m, full(x), lambda k, o, n: h4[:, k, o // TEXT:(o + n) // TEXT, 1 + PATCHES:SEQ], halves,
              lambda k: m.v("lnf_s", k), lambda k: m.v("lnf_b", k), fold=TEXT, work=work)


def pieces(base, n):
    at = base
    while at < base + n:
        k = min(base + n, (at // BANK + 1) * BANK) - at
        yield at, at - base, k
        at += k


def clear_results(nc, m):
    with stage(nc, "zeroed") as (block, zeroed):

        @block.vector
        def _(dve):
            nc.vector.memset(m.zeros[:, :], 0.0).then_inc(zeroed, 1)

        @block.sync
        def _(sp):
            sp.wait_ge(zeroed, 1)
            sp.dma_start(m.y_rows.rearrange("(p j r) n -> p j (r n)", p=P, r=4),
                         m.zeros[:, :].unsqueeze(1).broadcast_to([P, TABLE // 4, 4 * D])).then_inc(m.y_cleared, 16)


def selective_scan(nc, m, d):
    x2 = m.s3
    xi, z = m.big1[:, 0:4, :], m.big1[:, 4:8, :]
    xc, delta = m.big2[:, 0:4, :], m.big2[:, 4:8, :]
    w_in = m.wb[:, 0:2048].rearrange("p (k n) -> p k n", k=KD)
    w_dt = m.wb[:, 2048:2560].rearrange("p (k n) -> p k n", k=4)
    w_bc = m.wb[:, 2560:3072].rearrange("p (k n) -> p k n", k=4)
    w_out = m.wb[:, 3072:4096].rearrange("p (k n) -> p k n", k=4)
    neg_a = m.small[:, 1200:1264]
    layernorm(nc, m, full(m.h), full(m.xn), CHUNKS, ahead=lambda sp: fetch_attention1(sp, m, d))
    layernorm(nc, m, full(m.xn), full(x2), CHUNKS, lambda k: m.v("norm_w", k), lambda k: m.v("norm_b", k))
    with stage(nc, "product_ready", "product_taken", "conv_step", "conv_ready") as (
            block, product_ready, product_taken, conv_step, conv_ready):

        @block.tensor
        def _(pe):
            pe.wait_ge(m.landed["scan"], 16 * 4)
            g = 0
            for j in range(8):
                for o, n in CHUNKS:
                    if g >= 8:
                        pe.wait_ge(product_taken, g - 7)
                    for k in range(KD):
                        ins = nc.tensor.matmul(m.bank(g % 8, n), w_in[:, k, j * P:j * P + P], x2[:, k, o:o + n],
                                               start=k == 0, stop=k == KD - 1)
                    ins.then_inc(product_ready, 1)
                    g += 1

        @block.scalar
        def _(act):
            g = 0
            for j in range(8):
                for o, n in CHUNKS:
                    act.wait_ge(product_ready, g + 1)
                    nc.scalar.activation(m.big1[:, j, o:o + n], m.bank(g % 8, n),
                                         ACT.Copy if j < 4 else ACT.Silu).then_inc(product_taken, 1)
                    g += 1
                if j >= 4:
                    act.wait_ge(conv_ready, j - 3)
                    nc.scalar.activation(xc[:, j - 4, :], xc[:, j - 4, :], ACT.Silu)

        @block.vector
        def _(dve):
            link = linker(dve, conv_step)
            for k in range(4):
                dve.wait_ge(product_taken, NCH * (k + 1))
                link(nc.vector.tensor_scalar(xc[:, k, :], xi[:, k, :], m.v("conv_w", 4 * k + 3), m.v("conv_b", k),
                                             ALU.mult, ALU.add))
                to = xc[:, k, :].rearrange("p (b t) -> p b t", t=SEQ)
                of = xi[:, k, :].rearrange("p (b t) -> p b t", t=SEQ)
                for back in (1, 2, 3):
                    ins = nc.vector.scalar_tensor_tensor(
                        out=to[:, :, back:], in0=of[:, :, :SEQ - back], scalar=m.v("conv_w", 4 * k + 3 - back),
                        in1=to[:, :, back:], op0=ALU.mult, op1=ALU.add)
                    if back < 3:
                        link(ins)
                ins.then_inc(conv_ready, 1)

    low = [m.s1[:, 0, :], m.s1[:, 1, :], m.s2[:, 0, :], m.s2[:, 1, :]]
    rest = m.s3[:, 0, :]
    with stage(nc, "dt_ready", "bc_ready", "affine_ready", "low_ready", "exp_ready", "log_ready", "delta_ready",
               "split_step") as (
            block, dt_ready, bc_ready, affine_ready, low_ready, exp_ready, log_ready, delta_ready, split_step):
        @block.tensor
        def _(pe):
            for w, ready, first in ((w_dt, dt_ready, 0), (w_bc, bc_ready, NCH)):
                for c, (o, n) in enumerate(CHUNKS):
                    for k in range(4):
                        ins = nc.tensor.matmul(m.bank(first + c, n), w[:, k, :], xc[:, k, o:o + n], start=k == 0,
                                               stop=k == 3)
                    ins.then_inc(ready, 1)

        @block.scalar
        def _(act):
            for c, (o, n) in enumerate(CHUNKS):
                act.wait_ge(dt_ready, c + 1)
                for k in range(4):
                    nc.scalar.activation(delta[:, k, o:o + n], m.bank(c, n), ACT.Identity, scale=m.v("dt_w", k),
                                         bias=m.v("dt_b", k)).then_inc(affine_ready, 1)
            c = VEC["A_log"][0]
            nc.scalar.activation(neg_a, m.vec[:, c:c + 64], ACT.Exp).then_inc(exp_ready, 1)
            for k in range(4):
                act.wait_ge(low_ready, k + 1)
                nc.scalar.activation(low[k], low[k], ACT.Exp).then_inc(exp_ready, 1)
            for k in range(4):
                act.wait_ge(exp_ready, k + 2)
                nc.scalar.activation(low[k], low[k], ACT.Ln, bias=1.0).then_inc(log_ready, 1)

        @block.vector
        def _(dve):
            for k in range(4):
                dve.wait_ge(affine_ready, 4 * (NCH - 1) + k + 1)
                nc.vector.scalar_tensor_tensor(out=low[k], in0=delta[:, k, :], scalar=-1.0, in1=delta[:, k, :],
                                               op0=ALU.mult, op1=ALU.min).then_inc(low_ready, 1)
            dve.wait_ge(exp_ready, 1)
            nc.vector.tensor_scalar(neg_a, neg_a, -1.0, None, ALU.mult)
            link = linker(dve, split_step)
            for c, (o, n) in enumerate(CHUNKS):
                dve.wait_ge(bc_ready, c + 1)
                acc = m.bank(NCH + c, n)
                t1, r, t2 = m.parts[:, 0, o:o + n], rest[:, o:o + n], m.parts[:, 1, o:o + n]
                link(nc.vector.tensor_copy(t1, acc))
                link(nc.vector.tensor_tensor(r, acc, t1, ALU.subtract))
                link(nc.vector.tensor_copy(t2, r))
                link(nc.vector.tensor_copy(t1[32:64, :], t2[32:64, :]))
                link(nc.vector.tensor_tensor(r, r, t2, ALU.subtract))
                nc.vector.tensor_copy(t1[64:96, :], r[64:96, :])
            for k in range(4):
                dve.wait_ge(log_ready, k + 1)
                nc.vector.scalar_tensor_tensor(out=delta[:, k, :], in0=delta[:, k, :], scalar=0.0, in1=low[k],
                                               op0=ALU.max, op1=ALU.add).then_inc(delta_ready, 1)
            for k in (2, 3):
                dve.wait_ge(delta_ready, k + 1)
                nc.vector.tensor_tensor(xi[:, k, :], delta[:, k, :], xc[:, k, :], ALU.mult)

        @block.gpsimd
        def _(pool):
            for k in (0, 1):
                pool.wait_ge(delta_ready, k + 1)
                nc.gpsimd.tensor_tensor(xi[:, k, :], delta[:, k, :], xc[:, k, :], ALU.mult)

    decay = [m.s1[:, i, :] for i in range(2)]
    state = [m.s2[:, i, :] for i in range(2)]
    c_row = [m.s3[:, i, :] for i in range(2)]
    inflow, seen, whole = m.wa[:, 4096:4096 + N], [m.wa[:, 4096 + i * N:4096 + (i + 1) * N] for i in (1, 2)], \
        m.small[:, 0:N]
    tokens = lambda a: a.rearrange("p (b t) -> p b t", t=SEQ)
    Y, B = 0, 3 * BANK
    NQ, QW = 4, N // 4
    TILES = 4
    with stage(nc, "cleared", "y_taken", "b_ready", "c_ready", "c_taken", "summed", "decay_ready", "inflow_ready",
               "scanned", "seen_ready") as (
            block, cleared, y_taken, b_ready, c_ready, c_taken, summed, decay_ready, inflow_ready, scanned,
            seen_ready):

        @block.tensor
        def _(pe):
            def spread_b(row):
                for at, o, n in pieces(B, N):
                    ins = nc.tensor.matmul(m.ps[:, at:at + n], m.pick[:, bass.ds(row * P, P)],
                                           m.parts[:, 0, o:o + n], start=True, stop=True)
                ins.then_inc(b_ready, 1)

            def spread_c(k, i, quarters, peeled=False):
                for q in quarters:
                    if not peeled or q >= 2:
                        pe.wait_ge(c_taken, i * NQ + (DS * k * NQ + q - 1))
                    nc.tensor.matmul(m.bank(6 + q % 2, QW), m.pick[:, bass.ds((i + DS) * P, P)],
                                     m.parts[:, 0, q * QW:(q + 1) * QW], start=True, stop=True).then_inc(c_ready, 1)

            def add_y(what, first, parts=slice(None)):
                for at, o, n in list(pieces(Y, N))[parts]:
                    ins = nc.tensor.matmul(m.ps[:, at:at + n], m.ident[:, :], what[:, o:o + n], start=first,
                                           stop=False, skip_group_check=True)
                return ins

            def step(k, j, s, first=False):
                pe.wait_ge(inflow_ready, j + (DS * k + 1))
                spread_b(j + 1)
                spread_c(k, j + 1, (0, 1))
                pe.wait_ge(seen_ready, j + DS * k)
                if first and k:
                    pe.wait_ge(y_taken, k)
                add_y(seen[s], first, slice(0, 1))
                spread_c(k, j + 1, (2, 3))
                add_y(seen[s], first, slice(1, None)).then_inc(summed, 1)

            for k in range(TILES):
                if k:
                    pe.wait_ge(inflow_ready, DS * k)
                spread_b(0)
                spread_c(k, 0, range(NQ), k == 0)
                if k:
                    pe.wait_ge(seen_ready, DS * k - 1)
                    add_y(seen[0], False).then_inc(summed, 1)
                pe.wait_ge(inflow_ready, DS * k + 1)
                spread_b(1)
                spread_c(k, 1, range(NQ))
                if k:
                    pe.wait_ge(seen_ready, DS * k)
                    add_y(seen[1], False).then_inc(summed, 1)
                for s in range(2):
                    step(k, s + 1, s, s == 0)
                with pe.Fori(1, DS // 2 - 1) as pair:
                    for s in range(2):
                        step(k, pair * 2 + (s + 1), s)
            for s in range(2):
                pe.wait_ge(seen_ready, DS * TILES - 1 + s)
                add_y(seen[s], False).then_inc(summed, 1)

        @block.scalar
        def _(act):
            act.wait_ge(cleared, 1)

            def rates(k, i, s, peeled=False):
                if not peeled:
                    act.wait_ge(scanned, i + (DS * k + s - 1))
                nc.scalar.activation(
                    tokens(decay[s])[:, :, 1:], tokens(delta[:, k, :])[:, :, 1:], ACT.Exp,
                    scale=m.small[:, bass.ds(i + (1200 + k * DS + s), 1)]).then_inc(decay_ready, 1)
                for q in range(NQ):
                    act.wait_ge(c_ready, i * NQ + ((DS * k + s) * NQ + q + 1))
                    if q == 0 and not peeled:
                        act.wait_ge(seen_ready, i + (DS * k + s - 1))
                    nc.scalar.copy(c_row[s][:, q * QW:(q + 1) * QW], m.bank(6 + q % 2, QW)).then_inc(c_taken, 1)

            for k in range(TILES):
                for s in range(2):
                    rates(k, 0, s, k == 0)
                with act.Fori(1, DS // 2) as pair:
                    for s in range(2):
                        rates(k, pair * 2, s)

        @block.gpsimd
        def _(pool):
            def see(k, i, s, peeled=False):
                pool.wait_ge(scanned, i + (DS * k + s + 1))
                pool.wait_ge(c_taken, i * NQ + (DS * k + s + 1) * NQ)
                if not peeled:
                    pool.wait_ge(summed, i + (DS * k + s - 1))
                nc.gpsimd.tensor_tensor(seen[s], state[s], c_row[s], ALU.mult).then_inc(seen_ready, 1)

            for s in range(2):
                see(0, 0, s, True)
            with pool.Fori(1, DS * TILES // 2) as pair:
                for s in range(2):
                    see(0, pair * 2, s)

        @block.vector
        def _(dve):
            def gate(k):
                dve.wait_ge(summed, DS * (k + 1))
                nc.vector.scalar_tensor_tensor(out=whole, in0=xc[:, k, :], scalar=m.v("D_skip", k),
                                               in1=m.ps[:, Y:Y + N], op0=ALU.mult, op1=ALU.add).then_inc(y_taken, 1)
                dve.wait_ge(y_taken, k + 1)
                nc.vector.tensor_tensor(z[:, k, :], z[:, k, :], whole, ALU.mult)

            def step(k, i, s, peeled=False):
                dve.wait_ge(b_ready, i + (DS * k + s + 1))
                if not peeled or s:
                    dve.wait_ge(scanned, i + (DS * k + s))
                nc.vector.tensor_tensor(inflow, xi[:, k, :], m.ps[:, B:B + N], ALU.mult).then_inc(inflow_ready, 1)
                dve.wait_ge(inflow_ready, i + (DS * k + s + 1))
                dve.wait_ge(decay_ready, i + (DS * k + s + 1))
                if not peeled:
                    dve.wait_ge(seen_ready, i + (DS * k + s - 1))
                nc.vector.tensor_tensor_scan(state[s], decay[s], inflow, 0.0, ALU.mult,
                                             ALU.add).then_inc(scanned, 1)

            nc.vector.memset(tokens(decay[0])[:, :, 0:1], 0.0)
            nc.vector.memset(tokens(decay[1])[:, :, 0:1], 0.0).then_inc(cleared, 1)
            dve.wait_ge(cleared, 1)
            for k in range(TILES):
                for s in range(2):
                    step(k, 0, s, k == 0)
                if k:
                    gate(k - 1)
                with dve.Fori(1, DS // 2) as pair:
                    for s in range(2):
                        step(k, pair * 2, s)
            gate(TILES - 1)

    def residual(j, o, n, acc, link):
        out = m.h[:, j, o:o + n]
        link(nc.vector.tensor_tensor(out, out, acc, ALU.add))
        return nc.vector.tensor_tensor(out, out, m.xn[:, j, o:o + n], ALU.add)
    linear(nc, m, full(z), lambda k, j: w_out[:, k, j * P:j * P + P], 4, KD, CHUNKS, residual, on="vector")


def route(nc, m, groups, experts, w, sigmoid, meanwhile=None):
    g_all = NROWT * groups
    ne = groups * experts
    cols_ = g_all * experts
    flat = m.big1[:, :, :].rearrange("p a b -> p (a b)")
    tile3 = lambda i, e=experts: flat[0:ROWT, i * 768:i * 768 + g_all * e].rearrange("p (g e) -> p g e", e=e)
    sc, key, one, two, tmp = (tile3(i) for i in range(5))
    order = m.order[0:ROWT, E0 - experts:E0].unsqueeze(1).broadcast_to([ROWT, g_all, experts])
    red = [m.small[0:ROWT, 32 * i:32 * i + g_all].unsqueeze(2) for i in range(4)]
    wide = lambda a: a.broadcast_to([ROWT, g_all, experts])
    parts = m.big2[:, :, :].rearrange("p a b -> p (a b)")[0:ROWT, 0:g_all * 64].bitcast(BF16).rearrange(
        "p (g s) -> p g s", s=P)
    half = NROWT // 2
    with stage(nc, "logits_ready", "logits_taken", "exp_ready", "route_step", "parts_ready", "turned",
               "turned_taken", *(meanwhile[0] if meanwhile else ())) as (
            block, logits_ready, logits_taken, exp_ready, route_step, parts_ready, turned, turned_taken,
            *meanwhile_sems):

        @block.tensor
        def _(pe):
            pe.wait_ge(m.landed["masks"], 16 * 7)
            for t in range(NROWT):
                at = (t // half) * BANK + (t % half) * ne
                for k in range(KD):
                    ins = nc.tensor.matmul(m.ps[0:ROWT, at:at + ne], m.xn[:, k, t * ROWT:(t + 1) * ROWT],
                                           w[:, k, :], start=k == 0, stop=k == KD - 1)
            ins.then_inc(logits_ready, 1)
            if meanwhile:
                meanwhile[1](pe, *meanwhile_sems)
            if not sigmoid:
                return
            pe.wait_ge(parts_ready, 1)
            for g in range(groups):
                for t in range(NROWT):
                    at = (2 + 2 * g) * 2 * BANK + (t // 11) * 2 * BANK + (t % 11) * ROWT
                    ins = nc.tensor.transpose(m.ps_bf[:, at:at + ROWT], parts[:, t * groups + g, :],
                                              m.ident_bf[0:ROWT, 0:ROWT])
                ins.then_inc(turned, 1)

        @block.scalar
        def _(act):
            act.wait_ge(logits_taken, 1)
            nc.scalar.activation(sc, sc, ACT.Exp, scale=-1.0 if sigmoid else 1.0).then_inc(exp_ready, 1)
            if meanwhile:
                meanwhile[2](act, *meanwhile_sems)
            if not sigmoid:
                return
            for g in range(groups):
                act.wait_ge(turned, g + 1)
                base = (2 + 2 * g) * 2 * BANK
                nc.scalar.copy(m.parts[:, g, 0:11 * ROWT], m.ps_bf[:, base:base + 11 * ROWT])
                nc.scalar.copy(m.parts[:, g, 11 * ROWT:N], m.ps_bf[:, base + 2 * BANK:base + 2 * BANK + ROWT])

        @block.vector
        def _(dve):
            link = linker(dve, route_step)
            tt, ts = nc.vector.tensor_tensor, nc.vector.tensor_scalar
            if sigmoid:
                link(nc.vector.memset(parts, 0.0))
            dve.wait_ge(logits_ready, 1)
            for b in range(2):
                link(nc.vector.tensor_copy(sc[:, b * (g_all // 2):(b + 1) * (g_all // 2), :],
                                           m.ps[0:ROWT, b * BANK:b * BANK + cols_ // 2].rearrange(
                                               "p (g e) -> p g e", e=experts)))
            if sigmoid:
                nc.vector.engine_nop().then_inc(logits_taken, 1)
                dve.wait_ge(exp_ready, 1)
                link(ts(sc, sc, 1.0, None, ALU.add))
                link(nc.vector.reciprocal(sc, sc))
            else:
                link(nc.vector.tensor_reduce(red[0].squeeze(2), sc, AX_X, ALU.max))
                tt(sc, sc, wide(red[0]), ALU.subtract).then_inc(logits_taken, 1)
                dve.wait_ge(exp_ready, 1)
                link(nc.vector.tensor_reduce(red[0].squeeze(2), sc, AX_X, ALU.add))
                link(nc.vector.reciprocal(red[0], red[0]))
                link(tt(sc, sc, wide(red[0]), ALU.mult))

            def first_of_max(of, best, out):
                link(nc.vector.tensor_reduce(best.squeeze(2), of, AX_X, ALU.max))
                link(tt(key, of, wide(best), ALU.is_equal))
                link(tt(key, key, order, ALU.mult))
                link(nc.vector.tensor_reduce(red[3].squeeze(2), key, AX_X, ALU.max))
                link(tt(out, order, wide(red[3]), ALU.is_equal))

            first_of_max(sc, red[0], one)
            link(nc.vector.scalar_tensor_tensor(out=tmp, in0=one, scalar=-4.0, in1=sc, op0=ALU.mult, op1=ALU.add))
            first_of_max(tmp, red[1], two)
            if not sigmoid:
                for r in red[0:2]:
                    ts(r, r, 0.5, None, ALU.mult)
                return
            link(tt(one, one, wide(red[0]), ALU.mult))
            link(tt(two, two, wide(red[1]), ALU.mult))
            link(tt(one, one, two, ALU.add))
            link(tt(red[0], red[0], red[1], ALU.add))
            link(ts(red[0], red[0], 1e-20, None, ALU.add))
            link(nc.vector.reciprocal(red[0], red[0]))
            link(tt(one, one, wide(red[0]), ALU.mult))
            for p in range(3):
                part = parts[:, :, 32 * p:32 * p + experts]
                link(nc.vector.tensor_copy(part, one))
                if p < 2:
                    link(tt(one, one, part, ALU.subtract))
            nc.vector.engine_nop().then_inc(parts_ready, 1)


FLOOR = 0.498046875
MAGIC = 1.5 * 2.0 ** 23


def mixture0(nc, m, d):
    wr = m.routers[:, 0:KD * 2 * E0].rearrange("p (k n) -> p k n", k=KD)
    layernorm(nc, m, full(m.h), full(m.xn), CHUNKS, ahead=lambda sp: fetch_ternary(sp, m, d))
    route(nc, m, 2, E0, wr, False)
    blocks = dispatch(nc, m, d)
    run_blocks(nc, m, d, blocks)
    combine(nc, m, blocks)


def dispatch(nc, m, d):
    ne = 2 * E0
    g_all = 2 * NROWT
    wide_n = g_all * E0
    flat1 = m.big1[:, :, :].rearrange("p a b -> p (a b)")
    flat2 = m.big2[:, :, :].rearrange("p a b -> p (a b)")
    tile = lambda i, rows=ROWT: flat1[0:rows, i * 768:(i + 1) * 768]
    one, two, both, slot, tmp = tile(2), tile(3), tile(1), tile(0), tile(4)
    by_expert = lambda a: a.rearrange("p (t e) -> p t e", e=ne)
    by_group = lambda a: a.rearrange("p (g e) -> p g e", e=E0)
    before = flat1[:, 3840:3840 + wide_n]
    c = m.route_consts
    tri, ones, iota, token, place = c["tri"], c["ones"], c["iota"], c["token"], c["place"]
    counts, n_blocks, ends, starts, hits = (flat1[:, 4700 + 64 * i:4764 + 64 * i] for i in range(5))
    pair_slot, pair_block, pair_place = (flat1[0:ROWT, 5100 + 48 * i:5148 + 48 * i] for i in range(3))
    expert_col = flat1[:, 5300:5301]
    rounds_f = flat1[0:1, 5302:5303]
    place_hot = [flat1[0:ROWT, 5400 + P * i:5400 + P * (i + 1)] for i in range(4)]
    block_hot = [flat1[0:ROWT, 6000 + TABLE * i:6000 + TABLE * (i + 1)] for i in range(4)]
    rows = flat2[0:ROWT, 0:NROWT * D].rearrange("p (t n) -> p t n", n=D)
    x_rows, y_rows = m.x_rows, m.y_rows
    pair_idx = m.pair_idx
    slot_token, block_expert, rounds = m.slot_token, m.block_expert, m.rounds
    half = wide_n // 2
    pairs = 2 * g_all
    with stage(nc, "both_ready", "sums_ready", "step", "hot_ready", "hot_used",
               "experts_ready", "experts_turned", "rows_turned", "rows_taken", "rows_stored") as (
            block, both_ready, sums_ready, step, hot_ready, hot_used, experts_ready,
            experts_turned, rows_turned, rows_taken, rows_stored):

        @block.tensor
        def _(pe):
            pe.wait_ge(both_ready, 1)
            for b in range(2):
                nc.tensor.matmul(m.bank(b, half, ROWT), tri[0:ROWT, 0:ROWT], both[:, b * half:(b + 1) * half],
                                 start=True, stop=True)
                ins = nc.tensor.matmul(m.bank(2 + b, half), ones[0:ROWT, :], both[:, b * half:(b + 1) * half],
                                       start=True, stop=True)
            ins.then_inc(sums_ready, 1)
            for t in range(NROWT):
                if t >= 2:
                    pe.wait_ge(rows_taken, t - 1)
                for k in range(KD):
                    ins = nc.tensor.transpose(m.ps[0:ROWT, (4 + t % 2) * BANK + k * P:(4 + t % 2) * BANK + (k + 1) * P],
                                              m.xn[:, k, t * ROWT:(t + 1) * ROWT], m.ident[:, :])
                ins.then_inc(rows_turned, 1)
            pe.wait_ge(experts_ready, 1)
            nc.tensor.transpose(m.ps[0:1, 7 * BANK:7 * BANK + TABLE], expert_col[0:TABLE, :],
                                m.ident[0:TABLE, 0:TABLE]).then_inc(experts_turned, 1)
            for a in range(pairs):
                pe.wait_ge(hot_ready, 2 * (a + 1))
                nc.tensor.matmul(m.ps[:, 6 * BANK:6 * BANK + TABLE], place_hot[a % 4], block_hot[a % 4],
                                 start=a == 0, stop=a == pairs - 1).then_inc(hot_used, 1)

        @block.scalar
        def _(act):
            for t in range(NROWT):
                act.wait_ge(rows_turned, t + 1)
                nc.scalar.copy(rows[:, t, :], m.bank(4 + t % 2, D, ROWT)).then_inc(rows_taken, 1)

        @block.sync
        def _(sp):
            sp.wait_ge(rows_taken, NROWT)
            sp.dma_start(x_rows.rearrange("(t p) n -> p t n", p=ROWT), rows).then_inc(rows_stored, 16)
            sp.wait_ge(rows_stored, 16)
            sp.wait_ge(m.y_cleared, 16)

        @block.vector
        def _(dve):
            link = linker(dve, step)
            tt, ts = nc.vector.tensor_tensor, nc.vector.tensor_scalar
            tt(both, one, two, ALU.add).then_inc(both_ready, 1)
            link(nc.vector.memset(before[:, 0:ne], 0.0))
            dve.wait_ge(sums_ready, 1)
            per_bank = NROWT // 2
            for t in range(NROWT):
                total = m.ps[:, (2 + t // per_bank) * BANK + (t % per_bank) * ne:][:, 0:ne]
                out = counts if t == NROWT - 1 else before[:, (t + 1) * ne:(t + 2) * ne]
                link(tt(out, before[:, t * ne:(t + 1) * ne], total, ALU.add))
            link(ts(n_blocks, counts, 1.0 / P, (P - 1.0) / P - FLOOR, ALU.mult, ALU.add))
            link(ts(n_blocks, n_blocks, MAGIC, -MAGIC, ALU.add, ALU.add))
            link(nc.vector.tensor_tensor_scan(ends, ones[:, 0:ne], n_blocks, 0.0, ALU.mult, ALU.add))
            link(tt(starts, ends, n_blocks, ALU.subtract))
            link(ts(hits, ends, place, None, ALU.is_le))
            link(nc.vector.tensor_reduce(expert_col, hits, AX_X, ALU.add))
            ts(expert_col, expert_col, ne - 1.0, None, ALU.min).then_inc(experts_ready, 1)
            link(ts(rounds_f, ends[0:1, ne - 1:ne], 0.25, 0.75 - 0.375, ALU.mult, ALU.add))
            link(ts(rounds_f, rounds_f, MAGIC, -MAGIC, ALU.add, ALU.add))
            link(nc.vector.tensor_copy(rounds, rounds_f))
            link(ts(starts, starts, float(P), None, ALU.mult))
            for b in range(2):
                link(tt(slot[:, b * half:(b + 1) * half], before[0:ROWT, b * half:(b + 1) * half],
                        m.bank(b, half, ROWT), ALU.add))
            link(tt(by_expert(slot), by_expert(slot),
                    starts[0:ROWT, :].unsqueeze(1).broadcast_to([ROWT, NROWT, ne]), ALU.add))
            for i, pick in enumerate((one, two)):
                link(tt(tmp, pick, slot, ALU.mult))
                link(nc.vector.tensor_reduce(pair_slot[:, i * g_all:(i + 1) * g_all], by_group(tmp), AX_X, ALU.add))
            link(nc.vector.tensor_copy(pair_idx, pair_slot))
            link(ts(pair_block, pair_slot, 1.0 / P, -FLOOR, ALU.mult, ALU.add))
            link(ts(pair_block, pair_block, MAGIC, -MAGIC, ALU.add, ALU.add))
            link(nc.vector.scalar_tensor_tensor(out=pair_place, in0=pair_block, scalar=-float(P), in1=pair_slot,
                                                op0=ALU.mult, op1=ALU.add))
            dve.wait_ge(experts_turned, 1)
            link(nc.vector.tensor_copy(block_expert, m.ps[0:1, 7 * BANK:7 * BANK + TABLE]))
            for a in range(pairs):
                if a >= 4:
                    dve.wait_ge(hot_used, a - 3)
                t = (a % g_all) // 2
                ts(place_hot[a % 4], iota[:, 0:P], pair_place[:, a:a + 1], None, ALU.is_equal).then_inc(hot_ready, 1)
                ts(block_hot[a % 4], iota[:, 0:TABLE], pair_block[:, a:a + 1], token[:, t:t + 1], ALU.is_equal,
                   ALU.mult).then_inc(hot_ready, 1)
            dve.wait_ge(hot_used, pairs)
            nc.vector.tensor_copy(slot_token, m.ps[:, 6 * BANK:6 * BANK + TABLE])
    return x_rows, y_rows, pair_idx, slot_token, block_expert, rounds


def run_blocks(nc, m, d, blocks):
    x_rows, y_rows, _, slot_token, block_expert, rounds = blocks
    ROUND = 4
    flat1 = m.big1[:, :, :].rearrange("p a b -> p (a b)")
    flat2 = m.big2[:, :, :].rearrange("p a b -> p (a b)")
    w = [flat1[:, i * 768:(i + 1) * 768] for i in range(ROUND)]
    xr = [flat1[:, 3072 + i * D:3072 + (i + 1) * D] for i in range(ROUND)]
    xt = [flat1[:, 4096 + i * D:4096 + (i + 1) * D] for i in range(ROUND)]
    gated = [flat2[:, i * P:(i + 1) * P] for i in range(ROUND)]
    hidden = [flat2[:, 512 + i * P:512 + (i + 1) * P] for i in range(ROUND)]
    y = [flat2[:, 1024 + i * D:1024 + (i + 1) * D] for i in range(ROUND)]
    idx = m.block_idx
    gathered = m.gathered
    experts = d["experts"].rearrange("e p n -> (e p) n")

    def value(i, r, more=0):
        return i * ROUND + (r + more)

    def wait(eng, sem, i, r, more):
        n = value(i, r, more)
        if not (isinstance(n, int) and n <= 0):
            eng.wait_ge(sem, n)

    def shifted_by(i, r, more):
        return i + (r + more) // ROUND, (r + more) % ROUND

    def all_rounds(eng, step, lead):
        for t in range(-lead, ROUND):
            step(t // ROUND, t % ROUND)
        n = eng.value_load(rounds, min_val=2, max_val=MAX_ROUNDS)
        with eng.Fori(1, n) as i:
            for r in range(ROUND):
                step(i, r)
        return n

    with stage(nc, "weights_0", "weights_1", "weights_2", "weights_3", "stored_0", "stored_1", "stored_2", "stored_3",
               "index_ready", "rows_turned", "xt_ready", "gate_ready", "silu_ready", "hidden_ready", "down_ready",
               "y_ready") as (
            block, weights_0, weights_1, weights_2, weights_3, stored_0, stored_1, stored_2, stored_3, index_ready,
            rows_turned, xt_ready, gate_ready, silu_ready, hidden_ready, down_ready, y_ready):
        weights = (weights_0, weights_1, weights_2, weights_3)
        stored = (stored_0, stored_1, stored_2, stored_3)

        @block.sync
        def _(sp):
            def cleared():
                sp.wait_ge(m.y_cleared, 16)

            def load_expert(i, r):
                e = sp.value_load(block_expert[0:1, bass.ds(value(i, r), 1)], min_val=0, max_val=2 * E0 - 1)
                at = sp.snap(e * P)
                wait(sp, down_ready, i, r, 1 - ROUND)
                cleared()
                sp.dma_start(w[r], experts[bass.ds(at, P), :]).then_inc(weights[r], 16)

            def step(i, r):
                n = value(i, r)
                if not isinstance(n, int) or n >= 0:
                    at = n * P if isinstance(n, int) else sp.snap(n * P)
                    wait(sp, y_ready, i, r, 1)
                    cleared()
                    sp.dma_start(y_rows[bass.ds(at, P), :], y[r]).then_inc(stored[r], 16)
                load_expert(*shifted_by(i, r, ROUND))
            all_rounds(sp, step, ROUND)

        @block.gpsimd
        def _(pool):
            def gather(i, r):
                wait(pool, rows_turned, i, r, 1 - ROUND)
                nc.gpsimd.tensor_copy(idx[r], slot_token[:, bass.ds(value(i, r), 1)]).then_inc(index_ready, 1)
                wait(pool, index_ready, i, r, 1)
                nc.gpsimd.tensor_tensor(m.idle, m.idle, m.idle, ALU.add)
                pool.indirect_dma_start(xr[r], None, x_rows, bass.IndirectOffsetOnAxis(ap=idx[r], axis=0)).then_inc(
                    gathered[r], 16)

            def step(i, r):
                gather(*shifted_by(i, r, ROUND))
            n = all_rounds(pool, step, ROUND)
            for r in range(ROUND):
                pool.wait_ge(gathered[r], n * 16 + 16)
                pool.wait_ge(weights[r], n * 16 + 16)
                pool.wait_ge(stored[r], n * 16)

        @block.tensor
        def _(pe):
            def turn(i, r):
                pe.wait_ge(gathered[r], i * 16 + 16)
                wait(pe, xt_ready, i, r, -1)
                for k in range(KD):
                    to = (r % 2) * BANK + k * P
                    ins = nc.tensor.transpose(m.ps[:, to:to + P], xr[r][:, k * P:(k + 1) * P], m.ident[:, :])
                ins.then_inc(rows_turned, 1)

            def gate_up(i, r):
                pe.wait_ge(weights[r], i * 16 + 16)
                wait(pe, xt_ready, i, r, 1)
                wait(pe, hidden_ready, i, r, -1)
                for half in range(2):
                    to = (2 + r % 2) * BANK + half * P
                    for k in range(KD):
                        ins = nc.tensor.matmul(m.ps[:, to:to + P], w[r][:, half * D + k * P:half * D + (k + 1) * P],
                                               xt[r][:, k * P:(k + 1) * P], start=k == 0, stop=k == KD - 1)
                ins.then_inc(gate_ready, 1)

            def down(i, r):
                wait(pe, hidden_ready, i, r, 1)
                wait(pe, y_ready, i, r, -1)
                nc.tensor.matmul(m.bank(4 + r % 2, D), hidden[r], w[r][:, 2 * D:3 * D], start=True,
                                 stop=True).then_inc(down_ready, 1)

            def step(i, r):
                turn(*shifted_by(i, r, 2))
                n = value(i, r, 1)
                if not isinstance(n, int) or n >= 0:
                    gate_up(*shifted_by(i, r, 1))
                n = value(i, r)
                if not isinstance(n, int) or n >= 0:
                    down(i, r)
            all_rounds(pe, step, 2)

        @block.scalar
        def _(act):
            def step(i, r):
                n = value(i, r, 1)
                if not isinstance(n, int) or n >= 0:
                    i1, r1 = shifted_by(i, r, 1)
                    wait(act, gate_ready, i1, r1, 1)
                    wait(act, hidden_ready, i1, r1, 1 - ROUND)
                    nc.scalar.activation(gated[r1], m.ps[:, (2 + r1 % 2) * BANK:(2 + r1 % 2) * BANK + P],
                                         ACT.Silu).then_inc(silu_ready, 1)
                n = value(i, r)
                if not isinstance(n, int) or n >= 0:
                    wait(act, down_ready, i, r, 1)
                    if not isinstance(i, int) or i >= 1:
                        act.wait_ge(stored[r], i * 16)
                    nc.scalar.copy(y[r], m.bank(4 + r % 2, D)).then_inc(y_ready, 1)
            all_rounds(act, step, 1)

        @block.vector
        def _(dve):
            def step(i, r):
                i2, r2 = shifted_by(i, r, 2)
                wait(dve, rows_turned, i2, r2, 1)
                wait(dve, gate_ready, i2, r2, 1 - ROUND)
                nc.vector.tensor_copy(xt[r2], m.bank(r2 % 2, D)).then_inc(xt_ready, 1)
                n = value(i, r, 1)
                if not isinstance(n, int) or n >= 0:
                    i1, r1 = shifted_by(i, r, 1)
                    wait(dve, silu_ready, i1, r1, 1)
                    wait(dve, down_ready, i1, r1, 1 - ROUND)
                    at = (2 + r1 % 2) * BANK + P
                    nc.vector.tensor_tensor(hidden[r1], gated[r1], m.ps[:, at:at + P], ALU.mult).then_inc(
                        hidden_ready, 1)
            all_rounds(dve, step, 2)


def combine(nc, m, blocks):
    _, y_rows, pair_idx, _, _, _ = blocks
    g_all = 2 * NROWT
    flat2 = m.big2[:, :, :].rearrange("p a b -> p (a b)")
    ring = 16
    got = [flat2[0:ROWT, i * D:(i + 1) * D] for i in range(ring)]
    diag = [flat2[0:ROWT, ring * D + i * P:ring * D + i * P + ROWT] for i in range(8)]
    weight = [m.small[0:ROWT, 32 * i:32 * i + g_all] for i in range(2)]
    order = [(t, choice * g_all + 2 * t + g) for t in range(NROWT) for choice in range(2) for g in range(2)]
    with stage(nc, "diag_ready", "used", "sum_taken") as (block, diag_ready, used, sum_taken):

        @block.gpsimd
        def _(pool):
            for n, (_, a) in enumerate(order):
                if n >= ring:
                    pool.wait_ge(used, n - ring + 1)
                pool.indirect_dma_start(got[n % ring], None, y_rows, bass.IndirectOffsetOnAxis(
                    ap=pair_idx[:, a:a + 1], axis=0)).then_inc(m.fetched[n % ring], 16)

        @block.vector
        def _(dve):
            def diagonal(n):
                a = order[n][1]
                if n >= 8:
                    dve.wait_ge(used, n - 7)
                nc.vector.tensor_scalar(diag[n % 8], m.ident[0:ROWT, 0:ROWT],
                                        weight[a // g_all][:, a % g_all:a % g_all + 1], None,
                                        ALU.mult).then_inc(diag_ready, 1)
            for n in range(4):
                diagonal(n)
            for t in range(NROWT):
                if t + 1 < NROWT:
                    for n in range(4 * t + 4, 4 * t + 8):
                        diagonal(n)
                dve.wait_ge(used, 4 * (t + 1))
                out = m.h[:, :, t * ROWT:(t + 1) * ROWT]
                nc.vector.tensor_tensor(out, out, m.ps[:, (t % 2) * BANK:(t % 2) * BANK + KD * ROWT].rearrange(
                    "p (k n) -> p k n", k=KD), ALU.add).then_inc(sum_taken, 1)

        @block.tensor
        def _(pe):
            for t in range(NROWT):
                if t >= 2:
                    pe.wait_ge(sum_taken, t - 1)
                for q in range(4):
                    n = 4 * t + q
                    pe.wait_ge(m.fetched[n % ring], 16 * (n // ring + 1))
                    pe.wait_ge(diag_ready, n + 1)
                    for k in range(KD):
                        to = (t % 2) * BANK + k * ROWT
                        ins = nc.tensor.matmul(m.ps[:, to:to + ROWT], got[n % ring][:, k * P:(k + 1) * P],
                                               diag[n % 8], start=q == 0 and k == 0, stop=q == 3,
                                               skip_group_check=True)
                    ins.then_inc(used, 1)


def value_room(m):
    return m.big1[:, :, :].rearrange("p a b -> p (a b)")[0:SEQ, 4 * N:4 * N + BATCH * D].rearrange(
        "p (b n) -> p b n", b=BATCH)


def value_rows(nc, m, w_v, v):
    banks = (3, 4, 5, 0)

    def multiply(pe, normed, rows_ready, rows_taken):
        for b in range(BATCH):
            if b >= 4:
                pe.wait_ge(rows_taken, b - 3)
            for k in range(KD):
                ins = nc.tensor.matmul(m.bank(banks[b % 4], D, SEQ), m.xn[:, k, b * SEQ:(b + 1) * SEQ], w_v(k),
                                       start=k == 0, stop=k == KD - 1)
            ins.then_inc(rows_ready, 1)

    def take(act, normed, rows_ready, rows_taken):
        for b in range(BATCH):
            act.wait_ge(rows_ready, b + 1)
            nc.scalar.copy(v[:, b, :], m.bank(banks[b % 4], D, SEQ)).then_inc(rows_taken, 1)

    return ("rows_ready", "rows_taken"), multiply, take, None


def attend(nc, m, mask, v_bias, topk):
    q, k = m.big1[:, 0:2, :], m.big1[:, 2:4, :]
    v = value_room(m)
    flat2 = m.big2[:, :, :].rearrange("p a b -> p (a b)")
    used = [0]

    def room(rows, n, copies):
        start = used[0]
        used[0] += n * copies
        return [flat2[0:rows, start + i * n:start + (i + 1) * n] for i in range(copies)]

    q_out = room(P, QSET, 2)
    PAIR = 2 * HD
    v_out = room(SEQ, HPC * PAIR, 2)
    turned_sb = room(SEQ, HPC * SEQ, 2)
    score = room(P, NQT * SEQ, 4)
    left = room(P, NHARD * SEQ, 2)
    top8 = [a.rearrange("p (j r e) -> p j r e", j=NHARD, r=TOPK // 8) for a in room(P, NHARD * TOPK, 2)]
    head_of = m.head_of[:, :]
    row_max, row_sum = room(P, 8, 4), room(P, 8, 4)
    att = m.s3
    easy = 2 * SEQ
    tile3 = lambda a: a.rearrange("p (j n) -> p j n", n=SEQ)
    wide = lambda a: a.unsqueeze(2).broadcast_to([P, NQT, SEQ])
    steps, ROUND = 2 * BATCH, 4

    def value(i, r, more=0):
        return i * ROUND + (r + more)

    def wait(eng, sem, i, r, more):
        n = value(i, r, more)
        if not (isinstance(n, int) and n <= 0):
            eng.wait_ge(sem, n)

    def batch(i, r):
        return bass.ds((i * 2 + r // 2) * SEQ, SEQ)

    def rounds(eng, step, lead=2):
        for t in range(-lead, ROUND):
            step(t // ROUND, t % ROUND)
        with eng.Fori(1, steps // ROUND - 1) as i:
            for r in range(ROUND):
                step(i, r)
        for t in range(steps - ROUND, steps + 1):
            step(t // ROUND, t % ROUND)

    def has(i, r, more):
        n = value(i, r, more)
        return not isinstance(n, int) or 0 <= n < steps

    def shifted_by(i, r, more):
        return i + (r + more) // ROUND, (r + more) % ROUND

    with stage(nc, "cleared", "q_out_ready", "v_out_ready", "scores_ready", "scores_taken", "shifted", "exp_ready",
               "weights_ready", "turned", "turned_taken", "out_ready", "out_taken", "shift_step",
               "divide_step", "total_ready") as (
            block, cleared, q_out_ready, v_out_ready, scores_ready, scores_taken, shifted, exp_ready, weights_ready,
            turned, turned_taken, out_ready, out_taken, shift_step, divide_step,
            total_ready):

        @block.gpsimd
        def _(pool):
            for c in range(2):
                nc.gpsimd.memset(q_out[c], 0.0)
                nc.gpsimd.memset(v_out[c], 0.0).then_inc(cleared, 1)
            pool.wait_ge(cleared, 2)

            def set_out_queries(i, r):
                c = r % 2
                wait(pool, scores_ready, i, r, -1)
                for first, n, at in ((0, EASY, 0), (EASY, HARD, HPC * EASY)):
                    o = (i * 2 + r // 2) * SEQ + first
                    ins = nc.gpsimd.tensor_tensor(
                        q_out[c][:, at:at + HPC * n].rearrange("p (h t) -> p h t", h=HPC),
                        q[:, c:c + 1, bass.ds(o, n)].broadcast_to([P, HPC, n]),
                        head_of.unsqueeze(2).broadcast_to([P, HPC, n]), ALU.mult)
                ins.then_inc(q_out_ready, 1)

            def set_out_values(i, r):
                c = r % 2
                wait(pool, out_ready, i, r, -1)
                row = v[:, bass.ds(i * 2 + r // 2, 1), c * P:(c + 1) * P].squeeze(1)
                for odd in range(2):
                    ins = nc.gpsimd.tensor_copy(
                        v_out[c].rearrange("p (h n) -> p h n", n=2 * PAIR)[:, :, odd * (PAIR + HD):][:, :, 0:HD],
                        row.rearrange("p (h n) -> p h n", n=PAIR)[:, :, odd * HD:(odd + 1) * HD])
                ins.then_inc(v_out_ready, 1)

            def subtract_max(i, r):
                wait(pool, shift_step, i, r, 1)
                s = tile3(score[r])
                nc.gpsimd.tensor_tensor(s[:, 0:2, :], s[:, 0:2, :], row_max[r][:, 0:2].unsqueeze(2).broadcast_to(
                    [P, 2, SEQ]), ALU.subtract)
                high = top8[r % 2][:, :, 0, 0:1].broadcast_to([P, NHARD, SEQ])
                nc.gpsimd.tensor_tensor(s[:, 2:, :], s[:, 2:, :], high, ALU.subtract).then_inc(shifted, 1)

            def divide(i, r):
                wait(pool, total_ready, i, r, 1)
                s = tile3(score[r])
                nc.gpsimd.tensor_tensor(s, s, wide(row_sum[r][:, 0:NQT]), ALU.mult).then_inc(weights_ready, 1)

            def step(i, r):
                if has(i, r, 3):
                    set_out_queries(*shifted_by(i, r, 3))
                if has(i, r, 0):
                    if topk:
                        divide(i, r)
                    set_out_values(i, r)
                if topk and has(i, r, 2):
                    subtract_max(*shifted_by(i, r, 2))
            rounds(pool, step, 3)

        @block.tensor
        def _(pe):
            def scores(i, r):
                c = r % 2
                wait(pe, q_out_ready, i, r, 1)
                wait(pe, scores_taken, i, r, -1)
                if topk:
                    nc.tensor.matmul(m.bank(c, NQT * SEQ), m.ident[:, :], mask, start=True, stop=False,
                                     skip_group_check=True)
                for j in range(NQT):
                    ins = nc.tensor.matmul(m.ps[:, c * BANK + j * SEQ:c * BANK + (j + 1) * SEQ],
                                           q_out[c][:, QAT[j]:QAT[j] + P], k[:, c, batch(i, r)], start=not topk,
                                           stop=True, skip_group_check=topk)
                ins.then_inc(scores_ready, 1)

            def turn(i, r):
                wait(pe, weights_ready, i, r, 1)
                wait(pe, turned_taken, i, r, -1)
                for j in range(NQT):
                    to = (2 + 2 * (r % 2)) * BANK + j * P
                    ins = nc.tensor.transpose(m.ps[0:SEQ, to:to + P], score[r][:, j * SEQ:(j + 1) * SEQ],
                                              m.ident[:, :])
                ins.then_inc(turned, 1)

            def output(i, r):
                c = r % 2
                wait(pe, turned_taken, i, r, 1)
                wait(pe, v_out_ready, i, r, 1)
                wait(pe, out_taken, i, r, -1)
                for h in range(HPC):
                    at = PAIR * (h // 2)
                    ins = nc.tensor.matmul(m.ps[at:at + PAIR, (6 + c) * BANK:(6 + c) * BANK + SEQ],
                                           v_out[c][:, h * PAIR:(h + 1) * PAIR],
                                           turned_sb[c][:, h * SEQ:(h + 1) * SEQ], start=h % 2 == 0, stop=h % 2 == 1)
                ins.then_inc(out_ready, 1)

            def step(i, r):
                if has(i, r, 2):
                    scores(*shifted_by(i, r, 2))
                if has(i, r, 0):
                    turn(i, r)
                if has(i, r, -1):
                    output(*shifted_by(i, r, -1))
            rounds(pe, step)

        @block.scalar
        def _(act):
            def exp(i, r):
                wait(act, shifted, i, r, 1)
                nc.scalar.activation(score[r], score[r], ACT.Exp).then_inc(exp_ready, 1)

            def take_turned(i, r):
                wait(act, turned, i, r, 1)
                wait(act, out_ready, i, r, -1)
                at = (2 + 2 * (r % 2)) * BANK
                by_head = turned_sb[r % 2].rearrange("p (h n) -> p h n", h=HPC)
                nc.scalar.copy(by_head[:, :, 0:EASY],
                               m.ps[0:SEQ, at:at + 2 * P].rearrange("p (h n) -> p h n", h=HPC))
                for j, (h, n) in enumerate(HARD_HEADS):
                    o = at + (2 + j) * P
                    ins = nc.scalar.copy(by_head[:, h:h + n, EASY:SEQ],
                                         m.ps[0:SEQ, o:o + n * HARD].rearrange("p (h n) -> p h n", h=n))
                ins.then_inc(turned_taken, 1)

            def take_output(i, r):
                c = r % 2
                wait(act, out_ready, i, r, 1)
                nc.scalar.activation(att[:, c, batch(i, r)], m.bank(6 + c, SEQ), ACT.Identity,
                                     bias=v_bias(c)).then_inc(out_taken, 1)

            def take_scores(i, r):
                wait(act, scores_ready, i, r, 1)
                wait(act, turned, i, r, -3)
                nc.scalar.copy(score[r], m.bank(r % 2, NQT * SEQ)).then_inc(scores_taken, 1)

            def step(i, r):
                if has(i, r, 1):
                    exp(*shifted_by(i, r, 1))
                if topk and has(i, r, 2):
                    take_scores(*shifted_by(i, r, 2))
                if has(i, r, 0):
                    take_turned(i, r)
                if has(i, r, -1):
                    take_output(*shifted_by(i, r, -1))
            rounds(act, step)

        @block.vector
        def _(dve):
            divide_steps = 2

            def shift(i, r):
                wait(dve, scores_ready, i, r, 1)
                wait(dve, turned, i, r, -3)
                nc.vector.tensor_tensor(score[r], m.bank(r % 2, NQT * SEQ), mask, ALU.add).then_inc(scores_taken, 1)
                wait(dve, scores_taken, i, r, 1)
                s = tile3(score[r])
                high = row_max[r][:, 0:NQT]
                nc.vector.tensor_reduce(high, s, AX_X, ALU.max).then_inc(shift_step, 1)
                wait(dve, shift_step, i, r, 1)
                nc.vector.tensor_tensor(s, s, wide(high), ALU.subtract).then_inc(shifted, 1)

            def mark_top(i, r):
                c = r % 2
                wait(dve, scores_taken, i, r, 1)
                wait(dve, shifted, i, r, -1)
                s = tile3(score[r])
                nc.vector.tensor_reduce(row_max[r][:, 0:2], s[:, 0:2, :], AX_X, ALU.max)
                for e in range(TOPK // 8):
                    of = score[r][:, easy:] if e == 0 else left[c]
                    for j in range(NHARD):
                        nc.vector.max(top8[c][:, j, e, :], of[:, j * SEQ:(j + 1) * SEQ])
                    nc.vector.drain()
                    for j in range(NHARD):
                        ins = nc.vector.match_replace(left[c][:, j * SEQ:(j + 1) * SEQ], top8[c][:, j, e, :],
                                                      of[:, j * SEQ:(j + 1) * SEQ], TAKEN)
                    if e == 0:
                        ins.then_inc(shift_step, 1)
                    nc.vector.drain()

            def divide(i, r):
                link = linker(dve, divide_step, value(i, r) * divide_steps)
                wait(dve, exp_ready, i, r, 1)
                s = tile3(score[r])
                total = row_sum[r][:, 0:NQT]
                if topk:
                    hard = score[r][:, easy:]
                    link(nc.vector.scalar_tensor_tensor(out=hard, in0=left[r % 2], scalar=-1e35, in1=hard,
                                                        op0=ALU.is_lt, op1=ALU.mult))
                link(nc.vector.tensor_reduce(total, s, AX_X, ALU.add))
                if topk:
                    nc.vector.reciprocal(total, total).then_inc(total_ready, 1)
                    return
                link(nc.vector.reciprocal(total, total))
                nc.vector.tensor_tensor(s, s, wide(total), ALU.mult).then_inc(weights_ready, 1)

            def step(i, r):
                if has(i, r, 0):
                    divide(i, r)
                if has(i, r, 2):
                    (mark_top if topk else shift)(*shifted_by(i, r, 2))
            rounds(dve, step)


def project(nc, m, w_out, bias):
    linear(nc, m, full(m.s3), lambda k, j: w_out[:, k, j * P:j * P + P], KD, KD, CHUNKS, add_to(nc, m, m.h, bias),
           on="vector")


def queries_and_keys(nc, m, w_q, w_k, b_q, b_k, scale, landed):
    def drain(j, o, n, acc, link):
        out = m.big1[:, j, o:o + n]
        if j < KD:
            return nc.vector.tensor_scalar(out, acc, b_q(j), scale, ALU.add, ALU.mult)
        return nc.vector.tensor_scalar(out, acc, b_k(j - KD), None, ALU.add)
    return Products(lambda k, j: w_q(k, j) if j < KD else w_k(k, j - KD), 2 * KD, drain, landed, on="vector")


def fetch_attention1(sp, m, d):
    fetch(sp, m, "attention1", (m.wa[:, 0:KD * 3 * D], d["c_attn"]), (m.wa[:, 1536:2048], d["c_proj"]))


def attention1(nc, m, d):
    w = m.wa[:, 0:KD * 3 * D].rearrange("p (k n) -> p k n", k=KD)
    w_o = m.wa[:, 1536:2048].rearrange("p (k n) -> p k n", k=KD)
    layernorm(nc, m, full(m.h), full(m.xn), CHUNKS, ahead=lambda sp: fetch_attention2(sp, m, d),
              then=queries_and_keys(
                  nc, m, lambda k, j: w[:, k, j * P:j * P + P], lambda k, j: w[:, k, D + j * P:D + j * P + P],
                  lambda j: m.v("c_attn_b", j), lambda j: m.v("c_attn_b", 2 + j), HD ** -0.5,
                  (m.landed["attention1"], 16 * 2)),
              behind=value_rows(nc, m, lambda k: w[:, k, 2 * D:3 * D], value_room(m)))
    attend(nc, m, m.mask1[:, :], lambda c: m.v("c_attn_b", 4 + c), False)
    project(nc, m, w_o, lambda j: m.v("c_proj_b", j))


def qkvo(m, at):
    return [m.wa[:, at + i * 512:at + (i + 1) * 512].rearrange("p (k n) -> p k n", k=KD) for i in range(4)]


def fetch_qkvo(sp, m, d, name, of, at):
    fetch(sp, m, name, *[(w, d[of + part]) for w, part in zip(qkvo(m, at), ("Wq", "Wk", "Wv", "Wo"))])


def fetch_attention2(sp, m, d):
    fetch_qkvo(sp, m, d, "attention2", "L2", 4096)


def fetch_attention3(sp, m, d):
    fetch_qkvo(sp, m, d, "attention3", "L3", 0)


def attention3(nc, m, d):
    w_q, w_k, w_v, w_o = qkvo(m, 0)
    layernorm(nc, m, full(m.h), full(m.xn), CHUNKS, ahead=lambda sp: fetch_mixture3(sp, m, d),
              then=queries_and_keys(
                  nc, m, lambda k, j: w_q[:, k, j * P:j * P + P], lambda k, j: w_k[:, k, j * P:j * P + P],
                  lambda j: m.v("bq", j), lambda j: m.v("bk", j), HD ** -0.5, (m.landed["attention3"], 16 * 4)),
              behind=value_rows(nc, m, lambda k: w_v[:, k, :], value_room(m)))
    attend(nc, m, m.mask3[:, :], lambda c: m.v("bv", c), True)
    project(nc, m, w_o, lambda j: m.v("bo", j))


def attention2(nc, m, d):
    w_q, w_k, w_v, w_o = qkvo(m, 4096)
    layernorm(nc, m, full(m.h), full(m.xn), CHUNKS,
              then=queries_and_keys(
                  nc, m, lambda k, j: w_q[:, k, j * P:j * P + P], lambda k, j: w_k[:, k, j * P:j * P + P],
                  lambda j: m.v("Wq_b", j), lambda j: m.v("Wk_b", j), D ** -0.5, (m.landed["attention2"], 16 * 4)),
              behind=value_rows(nc, m, lambda k: w_v[:, k, :], value_room(m)))
    v = value_room(m)
    q, k = m.big1[:, 0:2, :], m.big1[:, 2:4, :]
    flat2 = m.big2[:, :, :].rearrange("p a b -> p (a b)")
    G = 4
    W = G * SEQ
    score = [flat2[0:SEQ, g * W:(g + 1) * W] for g in range(BATCH // G)]
    turned_sb = [flat2[0:SEQ, 1200 + g * W:1200 + (g + 1) * W] for g in range(BATCH // G)]
    mask = m.mask2[:, :]
    red = [flat2[0:SEQ, 2500 + 8 * g:2500 + 8 * g + G] for g in range(BATCH // G)]
    att = m.s3
    with stage(nc, "scores_ready", "abs_ready", "step", "shifted", "exp_ready", "weights_ready", "turned",
               "turned_taken", "out_ready", "out_taken") as (
            block, scores_ready, abs_ready, step, shifted, exp_ready, weights_ready, turned, turned_taken, out_ready,
            out_taken):
        wide = lambda a: a.unsqueeze(2).broadcast_to([SEQ, G, SEQ])
        tiles = range(BATCH // G)

        @block.tensor
        def _(pe):
            for g in tiles:
                for i in range(G):
                    o = (g * G + i) * SEQ
                    for c in range(KD):
                        ins = nc.tensor.matmul(m.ps[0:SEQ, g * BANK + i * SEQ:g * BANK + (i + 1) * SEQ],
                                               q[:, c, o:o + SEQ], k[:, c, o:o + SEQ], start=c == 0, stop=c == KD - 1)
                ins.then_inc(scores_ready, 1)
            for g in tiles:
                pe.wait_ge(weights_ready, g + 1)
                if g >= 2:
                    pe.wait_ge(turned_taken, g - 1)
                b4 = 4 + g % 2
                for i in range(G):
                    ins = nc.tensor.transpose(m.ps[0:SEQ, b4 * BANK + i * SEQ:b4 * BANK + (i + 1) * SEQ],
                                              score[g][:, i * SEQ:(i + 1) * SEQ], m.ident[0:SEQ, 0:SEQ])
                ins.then_inc(turned, 1)
                pe.wait_ge(turned_taken, g + 1)
                if g >= 1:
                    pe.wait_ge(out_taken, 2 * g)
                for c in range(KD):
                    for i in range(G):
                        ins = nc.tensor.matmul(m.ps[:, (6 + c) * BANK + i * SEQ:(6 + c) * BANK + (i + 1) * SEQ],
                                               v[:, g * G + i, c * P:(c + 1) * P],
                                               turned_sb[g][:, i * SEQ:(i + 1) * SEQ], start=True, stop=True)
                    ins.then_inc(out_ready, 1)

        @block.scalar
        def _(act):
            for g in tiles:
                act.wait_ge(scores_ready, g + 1)
                nc.scalar.activation(score[g], m.bank(g, W, SEQ), ACT.Abs).then_inc(abs_ready, 1)
            for g in tiles:
                act.wait_ge(shifted, g + 1)
                nc.scalar.activation(score[g], score[g], ACT.Exp).then_inc(exp_ready, 1)
            for g in tiles:
                act.wait_ge(turned, g + 1)
                nc.scalar.copy(turned_sb[g], m.bank(4 + g % 2, W, SEQ)).then_inc(turned_taken, 1)
                for c in range(KD):
                    act.wait_ge(out_ready, 2 * g + c + 1)
                    nc.scalar.activation(att[:, c, g * W:(g + 1) * W], m.bank(6 + c, W), ACT.Identity,
                                         bias=m.v("Wv_b", c)).then_inc(out_taken, 1)

        @block.vector
        def _(dve):
            link = linker(dve, step)
            for g in tiles:
                dve.wait_ge(abs_ready, g + 1)
                s = score[g].rearrange("p (i n) -> p i n", i=G)
                link(nc.vector.tensor_tensor(s, s, mask.unsqueeze(1).broadcast_to([SEQ, G, SEQ]), ALU.add))
                link(nc.vector.tensor_reduce(red[g], s, AX_X, ALU.max))
                nc.vector.tensor_tensor(s, s, wide(red[g]), ALU.subtract).then_inc(shifted, 1)
            for g in tiles:
                dve.wait_ge(exp_ready, g + 1)
                s = score[g].rearrange("p (i n) -> p i n", i=G)
                link(nc.vector.tensor_reduce(red[g], s, AX_X, ALU.add))
                link(nc.vector.reciprocal(red[g], red[g]))
                nc.vector.tensor_tensor(s, s, wide(red[g]), ALU.mult).then_inc(weights_ready, 1)
    project(nc, m, w_o, lambda j: m.v("Wo_b", j))


def mlp(m, w1, w2, activate, add, landed, beside=None):
    return Products(lambda k, j: w1[:, k, j * P:j * P + P], 8, activate, landed, hidden=m.big2,
                    second_w=lambda k, j: w2[:, k, j * P:j * P + P], second_drain=add, second_landed=landed,
                    beside=beside)


def ternary_input(m):
    fc = m.wb[:, 0:2048].rearrange("p (k n) -> p k n", k=8)
    proj = m.wb[:, 2048:4096].rearrange("p (k n) -> p k n", k=2)
    fast_b, v, u = m.wb[0:16, 4096:4112], m.wb[0:16, 4112:4112 + D], m.wb[0:16, 4400:4400 + FF]
    return fc, proj, fast_b, v, u


def fetch_ternary(sp, m, d):
    fetch(sp, m, "ternary", *zip(ternary_input(m), (d["w_fc"], d["w_proj"], d["fast_b"], d["v"], d["uT"])))


def ternary_mlp(nc, m, d):
    flat1 = m.big1[:, :, :].rearrange("p a b -> p (a b)")
    fc, proj, fast_b, v, u = ternary_input(m)
    tmp_fc = flat1[:, 4096:6144].rearrange("p (k n) -> p k n", k=8)
    tmp_proj = flat1[:, 6144:8192].rearrange("p (k n) -> p k n", k=2)
    mid = m.s1[0:16, 1, 0:FF]
    scale_fc, scale_proj = flat1[:, 8500:8516], flat1[:, 8520:8524]
    w1 = m.wa[:, 0:2048].rearrange("p (k n) -> p k n", k=KD)
    w2 = m.wa[:, 2048:4096].rearrange("p (k n) -> p k n", k=8)
    layers = ((fc, tmp_fc, scale_fc, D), (proj, tmp_proj, scale_proj, FF))
    with stage(nc, "step", "inverse_ready", "divided", "summed", "scaled", "mid_ready", "mid_taken", "turned",
               "turned_taken") as (
            block, step, inverse_ready, divided, summed, scaled, mid_ready, mid_taken, turned, turned_taken):

        @block.scalar
        def _(act):
            def scale_rows(i, of, by, sem):
                tmp = layers[i][1]
                for t in range(of.shape[1]):
                    ins = nc.scalar.activation(tmp[:, t, :], of[:, t, :], ACT.Copy, scale=by[:, t:t + 1])
                ins.then_inc(sem, 1)

            for i, (w, tmp, scale, _) in enumerate(layers):
                tiles = w.shape[1]
                act.wait_ge(inverse_ready, i + 1)
                scale_rows(i, w, scale[:, tiles:2 * tiles], divided)
            for i, (w, tmp, scale, _) in enumerate(layers):
                act.wait_ge(summed, i + 1)
                scale_rows(i, tmp, scale[:, 0:w.shape[1]], scaled)

        @block.tensor
        def _(pe):
            pe.wait_ge(m.landed["ternary"], 16 * 5)
            for c in range(2):
                nc.tensor.matmul(m.bank(c, BANK, 16), fast_b, u[:, c * BANK:(c + 1) * BANK], start=True,
                                 stop=True).then_inc(mid_ready, 1)
            pe.wait_ge(mid_taken, 2)
            pe.wait_ge(scaled, 1)
            for k in range(KD):
                for c in range(2):
                    b = 2 + 2 * k + c
                    for i in range(4):
                        j = 4 * c + i
                        to = m.ps[:, b * BANK + i * P:b * BANK + (i + 1) * P]
                        nc.tensor.matmul(to, tmp_fc[:, j, k * P:(k + 1) * P], m.ident[:, :], start=True, stop=False)
                        ins = nc.tensor.matmul(to, v[:, k * P:(k + 1) * P], mid[:, j * P:(j + 1) * P], start=False,
                                               stop=True)
                    ins.then_inc(turned, 1)
            pe.wait_ge(scaled, 2)
            for g in range(4):
                b = 2 + g
                pe.wait_ge(turned_taken, g + 1)
                for i in range(2):
                    for j in range(2):
                        k = 2 * g + i
                        to = m.ps[:, b * BANK + (2 * i + j) * P:b * BANK + (2 * i + j + 1) * P]
                        ins = nc.tensor.transpose(to, tmp_proj[:, j, k * P:(k + 1) * P], m.ident[:, :])
                ins.then_inc(turned, 1)

        @block.vector
        def _(dve):
            link = linker(dve, step)
            dve.wait_ge(m.landed["ternary"], 16 * 5)
            for w, tmp, scale, width in layers:
                tiles = w.shape[1]
                sc, inv = scale[:, 0:tiles], scale[:, tiles:2 * tiles]
                link(nc.vector.tensor_reduce(sc, w, AX_X, ALU.add, apply_absolute_value=True))
                link(nc.vector.tensor_scalar(sc, sc, 1.0 / width, 1e-5, ALU.mult, ALU.max))
                nc.vector.reciprocal(inv, sc).then_inc(inverse_ready, 1)

            def round_and_sum(i):
                w, tmp, _, _ = layers[i]
                dve.wait_ge(divided, i + 1)
                link(nc.vector.tensor_scalar(tmp, tmp, MAGIC, -MAGIC, ALU.add, ALU.add))
                link(nc.vector.tensor_scalar(tmp, tmp, -1.0, 1.0, ALU.max, ALU.min))
                link(nc.vector.tensor_tensor(tmp, tmp, w, ALU.subtract))
                nc.vector.tensor_tensor(tmp, w, tmp, ALU.add).then_inc(summed, 1)

            round_and_sum(0)
            for c in range(2):
                dve.wait_ge(mid_ready, c + 1)
                nc.vector.tensor_scalar(mid[:, c * BANK:(c + 1) * BANK], m.bank(c, BANK, 16),
                                        m.vec[0:16, VEC["gate"][0]:VEC["gate"][0] + 1], None,
                                        ALU.mult).then_inc(mid_taken, 1)
            round_and_sum(1)
            for g in range(4):
                dve.wait_ge(turned, g + 1)
                k, c = divmod(g, 2)
                nc.vector.tensor_copy(w1[:, k, c * BANK:(c + 1) * BANK], m.bank(2 + g)).then_inc(turned_taken, 1)
            for g in range(4):
                dve.wait_ge(turned, 5 + g)
                nc.vector.tensor_copy(w2[:, 2 * g:2 * g + 2, :].rearrange("p k n -> p (k n)"), m.bank(2 + g))
    def relu_squared(j, o, n, acc, link):
        out = m.big2[:, j, o:o + n]
        link(nc.scalar.activation(out, acc, ACT.Relu))
        return nc.scalar.activation(out, out, ACT.Square)
    layernorm(nc, m, full(m.h), full(m.xn), CHUNKS, ahead=lambda sp: fetch_dequantised(sp, m, d),
              then=mlp(m, w1, w2, relu_squared, add_to(nc, m, m.h), (m.landed["ternary"], 16 * 5),
                       beside=((m.landed["dequantised"], 16 * 4), lambda: dequantise(nc, m))))


def dequantised_input(m):
    return (m.wb[:, 0:2048], m.wb[:, 2048:4096], m.wb[:, 4096:6144].rearrange("p (k n) -> p k n", k=KD),
            m.wa[:, 6144:8192].rearrange("p (k n) -> p k n", k=8))


def fetch_dequantised(sp, m, d):
    q1, q2, s1, s2 = dequantised_input(m)
    fetch(sp, m, "dequantised", (q1.bitcast(I32), d["fc1_q"]), (q2.bitcast(I32), d["fc2_q"]),
          (s1, d["fc1_s"].unsqueeze(0).broadcast_to([P, KD, FF])),
          (s2, d["fc2_s"].unsqueeze(0).broadcast_to([P, 8, D])))


def dequantise(nc, m):
    w1, w2, s1, s2 = dequantised_input(m)
    for w, s, k in ((w1, s1, KD), (w2, s2, 8)):
        w = w.rearrange("p (k n) -> p k n", k=k)
        nc.vector.scalar_tensor_tensor(out=w, in0=w.bitcast(I32), scalar=-128.0, in1=s, op0=ALU.add, op1=ALU.mult)


def dequantised_mlp(nc, m, d):
    w1, w2, s1, s2 = dequantised_input(m)
    w1, w2 = (w.rearrange("p (k n) -> p k n", k=k) for w, k in ((w1, KD), (w2, 8)))
    layernorm(nc, m, full(m.h), full(m.xn), CHUNKS, ahead=lambda sp: fetch_attention3(sp, m, d))
    def half(j, o, n, acc, link):
        out, t = m.h[:, j, o:o + n], m.s2[:, j, o:o + n]
        link(nc.vector.tensor_tensor(out, out, m.xn[:, j, o:o + n], ALU.add))
        link(nc.vector.tensor_scalar(t, acc, m.v("fc2_b", j), 0.5, ALU.add, ALU.mult))
        return nc.vector.tensor_tensor(out, out, t, ALU.add)
    layernorm(nc, m, full(m.xn), full(m.s3), CHUNKS, lambda k: m.v("gamma", k), lambda k: m.v("beta", k),
              then=mlp(m, w1, w2, lambda j, o, n, acc, link: nc.scalar.activation(
                  m.big2[:, j, o:o + n], acc, ACT.Silu, bias=m.v("fc1_b", j)), half,
                  (m.landed["dequantised"], 16 * 4)))


def mixture3_weights(m):
    return (m.wb[:, 0:4096].rearrange("p (k n) -> p k n", k=KD), m.wa[:, 4096:8192].rearrange("p (k n) -> p k n", k=16))


def fetch_mixture3(sp, m, d):
    fetch(sp, m, "mixture3", *zip(mixture3_weights(m), (d["mw1"], d["mw2"])))


def mixture3(nc, m, d):
    w3 = m.routers[:, KD * 2 * E0:].rearrange("p (k n) -> p k n", k=KD)
    w1, w2 = mixture3_weights(m)
    layernorm(nc, m, full(m.h), full(m.xn), CHUNKS)
    flat1 = m.big1[:, :, :].rearrange("p a b -> p (a b)")
    flat2 = m.big2[:, :, :].rearrange("p a b -> p (a b)")
    nf = 16
    early = [flat2[:, 1024 + f * CW:1024 + (f + 1) * CW] for f in range(nf)]

    def early_up(pe, up_ready, up_taken):
        pe.wait_ge(m.landed["mixture3"], 16 * 2)
        for f in range(nf):
            if f >= 4:
                pe.wait_ge(up_taken, f - 3)
            for k in range(KD):
                ins = nc.tensor.matmul(m.bank(4 + f % 4, CW), w1[:, k, f * P:(f + 1) * P], m.xn[:, k, 0:CW],
                                       start=k == 0, stop=k == KD - 1)
            ins.then_inc(up_ready, 1)

    def early_square(act, up_ready, up_taken):
        for f in range(nf):
            act.wait_ge(up_ready, f + 1)
            nc.scalar.activation(early[f], m.bank(4 + f % 4, CW), ACT.Relu).then_inc(up_taken, 1)
            act.wait_ge(up_taken, f + 1)
            nc.scalar.activation(early[f], early[f], ACT.Square)

    route(nc, m, 1, E3, w3, True, (("up_ready", "up_taken"), early_up, early_square))
    units = [(c, f) for c in range(NCH) for f in range(nf)]
    squared = [flat1[:, i * CW:(i + 1) * CW] for i in range(2)]
    hidden = [flat1[:, (2 + i) * CW:(3 + i) * CW] for i in range(2)]
    with stage(nc, "up_ready", "spread", "relu_ready", "square_ready", "hidden_ready", "hidden_used", "sum_taken") as (
            block, up_ready, spread, relu_ready, square_ready, hidden_ready, hidden_used, sum_taken):

        @block.tensor
        def _(pe):
            def up(u):
                c, f = units[u]
                o = c * CW
                if u >= 2:
                    pe.wait_ge(hidden_ready, u - 1)
                if f % 2 == 0:
                    nc.tensor.matmul(m.bank(2 + (f // 2) % 2, CW), m.pick[:, (f // 2) * P:(f // 2 + 1) * P],
                                     m.parts[:, 0, o:o + CW], start=True, stop=True).then_inc(spread, 1)
                if c == 0:
                    return
                for k in range(KD):
                    ins = nc.tensor.matmul(m.bank(u % 2, CW), w1[:, k, f * P:(f + 1) * P], m.xn[:, k, o:o + CW],
                                           start=k == 0, stop=k == KD - 1)
                ins.then_inc(up_ready, 1)

            up(0)
            for u, (c, f) in enumerate(units):
                if u + 1 < len(units):
                    up(u + 1)
                pe.wait_ge(hidden_ready, u + 1)
                if f == 0 and c >= 2:
                    pe.wait_ge(sum_taken, KD * (c - 1))
                for j in range(KD):
                    ins = nc.tensor.matmul(m.bank(4 + 2 * (c % 2) + j, CW), w2[:, f, j * P:(j + 1) * P],
                                           hidden[u % 2], start=f == 0, stop=f == nf - 1)
                ins.then_inc(hidden_used, 1)

        @block.scalar
        def _(act):
            for u in range(nf, len(units)):
                act.wait_ge(up_ready, u - nf + 1)
                act.wait_ge(hidden_ready, u - 1)
                nc.scalar.activation(squared[u % 2], m.bank(u % 2, CW), ACT.Relu).then_inc(relu_ready, 1)
                act.wait_ge(relu_ready, u - nf + 1)
                nc.scalar.activation(squared[u % 2], squared[u % 2], ACT.Square).then_inc(square_ready, 1)

        @block.vector
        def _(dve):
            for u, (c, f) in enumerate(units):
                if c:
                    dve.wait_ge(square_ready, u - nf + 1)
                dve.wait_ge(spread, u // 2 + 1)
                if u >= 2:
                    dve.wait_ge(hidden_used, u - 1)
                nc.vector.tensor_tensor(hidden[u % 2], squared[u % 2] if c else early[f], m.bank(2 + (f // 2) % 2, CW),
                                        ALU.mult).then_inc(hidden_ready, 1)
                if f == nf - 1:
                    dve.wait_ge(hidden_used, nf * (c + 1))
                    for j in range(KD):
                        out = m.h[:, j, c * CW:(c + 1) * CW]
                        nc.vector.tensor_tensor(out, out, m.bank(4 + 2 * (c % 2) + j, CW),
                                                ALU.add).then_inc(sum_taken, 1)


def cols(a, n):
    return np.ascontiguousarray(np.reshape(a, (n, P)).T)


def rows_to_partitions(w):
    k = w.shape[-2] // P
    return np.ascontiguousarray(np.moveaxis(w.reshape(w.shape[:-2] + (k, P, w.shape[-1])), -3, -2)).reshape(
        w.shape[:-2] + (P, -1))


def lay_out(i):
    f = np.float32
    t = lambda name: np.asarray(i[name])
    d = {}
    x = t("x").reshape(BATCH, 3, 6, 16, 6, 16).transpose(1, 3, 5, 0, 2, 4).reshape(768, BATCH * PATCHES)
    d["patches"] = rows_to_partitions(x)
    d["tok_w"] = rows_to_partitions(t("L0_tok_W").T)
    d["tok_pos"] = rows_to_partitions(t("L0_tok_pos_embedding")[0].T)
    d["tokens"] = np.ascontiguousarray(t("x_txt").reshape(4, P).T)
    d["emb"] = t("L0_txt_emb")
    d["txt_pos"] = rows_to_partitions(t("L0_txt_pos_emb")[:TEXT].T)
    fresh = np.ones((STATE, BATCH, TEXT), f)
    fresh[:, :, 0] = 0
    d["fresh"] = fresh.reshape(STATE, -1)
    d["B"] = rows_to_partitions(t("L0_txt_B"))
    d["C"] = t("L0_txt_C")
    d["Dw"] = rows_to_partitions(t("L0_txt_D"))
    d["w1"] = rows_to_partitions(t("L0_txt_w1"))
    d["w2"] = rows_to_partitions(t("L0_txt_w2"))
    lvec = np.zeros((LAYERS, P, NLVEC), f)
    for l in range(LAYERS):
        for name in ("ln1_s", "ln1_b", "ln2_s", "ln2_b", "b2"):
            lvec[l][:, LVEC[name]:LVEC[name] + 2] = cols(t("L0_txt_" + name)[l], 2)
        lvec[l][:, LVEC["b1"]:LVEC["b1"] + 8] = cols(t("L0_txt_b1")[l], 8)
        lvec[l][:STATE, LVEC["A"]] = t("L0_txt_A_diag")[l]
    d["lvec"] = lvec
    vec = np.zeros((P, NVEC), f)

    def put(name, a):
        c, n = VEC[name]
        vec[:, c:c + n] = a

    names = {
        "tok_b": "L0_tok_b", "cls": "L0_tok_cls_token", "lnf_s": "L0_txt_lnf_s", "lnf_b": "L0_txt_lnf_b",
        "norm_w": "L0_attn_norm_w", "norm_b": "L0_attn_norm_b", "conv_b": "L0_attn_conv_b", "dt_w": "L0_attn_dt_w",
        "dt_b": "L0_attn_dt_b", "D_skip": "L0_attn_D_skip", "c_attn_b": "L1_attn_c_attn_b",
        "c_proj_b": "L1_attn_c_proj_b", "Wq_b": "L2_attn_Wq_b", "Wk_b": "L2_attn_Wk_b", "Wv_b": "L2_attn_Wv_b",
        "Wo_b": "L2_attn_Wo_b", "gamma": "L2_ffn_ln_gamma", "beta": "L2_ffn_ln_beta", "fc1_b": "L2_ffn_fc1_bias",
        "fc2_b": "L2_ffn_fc2_bias", "bq": "L3_attn_bq", "bk": "L3_attn_bk", "bv": "L3_attn_bv", "bo": "L3_attn_bo"}
    for short, name in names.items():
        put(short, cols(t(name), VEC[short][1]))
    put("gate", np.broadcast_to(t("L1_ffn_gate"), (P, 1)))
    put("conv_w", t("L0_attn_conv_w").reshape(4, P, 4).transpose(1, 0, 2).reshape(P, 16))
    put("A_log", t("L0_attn_A_log").reshape(4, P, DS).transpose(1, 0, 2).reshape(P, 4 * DS))
    d["vec"] = vec
    d["ident"] = np.eye(P, dtype=f)

    d["in_proj"] = rows_to_partitions(t("L0_attn_in_proj_w").T)
    xp = t("L0_attn_x_proj_w")
    d["dt_rows"] = rows_to_partitions(np.broadcast_to(xp[0:1].T, (DI, P)))
    d["bc_rows"] = rows_to_partitions(np.concatenate([xp[1:].T] * 3 + [np.zeros((DI, 32), f)], axis=1))
    d["out_proj"] = rows_to_partitions(t("L0_attn_out_proj_w").T)
    pick = np.zeros((P, 32, P), np.float32)
    for part in range(3):
        for e in range(32):
            pick[32 * part + e, e, :] = 1
    d["pick"] = pick.reshape(P, -1)

    d["routers"] = np.concatenate([
        rows_to_partitions(np.concatenate([t("L0_ffn_router_w0"), t("L0_ffn_router_w1")], axis=1)),
        rows_to_partitions(t("L3_ffn_router_w").T)], axis=1)
    experts = [np.concatenate([rows_to_partitions(t("L0_ffn_wg%d" % g)), rows_to_partitions(t("L0_ffn_wu%d" % g)),
                               t("L0_ffn_wd%d" % g)], axis=2) for g in range(2)]
    d["experts"] = np.concatenate(experts, axis=0)
    rc = np.zeros((P, ROUTE_CONSTS), f)
    rc[:ROWT, 0:ROWT] = np.triu(np.ones((ROWT, ROWT), f), 1)
    rc[:, 96:224] = 1
    rc[:, 224:352] = np.arange(P)
    rc[:, 352:364] = np.arange(NROWT)[None, :] * ROWT + np.arange(P)[:, None]
    rc[:, 364] = np.arange(P)
    d["route_consts"] = rc
    order = np.tile(np.arange(E0, 0, -1, dtype=f), (ROWT, 1))
    d["order"] = order

    d["c_attn"] = rows_to_partitions(t("L1_attn_c_attn_w"))
    d["c_proj"] = rows_to_partitions(t("L1_attn_c_proj_w"))
    for name in ("Wq", "Wk", "Wv", "Wo"):
        d["L2" + name] = rows_to_partitions(t("L2_attn_%s_w" % name).T)
        d["L3" + name] = rows_to_partitions(t("L3_attn_%s" % name).T)
    query = np.concatenate([np.tile(np.arange(EASY), HPC), np.tile(np.arange(EASY, SEQ), HPC),
                            np.full(P, SEQ - 1)])
    query = np.stack([query[a:a + P] for a in QAT], axis=1)
    key = np.arange(SEQ)
    late = key > query[:, :, None]
    twice = np.zeros(SEQ, f)
    twice[7:64:8] = np.log(2.0)
    d["mask1"] = (np.where(late, np.float32(-10000.0), np.float32(0)) + twice).reshape(P, -1).astype(f)
    d["mask3"] = np.where(late, NEG, 0.0).reshape(P, -1).astype(f)
    d["mask2"] = np.where(key[None, :] > key[:, None], NEG, 0.0).astype(f)
    d["head_of"] = np.repeat(np.eye(HPC, dtype=f), HD, axis=0)

    d["w_fc"] = rows_to_partitions(t("L1_ffn_w_fc"))
    d["w_proj"] = rows_to_partitions(t("L1_ffn_w_proj"))
    d["fast_b"] = t("L1_ffn_fast_b")
    d["uT"] = np.ascontiguousarray(t("L1_ffn_u").T)
    d["v"] = t("L1_ffn_v")
    d["fc1_q"] = rows_to_partitions(t("L2_ffn_fc1_q"))
    d["fc2_q"] = rows_to_partitions(t("L2_ffn_fc2_q"))
    d["fc1_s"] = t("L2_ffn_fc1_scales")
    d["fc2_s"] = t("L2_ffn_fc2_scales")
    d["mw1"] = rows_to_partitions(t("L3_ffn_w1"))
    d["mw2"] = rows_to_partitions(t("L3_ffn_w2"))
    return d


def store(nc, m, out):
    with stage(nc, "stored") as (block, stored):

        @block.sync
        def _(sp):
            sp.dma_start(out, m.h[:, :, :].rearrange("p k n -> p (k n)")).then_inc(stored, 16)
            sp.wait_ge(stored, 16)


STAGES = ["patch_tokens", "text_encoder", "selective_scan", "mixture0", "attention1", "ternary_mlp", "attention2",
          "dequantised_mlp", "attention3", "mixture3"]


def build(nc, d, out):
    m = Mem(nc)
    setup(nc, m, d)
    patch_tokens(nc, m, d)
    text_encoder(nc, m, d)
    clear_results(nc, m)
    selective_scan(nc, m, d)
    mixture0(nc, m, d)
    attention1(nc, m, d)
    ternary_mlp(nc, m, d)
    attention2(nc, m, d)
    dequantised_mlp(nc, m, d)
    attention3(nc, m, d)
    mixture3(nc, m, d)
    store(nc, m, out)


def kernel(**inputs):
    import concourse.bacc as bacc
    from concourse.bass_utils import run_bass_kernel_spmd

    arrays = lay_out(inputs)
    nc = bacc.Bacc("TRN2", target_bir_lowering=False, num_devices=1)
    d = {name: nc.dram_tensor("in_" + name, a.shape, mybir.dt.from_np(a.dtype), kind="ExternalInput").ap()
         for name, a in arrays.items()}
    out = nc.dram_tensor("out", (P, KD * N), F32, kind="ExternalOutput").ap()
    build(nc, d, out)
    r = run_bass_kernel_spmd(nc, [{"in_" + k: a for k, a in arrays.items()}], core_ids=[0])
    got = np.asarray(r.results[0]["out"]).reshape(P, KD, BATCH, SEQ)
    return np.ascontiguousarray(got.transpose(2, 3, 1, 0)).reshape(BATCH, SEQ, D)
```
